# Optimizing a Trainium2 kernel written in Bass

```python
import numpy as np
import jax
import jax.numpy as jnp

def _softmax(x, axis=-1):
    return jax.nn.softmax(x, axis=axis)

def _gelu(x):
    return jax.nn.gelu(x, approximate=True)

def _silu(x):
    return jax.nn.silu(x)

def _sigmoid(x):
    return jax.nn.sigmoid(x)

def _layernorm(x, axis=-1, eps=1e-05):
    m = jnp.mean(x, axis=axis, keepdims=True)
    v = jnp.var(x, axis=axis, keepdims=True)
    return (x - m) / jnp.sqrt(v + eps)

def _scatter_add(tgt, idx, src, axis=0):
    return tgt.at[idx].add(src)

def _segment_sum(src, seg, n):
    return jax.ops.segment_sum(src, seg, n)
kernel_name = 'mk_decoder_preln_d1_seqx_r4_bb4347'

def setup_inputs(seed: int=0):
    np.random.seed(seed)
    _w = jnp.asarray

    def _rec_inputs():
        import jax
        import jax.numpy as jnp
        _rk = jax.random.key(seed)
        x = 2.818e-05 + 1 * jax.random.normal(jax.random.fold_in(_rk, 1), (4, 512, 512), jnp.float32)
        _lenS = 512 - jax.random.randint(jax.random.fold_in(_rk, 7), (4,), 0, max(1, 512 // 4) + 1, jnp.int32)
        _lenS2 = 512 - jax.random.randint(jax.random.fold_in(_rk, 8), (4,), 0, max(1, 512 // 4) + 1, jnp.int32)
        _ctx_1024P = jax.random.normal(jax.random.fold_in(_rk, 11), (4, 16, 256), jnp.float32)
        _ctx_1024c = jax.random.dirichlet(jax.random.fold_in(_rk, 511), 0.3 * jnp.ones((16,), jnp.float32), (4, 512))
        _ctx_1024t = jnp.einsum('bsk,bkd->bsd', _ctx_1024c, _ctx_1024P)
        _ctx_1024t = _ctx_1024t * jax.lax.rsqrt(jnp.mean(jnp.square(_ctx_1024t)) + 1e-12) * 0.953939
        ctx_1024 = 7.22013e-05 + 1.00017 * (_ctx_1024t + 0.3 * jax.random.normal(jax.random.fold_in(_rk, 611), (4, 512, 256), jnp.float32))
        return (x, ctx_1024)
    x, ctx_1024 = _rec_inputs()

    def _L0_attn_setup():
        import jax, jax.numpy as jnp
        import numpy as np
        B, L, E = (2, 512, 512)
        NUM_HEADS = 16
        NUM_KV_HEADS = 2
        HEAD_DIM = E // NUM_HEADS
        THETA = 10000.0

        def apply_rope(x, theta=THETA):
            D = x.shape[-1]
            half = D // 2
            inv_freq = theta ** (-jnp.arange(half, dtype=jnp.float32) / half)
            pos = jnp.arange(x.shape[1], dtype=jnp.float32)
            ang = pos[:, None] * inv_freq[None, :]
            cos = jnp.cos(ang)[None, :, None, :].astype(x.dtype)
            sin = jnp.sin(ang)[None, :, None, :].astype(x.dtype)
            x1, x2 = (x[..., :half], x[..., half:])
            return jnp.concatenate([x1 * cos - x2 * sin, x2 * cos + x1 * sin], axis=-1)
        key = jax.random.key(seed)
        ks = jax.random.split(key, 8)
        s = 0.02
        return {'x': jax.random.normal(ks[0], (B, L, E), dtype=jnp.float32), 'wq': jax.random.normal(ks[1], (NUM_HEADS * HEAD_DIM, E), dtype=jnp.float32) * s, 'wk': jax.random.normal(ks[2], (NUM_KV_HEADS * HEAD_DIM, E), dtype=jnp.float32) * s, 'wv': jax.random.normal(ks[3], (NUM_KV_HEADS * HEAD_DIM, E), dtype=jnp.float32) * s, 'wo': jax.random.normal(ks[4], (E, NUM_HEADS * HEAD_DIM), dtype=jnp.float32) * s, 'bq': jax.random.normal(ks[5], (NUM_HEADS * HEAD_DIM,), dtype=jnp.float32) * s, 'bk': jax.random.normal(ks[6], (NUM_KV_HEADS * HEAD_DIM,), dtype=jnp.float32) * s, 'bv': jax.random.normal(ks[7], (NUM_KV_HEADS * HEAD_DIM,), dtype=jnp.float32) * s}
    _L0_attn_all = _L0_attn_setup()
    _L0_attn_in = {k: v for k, v in _L0_attn_all.items() if k in ('wq', 'wk', 'wv', 'wo', 'bq', 'bk', 'bv')}
    del _L0_attn_all

    def _L0_xattn_setup():
        import jax, jax.numpy as jnp
        import numpy as np
        B_, L_, D_MODEL = (4, 512, 256)
        D_STATE, D_CONV, EXPAND = (16, 4, 2)
        D_INNER = EXPAND * D_MODEL
        DT_RANK = (D_MODEL + 15) // 16

        def silu(x):
            return x * jax.nn.sigmoid(x)
        key = jax.random.key(seed)
        ks = jax.random.split(key, 10)
        f32 = jnp.float32
        hidden_states = jax.random.normal(ks[0], (B_, L_, D_MODEL), dtype=f32)
        z = jax.random.normal(ks[1], (B_, D_INNER, L_), dtype=f32)
        in_proj_w = jax.random.normal(ks[2], (D_INNER, D_MODEL), dtype=f32) * 0.02
        conv_w = jax.random.normal(ks[3], (D_INNER, 1, D_CONV), dtype=f32) * 0.1
        conv_b = jax.random.normal(ks[4], (D_INNER,), dtype=f32) * 0.02
        x_proj_w = jax.random.normal(ks[5], (DT_RANK + 2 * D_STATE, D_INNER), dtype=f32) * 0.02
        dt_proj_w = jax.random.uniform(ks[6], (D_INNER, DT_RANK), dtype=f32, minval=-DT_RANK ** (-0.5), maxval=DT_RANK ** (-0.5))
        dt = jnp.exp(jax.random.uniform(ks[7], (D_INNER,), dtype=f32, minval=np.log(0.001), maxval=np.log(0.1)))
        dt_proj_b = jnp.log(jnp.expm1(dt))
        A_log = jnp.log(jnp.broadcast_to(jnp.arange(1, D_STATE + 1, dtype=f32), (D_INNER, D_STATE)))
        D = jnp.ones((D_INNER,), f32)
        return {'hidden_states': hidden_states, 'z': z, 'in_proj_w': in_proj_w, 'conv_w': conv_w, 'conv_b': conv_b, 'x_proj_w': x_proj_w, 'dt_proj_w': dt_proj_w, 'dt_proj_b': dt_proj_b, 'A_log': A_log, 'D': D}
    _L0_xattn_all = _L0_xattn_setup()
    _L0_xattn_in = {k: v for k, v in _L0_xattn_all.items() if k in ('in_proj_w', 'conv_w', 'conv_b', 'x_proj_w', 'dt_proj_w', 'dt_proj_b', 'A_log', 'D')}
    del _L0_xattn_all

    def _L0_ffn_setup():
        import jax, jax.numpy as jnp
        import numpy as np
        B, S, D = (4, 512, 512)
        DFF = 1408
        E, K, R = (8, 2, 16)
        SCALING = 32.0 / 16.0
        key = jax.random.key(seed)
        ks = jax.random.split(key, 12)
        s = lambda k, shape, scale: jax.random.normal(k, shape, dtype=jnp.float32) * scale
        return {'x': s(ks[0], (B, S, D), 1.0), 'Wg': s(ks[1], (DFF, D), 0.02), 'Wu': s(ks[2], (DFF, D), 0.02), 'Wd': s(ks[3], (D, DFF), 0.02), 'Wr': s(ks[4], (E, D), 0.02), 'Ag': s(ks[5], (E, R, D), 0.02), 'Bg': s(ks[6], (E, DFF, R), 0.02), 'Au': s(ks[7], (E, R, D), 0.02), 'Bu': s(ks[8], (E, DFF, R), 0.02), 'Ad': s(ks[9], (E, R, DFF), 0.02), 'Bd': s(ks[10], (E, D, R), 0.02)}
    _L0_ffn_all = _L0_ffn_setup()
    _L0_ffn_in = {k: v for k, v in _L0_ffn_all.items() if k in ('Wg', 'Wu', 'Wd', 'Wr', 'Ag', 'Bg', 'Au', 'Bu', 'Ad', 'Bd')}
    del _L0_ffn_all
    return {'x': x, 'ctx_1024': ctx_1024, 'L0_attn_wq': _L0_attn_in['wq'], 'L0_attn_wk': _L0_attn_in['wk'], 'L0_attn_wv': _L0_attn_in['wv'], 'L0_attn_wo': _L0_attn_in['wo'], 'L0_attn_bq': _L0_attn_in['bq'], 'L0_attn_bk': _L0_attn_in['bk'], 'L0_attn_bv': _L0_attn_in['bv'], 'L0_xattn_in_proj_w': _L0_xattn_in['in_proj_w'], 'L0_xattn_conv_w': _L0_xattn_in['conv_w'], 'L0_xattn_conv_b': _L0_xattn_in['conv_b'], 'L0_xattn_x_proj_w': _L0_xattn_in['x_proj_w'], 'L0_xattn_dt_proj_w': _L0_xattn_in['dt_proj_w'], 'L0_xattn_dt_proj_b': _L0_xattn_in['dt_proj_b'], 'L0_xattn_A_log': _L0_xattn_in['A_log'], 'L0_xattn_D': _L0_xattn_in['D'], 'L0_ffn_Wg': _L0_ffn_in['Wg'], 'L0_ffn_Wu': _L0_ffn_in['Wu'], 'L0_ffn_Wd': _L0_ffn_in['Wd'], 'L0_ffn_Wr': _L0_ffn_in['Wr'], 'L0_ffn_Ag': _L0_ffn_in['Ag'], 'L0_ffn_Bg': _L0_ffn_in['Bg'], 'L0_ffn_Au': _L0_ffn_in['Au'], 'L0_ffn_Bu': _L0_ffn_in['Bu'], 'L0_ffn_Ad': _L0_ffn_in['Ad'], 'L0_ffn_Bd': _L0_ffn_in['Bd']}

def reference(x, ctx_1024, L0_attn_wq, L0_attn_wk, L0_attn_wv, L0_attn_wo, L0_attn_bq, L0_attn_bk, L0_attn_bv, L0_xattn_in_proj_w, L0_xattn_conv_w, L0_xattn_conv_b, L0_xattn_x_proj_w, L0_xattn_dt_proj_w, L0_xattn_dt_proj_b, L0_xattn_A_log, L0_xattn_D, L0_ffn_Wg, L0_ffn_Wu, L0_ffn_Wd, L0_ffn_Wr, L0_ffn_Ag, L0_ffn_Bg, L0_ffn_Au, L0_ffn_Bu, L0_ffn_Ad, L0_ffn_Bd):
    import jax
    import jax.numpy as jnp

    def _L0_attn_ref(x, wq, wk, wv, wo, bq, bk, bv):
        import jax, jax.numpy as jnp
        import numpy as np
        B, L, E = (2, 512, 512)
        NUM_HEADS = 16
        NUM_KV_HEADS = 2
        HEAD_DIM = E // NUM_HEADS
        THETA = 10000.0

        def apply_rope(x, theta=THETA):
            D = x.shape[-1]
            half = D // 2
            inv_freq = theta ** (-jnp.arange(half, dtype=jnp.float32) / half)
            pos = jnp.arange(x.shape[1], dtype=jnp.float32)
            ang = pos[:, None] * inv_freq[None, :]
            cos = jnp.cos(ang)[None, :, None, :].astype(x.dtype)
            sin = jnp.sin(ang)[None, :, None, :].astype(x.dtype)
            x1, x2 = (x[..., :half], x[..., half:])
            return jnp.concatenate([x1 * cos - x2 * sin, x2 * cos + x1 * sin], axis=-1)
        b, l, _ = x.shape
        Hq, Hkv, Dh = (NUM_HEADS, NUM_KV_HEADS, HEAD_DIM)
        G = Hq // Hkv
        scale = 1.0 / Dh ** 0.5
        q = (x @ wq.T + bq).reshape(b, l, Hq, Dh)
        k = (x @ wk.T + bk).reshape(b, l, Hkv, Dh)
        v = (x @ wv.T + bv).reshape(b, l, Hkv, Dh)
        q = apply_rope(q)
        k = apply_rope(k)
        q = q.transpose(0, 2, 1, 3).reshape(b, Hkv, G, l, Dh).astype(jnp.float32)
        k = k.transpose(0, 2, 1, 3).astype(jnp.float32)
        v = v.transpose(0, 2, 1, 3).astype(jnp.float32)
        scores = jnp.einsum('bhgqd,bhkd->bhgqk', q, k) * scale
        causal = jnp.tril(jnp.ones((l, l), dtype=bool))
        scores = jnp.where(causal[None, None, None, :, :], scores, -jnp.inf)
        attn = jax.nn.softmax(scores, axis=-1)
        out = jnp.einsum('bhgqk,bhkd->bhgqd', attn, v)
        out = out.reshape(b, Hq, l, Dh).transpose(0, 2, 1, 3).reshape(b, l, Hq * Dh)
        out = out.astype(x.dtype)
        return out @ wo.T

    def _L0_xattn_ref(hidden_states, z, in_proj_w, conv_w, conv_b, x_proj_w, dt_proj_w, dt_proj_b, A_log, D):
        import jax, jax.numpy as jnp
        import numpy as np
        B_, L_, D_MODEL = (4, 512, 256)
        D_STATE, D_CONV, EXPAND = (16, 4, 2)
        D_INNER = EXPAND * D_MODEL
        DT_RANK = (D_MODEL + 15) // 16

        def silu(x):
            return x * jax.nn.sigmoid(x)
        Bsz, L, _ = hidden_states.shape
        d_inner, _, d_conv = conv_w.shape
        dt_rank = dt_proj_w.shape[1]
        d_state = A_log.shape[1]
        x = jnp.einsum('bld,ed->bel', hidden_states, in_proj_w)
        xc = jax.lax.conv_general_dilated(x, conv_w, window_strides=(1,), padding=[(d_conv - 1, 0)], feature_group_count=d_inner, dimension_numbers=('NCH', 'OIH', 'NCH'))
        x = silu(xc + conv_b[None, :, None])
        x_dbl = jnp.einsum('bdl,ed->bel', x, x_proj_w)
        dt_low, Bm, Cm = jnp.split(x_dbl, [dt_rank, dt_rank + d_state], axis=1)
        dt = jnp.einsum('brl,dr->bdl', dt_low, dt_proj_w)
        dt = jax.nn.softplus(dt + dt_proj_b[None, :, None])
        A = -jnp.exp(A_log)
        dt_t = jnp.moveaxis(dt, -1, 0)
        B_t = jnp.moveaxis(Bm, -1, 0)
        C_t = jnp.moveaxis(Cm, -1, 0)
        u_t = jnp.moveaxis(x, -1, 0)

        def step(state, inp):
            d, b, c, u = inp
            dA = jnp.exp(d[..., None] * A)
            state = state * dA + (d * u)[..., None] * b[:, None, :]
            y = jnp.einsum('bdn,bn->bd', state, c)
            return (state, y)
        state0 = jnp.zeros((Bsz, d_inner, d_state), x.dtype)
        _, ys = jax.lax.scan(step, state0, (dt_t, B_t, C_t, u_t))
        y = jnp.moveaxis(ys, 0, 2)
        y = y + D[None, :, None] * x
        y = y * silu(z)
        return jnp.swapaxes(y, 1, 2)

    def _L0_ffn_ref(x, Wg, Wu, Wd, Wr, Ag, Bg, Au, Bu, Ad, Bd):
        import jax, jax.numpy as jnp
        import numpy as np
        B, S, D = (4, 512, 512)
        DFF = 1408
        E, K, R = (8, 2, 16)
        SCALING = 32.0 / 16.0
        b, s, d = x.shape
        xf = x.reshape(-1, d)
        gate_base = xf @ Wg.T
        up_base = xf @ Wu.T
        base_out = jax.nn.silu(gate_base) * up_base @ Wd.T
        router_logits = xf @ Wr.T
        probs = jax.nn.softmax(router_logits.astype(jnp.float32), axis=-1)
        topw, topi = jax.lax.top_k(probs, K)
        topw = topw.astype(x.dtype)
        expert_w = jnp.sum(jax.nn.one_hot(topi, E, dtype=x.dtype) * topw[..., None], axis=1)

        def expert_step(acc, params):
            Ag_e, Bg_e, Au_e, Bu_e, Ad_e, Bd_e, we = params
            g_lora = xf @ Ag_e.T @ Bg_e.T * SCALING
            u_lora = xf @ Au_e.T @ Bu_e.T * SCALING
            h = jax.nn.silu(gate_base + g_lora) * (up_base + u_lora)
            d_delta = h @ Ad_e.T @ Bd_e.T * SCALING
            return (acc + d_delta * we[:, None], None)
        acc0 = jnp.zeros_like(base_out)
        acc, _ = jax.lax.scan(expert_step, acc0, (Ag, Bg, Au, Bu, Ad, Bd, expert_w.T))
        return (base_out + acc).reshape(b, s, d)
    x = x + _L0_attn_ref(_layernorm(x, axis=-1), L0_attn_wq, L0_attn_wk, L0_attn_wv, L0_attn_wo, L0_attn_bq, L0_attn_bk, L0_attn_bv)
    x = x + _L0_xattn_ref(ctx_1024, _layernorm(x, axis=-1), L0_xattn_in_proj_w, L0_xattn_conv_w, L0_xattn_conv_b, L0_xattn_x_proj_w, L0_xattn_dt_proj_w, L0_xattn_dt_proj_b, L0_xattn_A_log, L0_xattn_D)
    x = x + _L0_ffn_ref(_layernorm(x, axis=-1), L0_ffn_Wg, L0_ffn_Wu, L0_ffn_Wd, L0_ffn_Wr, L0_ffn_Ag, L0_ffn_Bg, L0_ffn_Au, L0_ffn_Bu, L0_ffn_Ad, L0_ffn_Bd)
    return x

_drawn_inputs = setup_inputs


def setup_inputs(seed=0):
    import zlib

    import numpy as np

    out = dict(_drawn_inputs(seed))
    spreads = {'L0_xattn_D': (1.0, 0.6)}
    factors = {'ctx_1024': 2.89,
     'L0_attn_wq': 8.0,
     'L0_attn_wk': 8.0,
     'L0_attn_bq': 8.0,
     'L0_attn_bk': 8.0,
     'L0_attn_bv': 5.735,
     'L0_xattn_in_proj_w': 2.895,
     'L0_xattn_conv_w': 2.953,
     'L0_xattn_conv_b': 8.0,
     'L0_xattn_x_proj_w': 8.0,
     'L0_xattn_dt_proj_w': 8.0,
     'L0_xattn_dt_proj_b': 8.0,
     'L0_xattn_A_log': 8.0,
     'L0_ffn_Wr': 8.0,
     'L0_ffn_Ag': 8.0,
     'L0_ffn_Bg': 8.0,
     'L0_ffn_Au': 8.0,
     'L0_ffn_Bu': 8.0,
     'L0_ffn_Ad': 8.0,
     'L0_ffn_Bd': 8.0,
     'L0_ffn_Wd': 64.0}
    for name, (base, spread) in spreads.items():
        noise = np.random.default_rng([zlib.crc32(name.encode()), seed]).standard_normal(out[name].shape)
        drawn = base * np.exp(spread * noise) if base else spread * noise
        out[name] = jnp.asarray(drawn.astype(out[name].dtype))
    for name, factor in factors.items():
        out[name] = (out[name] * factor).astype(out[name].dtype)
    return out
```

```python
from contextlib import ExitStack

import concourse.bass as bass
from concourse import mybir

F32 = mybir.dt.float32
BF16 = mybir.dt.bfloat16
ALU = mybir.AluOpType
ACT = mybir.ActivationFunctionType
AX = mybir.AxisListType

P = 128
BATCH, L, D = 4, 512, 512
HEADS, KV_HEADS, HD = 16, 2, 32
NT = L // P
KT = D // P
MT = HEADS * HD // P
HPT = P // HD
CTX = 256
CT = CTX // P
DI = 512
JT = DI // P
NS = 16
RANK = 16
TAPS = 4
DFF = 1408
FT = DFF // P
NE, LR = 8, 16
EPS = 1e-5
SCALE = HD ** -0.5
NEG = -1e30

WG, WU, BG, BU, AD = 0, KT * P, 2 * KT * P, 2 * KT * P + P, 2 * KT * P + 2 * P
WTILE = 2 * KT * P + 3 * P
WSLOTS = 3
C_ID, C_ROT, C_MASK, C_SEL, C_COS, C_SIN = 0, 128, 256, 384, 416, 928
C_CAND, C_HALF = 1440, 1448
C_COLS = 1452
V_CW, V_CB, V_DTB, V_AL, V_D, V_BQ, V_BK, V_BV = 0, 16, 20, 24, 88, 92, 96, 98
V_COLS = 98 + KV_HEADS * HD

def log1p_coefficients(degree):
    import numpy as np
    nodes = 0.5 + 0.5 * np.cos(np.pi * (np.arange(64) + 0.5) / 64)
    fit = np.polynomial.Chebyshev.fit(nodes, np.log1p(nodes) / nodes, degree, domain=[0, 1])
    return [float(c) for c in fit.convert(kind=np.polynomial.Polynomial).coef]


POLY = log1p_coefficients(9)
NPOLY = len(POLY)


EVALS = 3 * FT
STEPS = MT * NT * 2
SLOTS = EVALS + STEPS


def plan(first, in_ffn):
    pieces = [("poly", k) for k in range(NPOLY + 2)]
    for n in range(NS):
        pieces += [("mul", n), ("run", n), ("out", n)]
    at = {}
    for k, piece in enumerate(pieces):
        if first:
            at[piece] = EVALS + k * STEPS // len(pieces)
        elif k < in_ffn:
            at[piece] = k * EVALS // in_ffn
        else:
            at[piece] = EVALS + (k - in_ffn) * STEPS // (len(pieces) - in_ffn)
    slots = [{"dve": [], "bc": [], "decay": [], "add": []} for _ in range(SLOTS + 1)]
    for piece in pieces:
        slots[at[piece]]["dve"].append(piece)
    for n in range(NS):
        slots[at["poly", NPOLY - 4] if n < 2 else at["out", n - 2]]["bc"].append(n)
        slots[at["poly", NPOLY + 1] if n < 2 else at["run", n - 2]]["decay"].append(n)
        slots[at["out", n]]["add"].append(n)
    return slots


PLAN_FIRST = plan(True, 0)
PLAN_NEXT = plan(False, 44)


def slot_of(slots, s):
    return slots[s]


def uses_of(first, last):
    names = []
    if not last:
        names += [("xin", j) for j in range(JT)]
    if first:
        names += [("dt", j) for j in range(JT)]
    else:
        names += [("xt2", k) for k in range(KT)] + [("mask", k) for k in range(4)] + [("lowg", 0), ("lowu", 0)]
        if not last:
            names += [("dt", j) for j in range(JT)]
            for e in range(EVALS):
                for n in PLAN_NEXT[e]["bc"]:
                    names += [("bc", 2 * n), ("bc", 2 * n + 1)]
    if not last:
        slots = PLAN_FIRST if first else PLAN_NEXT
        names += [("xt", k) for k in range(KT)]
        names += [("q", m) if part == 0 else ("qrot", m) for m in range(MT) for part in range(2)]
        names += [("k", g) if part == 0 else ("krot", g) for g in range(KV_HEADS) for part in range(2)]
        for s in range(STEPS + 4):
            if s >= 4 and s % 2 == 0:
                names.append(("pv", (s - 4) // 2))
            if s < STEPS:
                for n in slots[EVALS + s]["bc"]:
                    names += [("bc", 2 * n), ("bc", 2 * n + 1)]
        names += [("op", i) for i in range(NT)] + [("yt", i) for i in range(NT)]
    return {name: k for k, name in enumerate(names)}


USES_FIRST, USES_NEXT, USES_LAST = uses_of(True, False), uses_of(False, False), uses_of(False, True)
assert len(USES_FIRST) % 2 == 0 and len(USES_NEXT) % 2 == 0


def decoder_layer(nc, x, ctx_t, wq, wk, wv, wo, w_in, w_x, w_dt, w_lora, w_r, b_down, w_tiles, w_down,
                  vectors, constants, out):
    with ExitStack() as stack:
        def sb(name, shape, dt=F32):
            return stack.enter_context(nc.sbuf_tensor(name, shape, dt))

        def ps(name, shape):
            return stack.enter_context(nc.psum_tensor(name, shape, F32))

        def sem(name):
            return stack.enter_context(nc.semaphore(name))

        wq_sb = sb("wq_sb", [P, KT, HEADS * HD])
        wk_sb = sb("wk_sb", [P, KV_HEADS, KT, P])
        wv_sb = sb("wv_sb", [P, KT, KV_HEADS * HD])
        wo_sb = sb("wo_sb", [P, MT, D])
        win_sb = sb("win_sb", [P, CT, DI])
        wx_sb = sb("wx_sb", [P, JT, P])
        wdt_sb = sb("wdt_sb", [P, DI])
        lora_sb = sb("lora_sb", [P, 2, KT, P])
        wr_sb = sb("wr_sb", [P, KT, NE])
        bd_sb = sb("bd_sb", [P, D])
        vec = sb("vec", [P, V_COLS])
        cst = sb("cst", [P, C_COLS])
        ident_b = sb("ident_b", [P, P], BF16)
        mask_b = sb("mask_b", [P, P], BF16)
        sel_b = sb("sel_b", [P, 2 * NS], BF16)
        decay_rate = sb("decay_rate", [P, JT, NS])
        conv_half = sb("conv_half", [P, 20])
        ident = cst[:, C_ID:C_ID + P]
        rot = cst[:, C_ROT:C_ROT + P]
        cos_t, sin_t = cst[:, C_COS:C_COS + L], cst[:, C_SIN:C_SIN + L]
        xa = sb("xa", [P, NT, D])
        xb = sb("xb", [P, NT, D])
        xt = sb("xt", [P, KT, L])
        r1 = sb("r1", [P, 12, L])
        probs, probs_t, xn, hb = r1[:, 0:4, :], r1[:, 4:8, :], r1[:, 8:12, :], r1[:, 0:FT, :]
        attn_t = xn
        hz, silu_z = r1[:, 0:4, :], r1[:, 4:8, :]
        r2 = sb("r2", [P, 15, L])
        keys, q_t, q_raw, rope_tmp = r2[:, 0:8, :], r2[:, 8:12, :], r2[:, 12:14, :], r2[:, 14, :]
        gate, hk, low, mask_t, down_low = r2[:, 0:2, :], r2[:, 2:6, :], r2[:, 6:10, :], r2[:, 10:14, :], r2[:, 14, :]
        expanded = r2[:, 2:6, :]
        v_sb = sb("v_sb", [P, NT, KV_HEADS * HD])
        w_sb = sb("w_sb", [P, WSLOTS, WTILE])
        wd_sb = sb("wd_sb", [P, 2, D])
        ctx_sb = sb("ctx_sb", [P, CT, L])
        dt_sb = sb("dt_sb", [P, JT, L])
        du_sb = sb("du_sb", [P, JT, L])
        y_sb = sb("y_sb", [P, JT, L])
        state = sb("state", [P, 2, JT, L])
        decay = sb("decay", [P, 2, JT, L])
        bc_sb = sb("bc_sb", [P, 2, 2, L])
        xdt_sb = sb("xdt_sb", [P, L])
        bc_stack = sb("bc_stack", [P, L], BF16)
        split_f = sb("split_f", [P, L])
        split_b = sb("split_b", [P, L], BF16)
        u_sb, exp_v, relu_v, conv_sb = state[:, 0, :, :], state[:, 1, :, :], decay[:, 0, :, :], decay[:, 1, :, :]
        scrap = sb("scrap", [1, 1])
        scrap_a = sb("scrap_a", [1, 1])
        stats = sb("stats", [P, NT, 6])
        mv = sb("mv", [P, NT, 2])
        var_eps = sb("var_eps", [P, NT])
        rstd = sb("rstd", [P, NT])
        neg_max = sb("neg_max", [P, 2, 2])
        bias_max = sb("bias_max", [P, 2, 2])
        row_sum = sb("row_sum", [P, 2, 2])
        row_inv = sb("row_inv", [P, 2, 2])
        rt = sb("rt", [P, 8, NT, NE])
        rs = sb("rs", [P, 8, NT])

        ps_a = ps("ps_a", [P, 4, L])
        ps_b = ps("ps_b", [P, 2, L])
        ps_w = ps("ps_w", [P, 2, L])

        loaded = {k: sem("loaded_" + k) for k in ("const", "att", "mamba", "ffn", "ctx", "x")}
        w_loaded = [sem(f"w_loaded{k}") for k in range(WSLOTS)]
        wd_loaded = [sem(f"wd_loaded{k}") for k in range(2)]
        stored = sem("stored")
        consts_ready = sem("consts_ready")
        work_full = [sem("work_full0"), sem("work_full1")]
        work_free = [sem("work_free0"), sem("work_free1")]
        norm_chain = {k: sem("norm_chain_" + k) for k in ("att", "z", "ffn")}
        rstd_ready = {k: sem("rstd_ready_" + k) for k in ("att", "z", "ffn")}
        xn_ready = {k: sem("xn_ready_" + k) for k in ("att", "z", "ffn")}
        xt_ready = {k: sem("xt_ready_" + k) for k in ("att", "ffn")}
        q_raw_ready = sem("q_raw_ready")
        rope_chain = sem("rope_chain")
        qk_ready = sem("qk_ready")
        keys_zero = sem("keys_zero")
        v_full = sem("v_full")
        v_ready = sem("v_ready")
        scores_ready = sem("scores_ready")
        max_chain = sem("max_chain")
        bias_ready = sem("bias_ready")
        exp_done = sem("exp_done")
        inv_chain = sem("inv_chain")
        probs_ready = sem("probs_ready")
        pt_full = sem("pt_full")
        pt_ready = sem("pt_ready")
        pv_done = sem("pv_done")
        attn_ready = sem("attn_ready")
        x1_ready = sem("x1_ready")
        tanh_z = sem("tanh_z")
        z_chain = sem("z_chain")
        gated_ready = sem("gated_ready")
        x2_ready = sem("x2_ready")
        tap_ready = sem("tap_ready")
        conv_chain = sem("conv_chain")
        conv_tanh = sem("conv_tanh")
        u_ready = sem("u_ready")
        xdbl_full = sem("xdbl_full")
        xdt_ready = sem("xdt_ready")
        split_chain = sem("split_chain")
        bc_stack_ready = sem("bc_stack_ready")
        softplus_chain = sem("softplus_chain")
        softplus_in = sem("softplus_in")
        y_init = sem("y_init")
        poly_chain = sem("poly_chain")
        dt_ready = sem("dt_ready")
        bc_ready = sem("bc_ready")
        decay_ready = sem("decay_ready")
        scan_chain = sem("scan_chain")
        y_added = sem("y_added")
        router_full = sem("router_full")
        router_chain = sem("router_chain")
        router_shift = sem("router_shift")
        router_exp = sem("router_exp")
        expanded_ready = sem("expanded_ready")
        mask_ready = sem("mask_ready")
        low_ready = sem("low_ready")
        gu_ready = sem("gu_ready")
        tanh_ready = sem("tanh_ready")
        gate_chain = sem("gate_chain")
        h_ready = sem("h_ready")
        d_done = sem("d_done")
        down_chain = sem("down_chain")
        down_ready = sem("down_ready")
        wd_used = sem("wd_used")
        out_full = sem("out_full")
        x3_ready = sem("x3_ready")

        class Count:

            def __init__(self, semaphore, per, b):
                self.semaphore, self.per, self.b, self.n = semaphore, per, b, 0

            def inc(self, instruction):
                instruction.then_inc(self.semaphore, 1)
                self.n += 1

            def link(self, eng, instruction):
                self.inc(instruction)
                eng.wait_ge(self.semaphore, self.b * self.per + self.n)

            def end(self):
                assert self.n == self.per, (self.semaphore, self.n, self.per)

        def use(name, b, ffn=False):
            if ffn and isinstance(b, int) and b == BATCH - 1:
                k, before = USES_LAST[name], len(USES_FIRST) + (BATCH - 1) * len(USES_NEXT)
            elif not ffn and isinstance(b, int) and b == 0:
                k, before = USES_FIRST[name], 0
            else:
                i = b if ffn else b - 1
                k, before = USES_NEXT[name], None
                return k % 2, i * (len(USES_NEXT) // 2) + (len(USES_FIRST) // 2 + k // 2)
            return k % 2, (before + k) // 2

        def fill(eng, name, b, ffn=False):
            bank, count = use(name, b, ffn)
            if not (isinstance(count, int) and count == 0):
                eng.wait_ge(work_free[bank], count)
            return bank

        def filled(eng, name, b, ffn=False):
            bank, count = use(name, b, ffn)
            eng.wait_ge(work_full[bank], count + 1)
            return bank

        def first_batch(b):
            return isinstance(b, int) and b == 0

        block = stack.enter_context(nc.Block())

        @block.sync
        def _(sp):
            def load_ctx(b):
                if not first_batch(b):
                    sp.wait_ge(u_ready, b * JT)
                sp.dma_start(ctx_sb[:], ctx_t[b].rearrange("(t p) l -> p t l", p=P)).then_inc(loaded["ctx"], 16)

            def load_x(b):
                if not first_batch(b):
                    sp.wait_ge(x2_ready, b)
                sp.dma_start(xa[:], x[b].rearrange("(i p) d -> p i d", p=P)).then_inc(loaded["x"], 16)

            def load_w(t, f):
                if f >= WSLOTS:
                    sp.wait_ge(d_done, t * FT + f - WSLOTS + 1)
                else:
                    sp.wait_ge(scores_ready, t * STEPS + 1)
                sp.dma_start(w_sb[:, f % WSLOTS, :], w_tiles[f]).then_inc(w_loaded[f % WSLOTS], 16)

            def load_wd(t, f):
                if f >= 2:
                    sp.wait_ge(wd_used, t * FT + f - 1)
                else:
                    sp.wait_ge(scores_ready, t * STEPS + 1)
                sp.dma_start(wd_sb[:, f % 2, :], w_down[f]).then_inc(wd_loaded[f % 2], 16)

            def ffn_loads(t, first):
                for f in range(first, FT):
                    load_w(t, f)
                for f in range(FT):
                    load_wd(t, f)
                for i in range(NT):
                    sp.wait_ge(x3_ready, t * NT + i + 1)
                    sp.dma_start(out[t].rearrange("(i p) d -> p i d", p=P)[:, i, :], xb[:, i, :]).then_inc(stored, 16)

            load_ctx(0)
            load_x(0)
            sp.dma_start(wk_sb[:], wk).then_inc(loaded["att"], 16)
            sp.dma_start(wv_sb[:], wv).then_inc(loaded["att"], 16)
            sp.dma_start(wo_sb[:], wo).then_inc(loaded["att"], 16)
            sp.dma_start(lora_sb[:], w_lora).then_inc(loaded["ffn"], 16)
            sp.dma_start(wr_sb[:], w_r).then_inc(loaded["ffn"], 16)
            sp.dma_start(bd_sb[:], b_down).then_inc(loaded["ffn"], 16)
            with sp.Fori(0, BATCH - 1) as t:
                load_ctx(t + 1)
                for f in range(WSLOTS):
                    load_w(t, f)
                load_x(t + 1)
                ffn_loads(t, WSLOTS)
            for f in range(WSLOTS):
                load_w(BATCH - 1, f)
            ffn_loads(BATCH - 1, WSLOTS)
            sp.wait_ge(stored, 16 * NT * BATCH)

        @block.gpsimd
        def _(pool):
            def inverse_deviation(kind, b):
                pool.wait_ge(norm_chain[kind], b * 9 + 9)
                nc.gpsimd.tensor_tensor(rstd[:], var_eps[:], cst[:, C_HALF:C_HALF + NT], ALU.pow).then_inc(rstd_ready[kind], 1)

            def add_states(b, slot):
                for n in slot["add"]:
                    pool.wait_ge(scan_chain, b * 3 * NS + 3 * n + 3)
                    if n == 0:
                        pool.wait_ge(y_init, b * JT + JT)
                    else:
                        pool.wait_ge(y_added, b * NS + n)
                    nc.gpsimd.tensor_tensor(y_sb[:], y_sb[:], state[:, n % 2, :, :], ALU.add).then_inc(y_added, 1)

            def clear_keys(b):
                pool.wait_ge(loaded["const"], 32)
                if not first_batch(b):
                    pool.wait_ge(down_ready, b)
                nc.gpsimd.memset(keys, 0.0).then_inc(keys_zero, 1)

            def attention(b, slots):
                clear_keys(b)
                inverse_deviation("att", b)
                for s in range(STEPS):
                    add_states(b, slots[EVALS + s])
                inverse_deviation("z", b)

            pool.wait_ge(loaded["const"], 32)
            attention(0, PLAN_FIRST)
            with pool.Fori(0, BATCH - 1) as t:
                inverse_deviation("ffn", t)
                for e in range(EVALS):
                    add_states(t + 1, PLAN_NEXT[e])
                attention(t + 1, PLAN_NEXT)
            inverse_deviation("ffn", BATCH - 1)

        @block.scalar
        def _(act):
            def to_sbuf(dst, src, name, b, ffn=False):
                bank = use(name, b, ffn)[0]
                return nc.scalar.activation(dst, src, ACT.Copy).then_inc(work_free[bank], 1)

            def conv_tap(b):
                for j in range(JT):
                    bank = filled(act, ("xin", j), b)
                    nc.scalar.activation(conv_sb[:, j, :], ps_w[:, bank, :], ACT.Identity,
                                         bias=conv_half[:, 16 + j:17 + j],
                                         scale=conv_half[:, TAPS * j + 3:TAPS * j + 4]).then_inc(tap_ready, 1)

            def conv_gate(b):
                for j in range(JT):
                    act.wait_ge(conv_chain, b * 3 * JT + 3 * j + 3)
                    nc.scalar.activation(exp_v[:, j, :], conv_sb[:, j, :], ACT.Tanh).then_inc(conv_tanh, 1)

            def split_first(b):
                act.wait_ge(xdbl_full, b + 1)
                nc.scalar.activation(xdt_sb[:], ps_b[:, 1, :], ACT.Copy).then_inc(xdt_ready, 1)
                act.wait_ge(u_ready, b * JT + JT)
                for j in range(JT):
                    nc.scalar.activation(y_sb[:, j, :], u_sb[:, j, :], ACT.Identity,
                                         scale=vec[:, V_D + j:V_D + j + 1]).then_inc(y_init, 1)

            def softplus_parts(b):
                chain = Count(softplus_chain, 2 * JT, b)
                for j in range(JT):
                    bank = filled(act, ("dt", j), b)
                    bias = vec[:, V_DTB + j:V_DTB + j + 1]
                    chain.link(act, nc.scalar.activation(exp_v[:, j, :], ps_w[:, bank, :], ACT.Abs, bias=bias))
                    chain.inc(nc.scalar.activation(exp_v[:, j, :], exp_v[:, j, :], ACT.Exp, scale=-1.0))
                    nc.scalar.activation(relu_v[:, j, :], ps_w[:, bank, :], ACT.Relu, bias=bias)\
                        .then_inc(work_free[bank], 1)
                act.wait_ge(softplus_chain, (b + 1) * 2 * JT)
                nc.scalar.activation(scrap_a[:], vec[0:1, 0:1], ACT.Copy).then_inc(softplus_in, 1)
                chain.end()

            def scan_inputs(b, slot):
                for n in slot["bc"]:
                    for c in range(2):
                        if n >= 2:
                            act.wait_ge(scan_chain, b * 3 * NS + 3 * (n - 2) + (1 if c == 0 else 3))
                        elif not first_batch(b):
                            act.wait_ge(scan_chain, b * 3 * NS)
                        bank = filled(act, ("bc", 2 * n + c), b)
                        nc.scalar.activation(bc_sb[:, n % 2, c, :], ps_w[:, bank, :], ACT.Copy)\
                            .then_inc(work_free[bank], 1)
                for n in slot["decay"]:
                    if n == 0:
                        act.wait_ge(dt_ready, b + 1)
                    if n >= 2:
                        act.wait_ge(scan_chain, b * 3 * NS + 3 * (n - 2) + 2)
                    for j in range(JT):
                        nc.scalar.activation(decay[:, n % 2, j, 1:L], dt_sb[:, j, 1:L], ACT.Exp,
                                             scale=decay_rate[:, j, n:n + 1]).then_inc(decay_ready, 1)

            def transposed(kind, name, b, ffn):
                for k in range(KT):
                    bank = filled(act, (name, k), b, ffn)
                    nc.scalar.activation(xt[:, k, :], ps_w[:, bank, :], ACT.Copy).then_inc(work_free[bank], 1)

            def attention(b, slots):
                transposed("att", "xt", b, False)
                for n in range(MT + KV_HEADS):
                    name = ("q", n) if n < MT else ("k", n - MT)
                    bank = filled(act, name, b)
                    if n >= 2:
                        act.wait_ge(qk_ready, b * (MT + KV_HEADS) + n - 1)
                    nc.scalar.activation(q_raw[:, n % 2, :], ps_w[:, bank, :], ACT.Identity,
                                         bias=vec[:, V_BQ + n:V_BQ + n + 1]).then_inc(work_free[bank], 1)

                def exponents(s):
                    i = (s // 2) % NT
                    act.wait_ge(bias_ready, b * STEPS + s + 1)
                    for k in range(2):
                        if s >= 2:
                            act.wait_ge(pt_full, b * 2 * STEPS + 2 * (s - 2) + k + 1)
                        nc.scalar.activation(probs[:, (2 * s + k) % 4, 0:(i + 1) * P],
                                             ps_a[:, 2 * (s % 2) + k, 0:(i + 1) * P], ACT.Exp,
                                             bias=bias_max[:, s % 2, k:k + 1], scale=SCALE,
                                             accum_out=row_sum[:, s % 2, k:k + 1]).then_inc(exp_done, 1)

                def move_transposed(s):
                    i = (s // 2) % NT
                    for k in range(2):
                        act.wait_ge(pt_full, b * 2 * STEPS + 2 * s + k + 1)
                        if s >= 2:
                            act.wait_ge(pv_done, b * (STEPS // 2) + s // 2)
                        nc.scalar.activation(probs_t[:, (2 * s + k) % 4, 0:(i + 1) * P],
                                             ps_b[:, k, 0:(i + 1) * P], ACT.Copy).then_inc(pt_ready, 1)

                def move_output(g):
                    m, i = g // NT, g % NT
                    bank = filled(act, ("pv", g), b)
                    nc.scalar.activation(attn_t[:, m, i * P:(i + 1) * P], ps_w[:, bank, 0:P], ACT.Copy)\
                        .then_inc(work_free[bank], 1)

                for s in range(STEPS + 4):
                    if s < STEPS:
                        exponents(s)
                    if s >= 4 and s % 2 == 0:
                        move_output((s - 4) // 2)
                    if 2 <= s < STEPS + 2:
                        move_transposed(s - 2)
                    if s < STEPS:
                        scan_inputs(b, slots[EVALS + s])
                for i in range(NT):
                    act.wait_ge(xn_ready["z"], b * NT + i + 1)
                    nc.scalar.activation(silu_z[:, i, :], hz[:, i, :], ACT.Tanh, scale=0.5).then_inc(tanh_z, 1)

            def ffn_head(t):
                transposed("ffn", "xt2", t, True)

            def ffn_masks(t):
                act.wait_ge(router_shift, t + 1)
                nc.scalar.activation(rt[:, 1, :, :], rt[:, 0, :, :], ACT.Exp).then_inc(router_exp, 1)
                for k in range(4):
                    bank = filled(act, ("mask", k), t, True)
                    nc.scalar.activation(mask_t[:, k, :], ps_w[:, bank, :], ACT.Copy).then_inc(work_free[bank], 1)

            def evaluate(t, e):
                f, k = e // 3, e % 3
                act.wait_ge(gu_ready, t * EVALS + e + 1)
                if e >= 2:
                    act.wait_ge(h_ready, t * EVALS + e - 1)
                nc.scalar.activation(gate[:, e % 2, :], ps_a[:, 2 * (f % 2), :], ACT.Tanh, scale=0.5)\
                    .then_inc(tanh_ready, 1)

            act.dma_start(vec[:], vectors).then_inc(loaded["const"], 16)
            act.dma_start(cst[:], constants).then_inc(loaded["const"], 16)
            act.dma_start(win_sb[:], w_in).then_inc(loaded["mamba"], 16)
            act.dma_start(wx_sb[:], w_x).then_inc(loaded["mamba"], 16)
            act.dma_start(wdt_sb[:], w_dt).then_inc(loaded["mamba"], 16)
            act.dma_start(wq_sb[:], wq).then_inc(loaded["att"], 16)
            act.wait_ge(loaded["const"], 32)
            nc.scalar.activation(ident_b[:], ident, ACT.Copy).then_inc(consts_ready, 1)
            nc.scalar.activation(mask_b[:], cst[:, C_MASK:C_MASK + P], ACT.Copy).then_inc(consts_ready, 1)
            nc.scalar.activation(sel_b[:], cst[:, C_SEL:C_SEL + 2 * NS], ACT.Copy).then_inc(consts_ready, 1)
            nc.scalar.activation(decay_rate[:], vec[:, V_AL:V_AL + JT * NS].rearrange("p (j n) -> p j n", n=NS),
                                 ACT.Exp).then_inc(consts_ready, 1)
            act.wait_ge(consts_ready, 7)

            conv_tap(0)
            conv_gate(0)
            split_first(0)
            softplus_parts(0)
            attention(0, PLAN_FIRST)
            with act.Fori(0, BATCH - 1) as t:
                conv_tap(t + 1)
                ffn_head(t)
                conv_gate(t + 1)
                ffn_masks(t)
                split_first(t + 1)
                softplus_parts(t + 1)
                for e in range(EVALS):
                    evaluate(t, e)
                    scan_inputs(t + 1, PLAN_NEXT[e])
                attention(t + 1, PLAN_NEXT)
            ffn_head(BATCH - 1)
            ffn_masks(BATCH - 1)
            for e in range(EVALS):
                evaluate(BATCH - 1, e)

        @block.tensor
        def _(pe):
            def project_in(b):
                pe.wait_ge(loaded["ctx"], 16 * b + 16)
                for j in range(JT):
                    bank = fill(pe, ("xin", j), b)
                    for k in range(CT):
                        mm = nc.tensor.matmul(ps_w[:, bank, :], win_sb[:, k, j * P:(j + 1) * P], ctx_sb[:, k, :],
                                              start=(k == 0), stop=(k == CT - 1))
                    mm.then_inc(work_full[bank], 1)

            def project_x(b):
                for j in range(JT):
                    pe.wait_ge(u_ready, b * JT + j + 1)
                    mm = nc.tensor.matmul(ps_b[:, 1, :], wx_sb[:, j, :], u_sb[:, j, :],
                                          start=(j == 0), stop=(j == JT - 1))
                mm.then_inc(xdbl_full, 1)

            def project_dt(b):
                pe.wait_ge(xdt_ready, b + 1)
                for j in range(JT):
                    bank = fill(pe, ("dt", j), b)
                    nc.tensor.matmul(ps_w[:, bank, :], wdt_sb[:, j * P:(j + 1) * P], xdt_sb[:],
                                     start=True, stop=True).then_inc(work_full[bank], 1)

            def broadcast_bc(b, slot):
                for n in slot["bc"]:
                    if n == 0:
                        pe.wait_ge(bc_stack_ready, b + 1)
                    for c in range(2):
                        bank = fill(pe, ("bc", 2 * n + c), b)
                        pick = sel_b[:, NS * c + n:NS * c + n + 1].to_broadcast([P, P])
                        nc.tensor.matmul(ps_w[:, bank, :], pick, bc_stack[:], start=True, stop=True)\
                            .then_inc(work_full[bank], 1)

            def transpose_normed(kind, name, b, ffn):
                pe.wait_ge(xn_ready[kind], b * NT + NT)
                for k in range(KT):
                    bank = fill(pe, (name, k), b, ffn)
                    for i in range(NT):
                        mm = nc.tensor.transpose(ps_w[:, bank, i * P:(i + 1) * P], xn[:, i, k * P:(k + 1) * P], ident)
                    mm.then_inc(work_full[bank], 1)

            def xt_moved(name, b, ffn):
                for k in (KT - 2, KT - 1):
                    bank, count = use((name, k), b, ffn)
                    pe.wait_ge(work_free[bank], count + 1)

            def attention(b, slots):
                transpose_normed("att", "xt", b, False)
                xt_moved("xt", b, False)
                for n in range(MT + KV_HEADS):
                    name, back = (("q", n), ("qrot", n)) if n < MT else (("k", n - MT), ("krot", n - MT))
                    bank = fill(pe, name, b)
                    for k in range(KT):
                        w = wq_sb[:, k, n * P:(n + 1) * P] if n < MT else wk_sb[:, n - MT, k, :]
                        mm = nc.tensor.matmul(ps_w[:, bank, :], w, xt[:, k, :], start=(k == 0), stop=(k == KT - 1))
                    mm.then_inc(work_full[bank], 1)
                    raw_bank, raw_count = use(name, b)
                    bank = fill(pe, back, b)
                    pe.wait_ge(work_free[raw_bank], raw_count + 1)
                    nc.tensor.matmul(ps_w[:, bank, :], rot, q_raw[:, n % 2, :], start=True, stop=True)\
                        .then_inc(work_full[bank], 1)
                if not first_batch(b):
                    pe.wait_ge(down_ready, b)
                for i in range(NT):
                    for k in range(KT):
                        mm = nc.tensor.matmul(ps_b[:, 0, i * 64:(i + 1) * 64], xt[:, k, i * P:(i + 1) * P],
                                              wv_sb[:, k, :], start=(k == 0), stop=(k == KT - 1))
                mm.then_inc(v_full, 1)
                pe.wait_ge(qk_ready, (b + 1) * (MT + KV_HEADS))
                pe.wait_ge(v_ready, b + 1)
                if not first_batch(b):
                    pe.wait_ge(x3_ready, b * NT)

                def scores(s):
                    m, i, pair = s // (2 * NT), (s // 2) % NT, s % 2
                    if s >= 2:
                        pe.wait_ge(exp_done, b * 2 * STEPS + 2 * (s - 2) + 2)
                    for k in range(2):
                        bank, head = 2 * (s % 2) + k, 2 * pair + k
                        nc.tensor.matmul(ps_a[:, bank, 0:(i + 1) * P], q_t[:, m, i * P:(i + 1) * P],
                                         keys[:, (m * KV_HEADS // MT) * HPT + head, 0:(i + 1) * P],
                                         start=True, stop=False)
                        mm = nc.tensor.matmul(ps_a[:, bank, i * P:(i + 1) * P], ident_b[:], mask_b[:],
                                              start=False, stop=True)
                    mm.then_inc(scores_ready, 1)

                def transpose_probs(s):
                    i = (s // 2) % NT
                    pe.wait_ge(probs_ready, b * STEPS + s + 1)
                    for k in range(2):
                        if s >= 1:
                            pe.wait_ge(pt_ready, b * 2 * STEPS + 2 * (s - 1) + k + 1)
                        for kt in range(i + 1):
                            mm = nc.tensor.transpose(ps_b[:, k, kt * P:(kt + 1) * P],
                                                     probs[:, (2 * s + k) % 4, kt * P:(kt + 1) * P], ident)
                        mm.then_inc(pt_full, 1)

                def weigh_values(g):
                    m, i = g // NT, g % NT
                    bank = fill(pe, ("pv", g), b)
                    pe.wait_ge(pt_ready, b * 2 * STEPS + 4 * g + 4)
                    kv = m * KV_HEADS // MT
                    for kt in range(i + 1):
                        for j in range(HPT):
                            mm = nc.tensor.matmul(ps_w[j * HD:(j + 1) * HD, bank, 0:P],
                                                  v_sb[:, kt, kv * HD:(kv + 1) * HD],
                                                  probs_t[:, j, kt * P:(kt + 1) * P],
                                                  start=(kt == 0), stop=(kt == i), tile_position=(0, j * HD))
                    mm.then_inc(work_full[bank], 1)
                    nc.tensor.nop().then_inc(pv_done, 1)

                for s in range(STEPS + 4):
                    if s < STEPS:
                        scores(s)
                    if s >= 4 and s % 2 == 0:
                        weigh_values((s - 4) // 2)
                    if 2 <= s < STEPS + 2:
                        transpose_probs(s - 2)
                    if s < STEPS:
                        broadcast_bc(b, slots[EVALS + s])
                for g in (MT * NT - 2, MT * NT - 1):
                    bank, count = use(("pv", g), b)
                    pe.wait_ge(work_free[bank], count + 1)
                for i in range(NT):
                    bank = fill(pe, ("op", i), b)
                    for m in range(MT):
                        mm = nc.tensor.matmul(ps_w[:, bank, :], attn_t[:, m, i * P:(i + 1) * P], wo_sb[:, m, :],
                                              start=(m == 0), stop=(m == MT - 1))
                    mm.then_inc(work_full[bank], 1)
                pe.wait_ge(gated_ready, b * JT + JT)
                for i in range(NT):
                    bank = fill(pe, ("yt", i), b)
                    for j in range(JT):
                        mm = nc.tensor.transpose(ps_w[:, bank, j * P:(j + 1) * P], silu_z[:, j, i * P:(i + 1) * P], ident)
                    mm.then_inc(work_full[bank], 1)

            def base_half(t, f, half):
                slot = f % WSLOTS
                if half == 0:
                    of_slot = (FT - slot + WSLOTS - 1) // WSLOTS
                    pe.wait_ge(w_loaded[slot], 16 * (t * of_slot + f // WSLOTS + 1))
                    if f >= 2:
                        pe.wait_ge(h_ready, t * EVALS + 3 * (f - 2) + 3)
                at = WU if half else WG
                for k in range(KT):
                    mm = nc.tensor.matmul(ps_a[:, 2 * (f % 2) + half, :], w_sb[:, slot, at + k * P:at + (k + 1) * P],
                                          xt[:, k, :], start=(k == 0), stop=False, skip_group_check=True)
                if half == 1:
                    mm.then_inc(gu_ready, 1)

            def add_slot(t, f, k):
                pe.wait_ge(h_ready, t * EVALS + 3 * f + k)
                for half, at in ((0, BG), (1, BU)):
                    mm = nc.tensor.matmul(ps_a[:, 2 * (f % 2) + half, :], w_sb[:, f % WSLOTS, at:at + P],
                                          low[:, 2 * half + k - 1, :], start=False, stop=(k == 2),
                                          skip_group_check=True)
                mm.then_inc(gu_ready, 1)

            def down_adapter(t, f, k):
                pe.wait_ge(h_ready, t * EVALS + 3 * f + 1 + k)
                mm = nc.tensor.matmul(ps_b[:, k - 1, :], w_sb[:, f % WSLOTS, AD:AD + P], hk[:, (2 * f + k - 1) % 4, :],
                                      start=(f == 0), stop=(f == FT - 1), skip_group_check=True)
                if k == 2:
                    mm.then_inc(d_done, 1)

            def ffn_head(t):
                transpose_normed("ffn", "xt2", t, True)
                xt_moved("xt2", t, True)
                for i in range(NT):
                    for k in range(KT):
                        mm = nc.tensor.matmul(ps_b[:, 0, i * NE:(i + 1) * NE], xt[:, k, i * P:(i + 1) * P],
                                              wr_sb[:, k, :], start=(k == 0), stop=(k == KT - 1))
                mm.then_inc(router_full, 1)
                base_half(t, 0, 0)
                base_half(t, 0, 1)

            def ffn_masks(t):
                pe.wait_ge(expanded_ready, 4 * t + 4)
                for k in range(4):
                    bank = fill(pe, ("mask", k), t, True)
                    for i in range(NT):
                        mm = nc.tensor.transpose(ps_w[:, bank, i * P:(i + 1) * P], expanded[:, k, i * P:(i + 1) * P],
                                                 ident)
                    mm.then_inc(work_full[bank], 1)
                for half, name in ((0, "lowg"), (1, "lowu")):
                    bank = fill(pe, (name, 0), t, True)
                    for k in range(KT):
                        mm = nc.tensor.matmul(ps_w[:, bank, :], lora_sb[:, half, k, :], xt[:, k, :],
                                              start=(k == 0), stop=(k == KT - 1))
                    mm.then_inc(work_full[bank], 1)

            def ffn_tiles(t, b, slots):
                pe.wait_ge(low_ready, 4 * t + 4)
                if b is not None:
                    pe.wait_ge(xdt_ready, b + 1)
                for f in range(FT):
                    add_slot(t, f, 1)
                    if b is not None:
                        broadcast_bc(b, slots[3 * f])
                    if f + 1 < FT:
                        base_half(t, f + 1, 0)
                    if f > 0:
                        down_adapter(t, f - 1, 1)
                    add_slot(t, f, 2)
                    if b is not None:
                        broadcast_bc(b, slots[3 * f + 1])
                    if f + 1 < FT:
                        base_half(t, f + 1, 1)
                    if f > 0:
                        down_adapter(t, f - 1, 2)
                    if b is not None:
                        broadcast_bc(b, slots[3 * f + 2])
                down_adapter(t, FT - 1, 1)
                down_adapter(t, FT - 1, 2)
                for f in range(FT):
                    of_slot = (FT - f % 2 + 1) // 2
                    pe.wait_ge(wd_loaded[f % 2], 16 * (t * of_slot + f // 2 + 1))
                    for i in range(NT):
                        mm = nc.tensor.matmul(ps_a[:, i, :], hb[:, f, i * P:(i + 1) * P], wd_sb[:, f % 2, :],
                                              start=(f == 0), stop=False, skip_group_check=True)
                    mm.then_inc(wd_used, 1)
                pe.wait_ge(down_ready, t + 1)
                for i in range(NT):
                    nc.tensor.matmul(ps_a[:, i, :], down_low[:, i * P:(i + 1) * P], bd_sb[:],
                                     start=False, stop=True, skip_group_check=True).then_inc(out_full, 1)

            pe.wait_ge(consts_ready, 7)
            pe.wait_ge(loaded["mamba"], 48)
            project_in(0)
            project_x(0)
            project_dt(0)
            pe.wait_ge(loaded["att"], 64)
            attention(0, PLAN_FIRST)
            pe.wait_ge(loaded["ffn"], 48)
            with pe.Fori(0, BATCH - 1) as t:
                project_in(t + 1)
                ffn_head(t)
                project_x(t + 1)
                ffn_masks(t)
                project_dt(t + 1)
                ffn_tiles(t, t + 1, PLAN_NEXT)
                attention(t + 1, PLAN_NEXT)
            ffn_head(BATCH - 1)
            ffn_masks(BATCH - 1)
            ffn_tiles(BATCH - 1, None, None)

        @block.vector
        def _(dve):
            tt, ts, stt = nc.vector.tensor_tensor, nc.vector.tensor_scalar, nc.vector.scalar_tensor_tensor

            def normalize(kind, b, src, dst):
                chain = Count(norm_chain[kind], 9, b)
                for i in range(NT):
                    chain.inc(nc.vector.bn_stats(stats[:, i, :], src[:, i, :]))
                dve.wait_ge(norm_chain[kind], b * 9 + 4)
                nc.vector.tensor_copy(scrap[:], vec[0:1, 0:1])
                for i in range(NT):
                    chain.inc(nc.vector.bn_aggr(mv[:, i, :], stats[:, i, :]))
                dve.wait_ge(norm_chain[kind], b * 9 + 8)
                chain.inc(ts(var_eps[:], mv[:, :, 1], EPS, None, ALU.add))
                chain.end()
                dve.wait_ge(rstd_ready[kind], b + 1)
                for i in range(NT):
                    ts(dst[:, i, :], src[:, i, :], mv[:, i, 0:1], rstd[:, i:i + 1], ALU.subtract, ALU.mult)\
                        .then_inc(xn_ready[kind], 1)

            def convolve(b):
                chain = Count(conv_chain, 3 * JT, b)
                for j in range(JT):
                    bank = use(("xin", j), b)[0]
                    dve.wait_ge(tap_ready, b * JT + j + 1)
                    for back in range(1, TAPS):
                        tap = conv_half[:, TAPS * j + TAPS - 1 - back:TAPS * j + TAPS - back]
                        op = stt(conv_sb[:, j, back:L], ps_w[:, bank, 0:L - back], tap, conv_sb[:, j, back:L],
                                 ALU.mult, ALU.add)
                        chain.link(dve, op)
                    nc.vector.tensor_copy(scrap[:], ps_w[0:1, bank, 0:1]).then_inc(work_free[bank], 1)
                chain.end()
                for j in range(JT):
                    dve.wait_ge(conv_tanh, b * JT + j + 1)
                    stt(u_sb[:, j, :], exp_v[:, j, :], 1.0, conv_sb[:, j, :], ALU.add, ALU.mult).then_inc(u_ready, 1)

            def split_bc(b):
                chain = Count(split_chain, 3, b)
                dve.wait_ge(xdt_ready, b + 1)
                nc.vector.tensor_copy(bc_stack[32:64, :], xdt_sb[32:64, :])
                chain.link(dve, nc.vector.tensor_copy(split_b[64:128, :], xdt_sb[64:128, :]))
                chain.link(dve, tt(split_f[64:128, :], xdt_sb[64:128, :], split_b[64:128, :], ALU.subtract))
                nc.vector.tensor_copy(bc_stack[64:96, :], split_f[64:96, :])
                chain.link(dve, nc.vector.tensor_copy(split_b[96:128, :], split_f[96:128, :]))
                tt(bc_stack[96:128, :], split_f[96:128, :], split_b[96:128, :], ALU.subtract).then_inc(bc_stack_ready, 1)
                chain.end()

            def scan_piece(b, piece):
                kind, n = piece
                if kind == "poly":
                    if n == 0:
                        dve.wait_ge(softplus_in, b + 1)
                        ts(du_sb[:], exp_v, POLY[-1], None, ALU.mult).then_inc(poly_chain, 1)
                    elif n < NPOLY:
                        dve.wait_ge(poly_chain, b * (NPOLY + 2) + n)
                        stt(du_sb[:].rearrange("p j l -> p (j l)"), du_sb[:].rearrange("p j l -> p (j l)"),
                            POLY[NPOLY - 1 - n], exp_v.rearrange("p j l -> p (j l)"), ALU.add, ALU.mult)\
                            .then_inc(poly_chain, 1)
                    elif n == NPOLY:
                        dve.wait_ge(poly_chain, b * (NPOLY + 2) + n)
                        tt(dt_sb[:], du_sb[:], relu_v, ALU.add).then_inc(poly_chain, 1)
                    else:
                        dve.wait_ge(poly_chain, b * (NPOLY + 2) + n)
                        tt(du_sb[:], dt_sb[:], u_sb, ALU.mult).then_inc(poly_chain, 1)
                        nc.vector.memset(decay[:, :, :, 0:1], 0.0).then_inc(dt_ready, 1)
                    return
                base = b * 3 * NS + 3 * n
                flat = state[:, n % 2, :, :].rearrange("p j l -> p (j l)")
                if kind == "mul":
                    if n == 0:
                        dve.wait_ge(poly_chain, (b + 1) * (NPOLY + 2))
                        dve.wait_ge(y_init, b * JT + JT)
                    elif n >= 2:
                        dve.wait_ge(y_added, b * NS + n - 1)
                    bank, count = use(("bc", 2 * n), b)
                    dve.wait_ge(work_free[bank], count + 1)
                    row = bc_sb[:, n % 2, 0, :].unsqueeze(1).to_broadcast([P, JT, L])
                    tt(state[:, n % 2, :, :], du_sb[:], row, ALU.mult).then_inc(scan_chain, 1)
                elif kind == "run":
                    dve.wait_ge(decay_ready, b * JT * NS + JT * n + JT)
                    dve.wait_ge(dt_ready, b + 1)
                    dve.wait_ge(scan_chain, base + 1)
                    nc.vector.tensor_tensor_scan(flat, decay[:, n % 2, :, :].rearrange("p j l -> p (j l)"), flat, 0.0,
                                                 ALU.mult, ALU.add).then_inc(scan_chain, 1)
                else:
                    bank, count = use(("bc", 2 * n + 1), b)
                    dve.wait_ge(work_free[bank], count + 1)
                    dve.wait_ge(scan_chain, base + 2)
                    row = bc_sb[:, n % 2, 1, :].unsqueeze(1).to_broadcast([P, JT, L])
                    tt(state[:, n % 2, :, :], state[:, n % 2, :, :], row, ALU.mult).then_inc(scan_chain, 1)

            def attention(b, slots):
                total = MT + KV_HEADS
                chain = Count(rope_chain, 2 * total, b)
                for n in range(total):
                    raw = ("q", n) if n < MT else ("k", n - MT)
                    raw_bank, raw_count = use(raw, b)
                    dve.wait_ge(work_free[raw_bank], raw_count + 1)
                    chain.inc(tt(rope_tmp, q_raw[:, n % 2, :], cos_t, ALU.mult))
                    back = ("qrot", n) if n < MT else ("krot", n - MT)
                    bank = filled(dve, back, b)
                    part = q_t[:, n, :] if n < MT else split_f[:]
                    tt(part, ps_w[:, bank, :], sin_t, ALU.mult).then_inc(work_free[bank], 1)
                    chain.link(dve, nc.vector.tensor_copy(scrap[:], sin_t[0:1, 0:1]))
                    bank2, count2 = use(back, b)
                    dve.wait_ge(work_free[bank2], count2 + 1)
                    if n < MT:
                        tt(part, part, rope_tmp, ALU.add).then_inc(qk_ready, 1)
                    else:
                        if n == MT:
                            dve.wait_ge(keys_zero, b + 1)
                        for j in range(HPT):
                            rows = slice(j * HD, (j + 1) * HD)
                            op = tt(keys[rows, (n - MT) * HPT + j, :], split_f[rows, :], rope_tmp[rows, :], ALU.add)
                        op.then_inc(qk_ready, 1)
                    dve.wait_ge(qk_ready, b * total + n + 1)
                chain.end()
                dve.wait_ge(v_full, b + 1)
                tt(v_sb[:], ps_b[:, 0, 0:NT * 64].rearrange("p (i d) -> p i d", i=NT),
                   vec[:, V_BV:V_BV + 64].unsqueeze(1).to_broadcast([P, NT, 64]), ALU.add).then_inc(v_ready, 1)

                def maxima(s):
                    i = (s // 2) % NT
                    dve.wait_ge(scores_ready, b * STEPS + s + 1)
                    nc.vector.tensor_reduce(neg_max[:, s % 2, :], ps_a[:, 2 * (s % 2):2 * (s % 2) + 2, 0:(i + 1) * P],
                                            AX.X, ALU.max).then_inc(max_chain, 1)
                    dve.wait_ge(max_chain, b * STEPS + s + 1)
                    ts(bias_max[:, s % 2, :], neg_max[:, s % 2, :], -SCALE, None, ALU.mult).then_inc(bias_ready, 1)

                def divide(s):
                    i = (s // 2) % NT
                    dve.wait_ge(exp_done, b * 2 * STEPS + 2 * s + 2)
                    nc.vector.reciprocal(row_inv[:, s % 2, :], row_sum[:, s % 2, :]).then_inc(inv_chain, 1)
                    dve.wait_ge(inv_chain, b * STEPS + s + 1)
                    for k in range(2):
                        place = probs[:, (2 * s + k) % 4, 0:(i + 1) * P]
                        op = ts(place, place, row_inv[:, s % 2, k:k + 1], None, ALU.mult)
                    op.then_inc(probs_ready, 1)

                for s in range(STEPS + 1):
                    if s < STEPS:
                        maxima(s)
                    if s >= 1:
                        divide(s - 1)
                    if s < STEPS:
                        for piece in slots[EVALS + s]["dve"]:
                            scan_piece(b, piece)
                for i in range(NT):
                    bank = filled(dve, ("op", i), b)
                    tt(xa[:, i, :], ps_w[:, bank, :], xa[:, i, :], ALU.add).then_inc(work_free[bank], 1)
                for k in (NT - 2, NT - 1):
                    bank, count = use(("op", k), b)
                    dve.wait_ge(work_free[bank], count + 1)
                normalize("z", b, xa, hz)
                chain = Count(z_chain, NT, b)
                for i in range(NT):
                    dve.wait_ge(tanh_z, b * NT + i + 1)
                    chain.inc(stt(silu_z[:, i, :], silu_z[:, i, :], 1.0, hz[:, i, :], ALU.add, ALU.mult))
                chain.end()
                dve.wait_ge(y_added, b * NS + NS)
                dve.wait_ge(z_chain, b * NT + NT)
                for i in range(NT):
                    stt(silu_z[:, i, :], y_sb[:, i, :], 0.5, silu_z[:, i, :], ALU.mult, ALU.mult)\
                        .then_inc(gated_ready, 1)
                if not first_batch(b):
                    dve.wait_ge(stored, b * 16 * NT)
                for i in range(NT):
                    bank = filled(dve, ("yt", i), b)
                    tt(xb[:, i, :], ps_w[:, bank, :], xa[:, i, :], ALU.add).then_inc(work_free[bank], 1)
                for k in (NT - 2, NT - 1):
                    bank, count = use(("yt", k), b)
                    dve.wait_ge(work_free[bank], count + 1)
                nc.vector.tensor_copy(scrap[:], vec[0:1, 0:1]).then_inc(x2_ready, 1)

            def route(t):
                logits, prob, onehot, second = rt[:, 0], rt[:, 1], rt[:, 2], rt[:, 3]
                rank, tmp = rt[:, 4], rt[:, 5]
                cand = cst[:, C_CAND:C_CAND + NE].unsqueeze(1).to_broadcast([P, NT, NE])

                def spread(v):
                    return v.unsqueeze(2).to_broadcast([P, NT, NE])

                chain = Count(router_chain, 18, t)

                def then(op):
                    chain.link(dve, op)

                raw = ps_b[:, 0, 0:NT * NE].rearrange("p (i e) -> p i e", i=NT)
                dve.wait_ge(router_full, t + 1)
                then(nc.vector.tensor_reduce(rs[:, 0, :], raw, AX.X, ALU.max))
                tt(logits, raw, spread(rs[:, 0, :]), ALU.subtract).then_inc(router_shift, 1)
                dve.wait_ge(router_exp, t + 1)
                then(nc.vector.tensor_reduce(rs[:, 1, :], prob, AX.X, ALU.add))
                then(nc.vector.reciprocal(rs[:, 2, :], rs[:, 1, :]))
                then(tt(prob, prob, spread(rs[:, 2, :]), ALU.mult))

                def pick(source, weight, winner):
                    then(nc.vector.tensor_reduce(weight, source, AX.X, ALU.max))
                    then(tt(rank, source, spread(weight), ALU.is_equal))
                    then(tt(rank, rank, cand, ALU.mult))
                    then(nc.vector.tensor_reduce(rs[:, 5, :], rank, AX.X, ALU.max))
                    then(tt(winner, rank, spread(rs[:, 5, :]), ALU.is_equal))

                pick(prob, rs[:, 3, :], onehot)
                then(stt(tmp, onehot, -2.0, prob, ALU.mult, ALU.add))
                pick(tmp, rs[:, 4, :], second)

                then(tt(rt[:, 6], second, onehot, ALU.subtract))
                then(tt(rt[:, 7], onehot, spread(rs[:, 3, :]), ALU.mult))
                then(tt(rt[:, 5], second, spread(rs[:, 4, :]), ALU.mult))
                for k, table in enumerate((onehot, rt[:, 6], rt[:, 7], rt[:, 5])):
                    wide = expanded[:, k, :].rearrange("p (ie r) -> p ie r", r=LR)
                    narrow = table.rearrange("p i e -> p (i e)").unsqueeze(2).to_broadcast([P, NT * NE, LR])
                    ts(wide, narrow, 2.0, None, ALU.mult).then_inc(expanded_ready, 1)
                chain.end()

            def mask_low(t):
                for k in (2, 3):
                    bank, count = use(("mask", k), t, True)
                    dve.wait_ge(work_free[bank], count + 1)
                for half, name in ((0, "lowg"), (1, "lowu")):
                    bank = filled(dve, (name, 0), t, True)
                    tt(low[:, 2 * half, :], ps_w[:, bank, :], mask_t[:, 0, :], ALU.mult).then_inc(low_ready, 1)
                    tt(low[:, 2 * half + 1, :], ps_w[:, bank, :], mask_t[:, 1, :], ALU.mult).then_inc(low_ready, 1)
                    dve.wait_ge(low_ready, 4 * t + 2 * half + 2)
                    nc.vector.tensor_copy(scrap[:], ps_w[0:1, bank, 0:1]).then_inc(work_free[bank], 1)

            def evaluate(t, e):
                f, k = e // 3, e % 3
                bank = 2 * (f % 2)
                dve.wait_ge(tanh_ready, t * EVALS + e + 1)
                stt(gate[:, e % 2, :], gate[:, e % 2, :], 1.0, ps_a[:, bank, :], ALU.add, ALU.mult)\
                    .then_inc(gate_chain, 1)
                if k > 0 and f >= 2:
                    dve.wait_ge(d_done, t * FT + f - 1)
                dst = hb[:, f, :] if k == 0 else hk[:, (2 * f + k - 1) % 4, :]
                dve.wait_ge(gate_chain, t * EVALS + e + 1)
                tt(dst, gate[:, e % 2, :], ps_a[:, bank + 1, :], ALU.mult).then_inc(h_ready, 1)

            def ffn_end(t):
                dve.wait_ge(d_done, t * FT + FT)
                chain = Count(down_chain, 2, t)
                chain.inc(tt(mask_t[:, 2, :], ps_b[:, 0, :], mask_t[:, 2, :], ALU.mult))
                chain.link(dve, tt(mask_t[:, 3, :], ps_b[:, 1, :], mask_t[:, 3, :], ALU.mult))
                tt(down_low, mask_t[:, 2, :], mask_t[:, 3, :], ALU.add).then_inc(down_ready, 1)
                chain.end()
                for i in range(NT):
                    dve.wait_ge(out_full, t * NT + i + 1)
                    stt(xb[:, i, :], ps_a[:, i, :], 0.5, xb[:, i, :], ALU.mult, ALU.add).then_inc(x3_ready, 1)

            dve.wait_ge(consts_ready, 4)
            ts(decay_rate[:], decay_rate[:], -1.0, None, ALU.mult).then_inc(consts_ready, 1)
            ts(conv_half[:], vec[:, V_CW:V_CW + 20], 0.5, None, ALU.mult).then_inc(consts_ready, 1)
            nc.vector.memset(bc_stack[0:32, :], 0.0).then_inc(consts_ready, 1)
            dve.wait_ge(consts_ready, 7)
            dve.wait_ge(loaded["x"], 16)
            normalize("att", 0, xa, xn)
            convolve(0)
            split_bc(0)
            attention(0, PLAN_FIRST)
            with dve.Fori(0, BATCH - 1) as t:
                dve.wait_ge(x2_ready, t + 1)
                normalize("ffn", t, xb, xn)
                convolve(t + 1)
                route(t)
                split_bc(t + 1)
                mask_low(t)
                for e in range(EVALS):
                    evaluate(t, e)
                    for piece in PLAN_NEXT[e]["dve"]:
                        scan_piece(t + 1, piece)
                ffn_end(t)
                dve.wait_ge(loaded["x"], 16 * t + 32)
                normalize("att", t + 1, xa, xn)
                attention(t + 1, PLAN_NEXT)
            dve.wait_ge(x2_ready, BATCH)
            normalize("ffn", BATCH - 1, xb, xn)
            route(BATCH - 1)
            mask_low(BATCH - 1)
            for e in range(EVALS):
                evaluate(BATCH - 1, e)
            ffn_end(BATCH - 1)


def constant_table():
    import numpy as np
    c = np.zeros((P, C_COLS), np.float32)
    p = np.arange(P)
    c[:, C_ID:C_ID + P] = np.eye(P)
    half = HD // 2
    for m in range(P):
        if m % HD < half:
            c[m + half, C_ROT + m] = -1.0
        else:
            c[m - half, C_ROT + m] = 1.0
    c[:, C_MASK:C_MASK + P] = np.where(p[None, :] <= p[:, None], 0.0, NEG)
    for k in range(32, P):
        c[k, C_SEL + k % 32] = 1.0
    inv = (np.float32(10000.0) ** (-np.arange(half, dtype=np.float32) / np.float32(half))).astype(np.float32)
    ang = (np.arange(L, dtype=np.float32)[None, :] * inv[p % half][:, None]).astype(np.float32)
    c[:, C_COS:C_COS + L] = np.cos(ang)
    c[:, C_SIN:C_SIN + L] = np.sin(ang)
    c[:, C_CAND:C_CAND + NE] = np.arange(NE, 0, -1)
    c[:, C_HALF:C_HALF + NT] = -0.5
    return c


def kernel(**inputs):
    import numpy as np
    import concourse.bacc as bacc
    from concourse.bass_utils import run_bass_kernel_spmd

    a = {k: np.asarray(v) for k, v in inputs.items()}

    def rows(w):
        return w.reshape(-1, P, w.shape[1]).transpose(1, 0, 2)

    def column(v):
        return v.reshape(-1, P).T

    wk4 = [rows(np.tile(a["L0_attn_wk"][g * HD:(g + 1) * HD].T, (1, HPT))) for g in range(KV_HEADS)]
    xw = a["L0_xattn_x_proj_w"].T
    bc = xw[:, RANK:]
    w_x = rows(np.concatenate([xw[:, :RANK], np.zeros((DI, 16), np.float32), bc, bc, bc], axis=1))
    w_dt = np.zeros((P, DI), np.float32)
    w_dt[:RANK] = a["L0_xattn_dt_proj_w"].T

    def adapters(w):
        return rows(w.reshape(NE * LR, D).T)

    wg, wu = rows(a["L0_ffn_Wg"].T), rows(a["L0_ffn_Wu"].T)
    bg = a["L0_ffn_Bg"].transpose(0, 2, 1).reshape(NE * LR, DFF)
    bu = a["L0_ffn_Bu"].transpose(0, 2, 1).reshape(NE * LR, DFF)
    ad = a["L0_ffn_Ad"].reshape(NE * LR, DFF).T
    tiles = []
    for f in range(FT):
        cols = slice(f * P, (f + 1) * P)
        tiles.append(np.concatenate([wg[:, :, cols].reshape(P, -1), wu[:, :, cols].reshape(P, -1),
                                     bg[:, cols], bu[:, cols], ad[cols, :]], axis=1))
    vectors = np.concatenate([
        a["L0_xattn_conv_w"].reshape(JT, P, TAPS).transpose(1, 0, 2).reshape(P, -1),
        column(a["L0_xattn_conv_b"]), column(a["L0_xattn_dt_proj_b"]),
        a["L0_xattn_A_log"].reshape(JT, P, NS).transpose(1, 0, 2).reshape(P, -1),
        column(a["L0_xattn_D"]), column(a["L0_attn_bq"]),
        np.stack([np.tile(a["L0_attn_bk"][g * HD:(g + 1) * HD], HPT) for g in range(KV_HEADS)], axis=1),
        np.tile(a["L0_attn_bv"][None, :], (P, 1)),
    ], axis=1)
    arrays = {
        "x": a["x"],
        "ctx_t": a["ctx_1024"].transpose(0, 2, 1),
        "wq": rows(a["L0_attn_wq"].T),
        "wk": np.stack(wk4, axis=1),
        "wv": rows(a["L0_attn_wv"].T),
        "wo": rows(a["L0_attn_wo"].T),
        "w_in": rows(a["L0_xattn_in_proj_w"].T),
        "w_x": w_x,
        "w_dt": w_dt,
        "w_lora": np.stack([adapters(a["L0_ffn_Ag"]), adapters(a["L0_ffn_Au"])], axis=1),
        "w_r": rows(a["L0_ffn_Wr"].T),
        "b_down": a["L0_ffn_Bd"].transpose(0, 2, 1).reshape(NE * LR, D),
        "w_tiles": np.stack(tiles),
        "w_down": a["L0_ffn_Wd"].T.reshape(FT, P, D),
        "vectors": vectors,
        "constants": constant_table(),
    }
    arrays = {k: np.ascontiguousarray(v) for k, v in arrays.items()}
    nc = bacc.Bacc("TRN2", target_bir_lowering=False, num_devices=1, dynamic_dma_scratch_size=1024)
    args = [nc.dram_tensor("in_" + k, v.shape, mybir.dt.from_np(v.dtype), kind="ExternalInput").ap()
            for k, v in arrays.items()]
    args.append(nc.dram_tensor("out_x", (BATCH, L, D), F32, kind="ExternalOutput").ap())
    decoder_layer(nc, *args)
    r = run_bass_kernel_spmd(nc, [{"in_" + k: v for k, v in arrays.items()}], core_ids=[0])
    return r.results[0]["out_x"]
```

```python
from contextlib import ExitStack

import concourse.bass as bass
from concourse import mybir

F32 = mybir.dt.float32
BF16 = mybir.dt.bfloat16
ALU = mybir.AluOpType
ACT = mybir.ActivationFunctionType
AX = mybir.AxisListType

P = 128
BATCH, L, D = 4, 512, 512
HEADS, KV_HEADS, HD = 16, 2, 32
NT = L // P
KT = D // P
MT = HEADS * HD // P
HPT = P // HD
CTX = 256
CT = CTX // P
DI = 512
JT = DI // P
NS = 16
RANK = 16
TAPS = 4
DFF = 1408
FT = DFF // P
NE, LR = 8, 16
EPS = 1e-5
SCALE = HD ** -0.5
NEG = -1e30

WG, WU, WBASE = 0, KT * P, 2 * KT * P
BG, BU, WADAPT = 0, P, 2 * P
C_ID, C_ROT, C_MASK, C_SEL, C_COS, C_SIN = 0, 128, 256, 384, 416, 928
C_CAND, C_HALF = 1440, 1448
C_COLS = 1452
V_CW, V_CB, V_DTB, V_AL, V_D, V_BQ, V_BK, V_BV = 0, 16, 20, 24, 88, 92, 96, 98
V_COLS = 98 + KV_HEADS * HD

def log1p_coefficients(degree):
    import numpy as np
    nodes = 0.5 + 0.5 * np.cos(np.pi * (np.arange(64) + 0.5) / 64)
    fit = np.polynomial.Chebyshev.fit(nodes, np.log1p(nodes) / nodes, degree, domain=[0, 1])
    return [float(c) for c in fit.convert(kind=np.polynomial.Polynomial).coef]


POLY = log1p_coefficients(9)
NPOLY = len(POLY)


EVAL = [(0, 0)]
for _f in range(FT):
    EVAL += [(_f, 1)] + [(_f + 1, 0)] * (_f + 1 < FT) + [(_f, 2)]
EVAL_AT = {fk: e for e, fk in enumerate(EVAL)}
EVALS = len(EVAL)
STEPS = MT * NT * 2
DOWN = EVALS
ATT = DOWN + FT
SLOTS = ATT + STEPS
NORM_SLOT = EVAL_AT[8, 2]


def plan(counts):
    pieces = [("poly", k) for k in range(NPOLY + 2)]
    for n in range(NS):
        pieces += [("mul", n), ("run", n), ("out", n)]
    assert sum(counts) == len(pieces), (sum(counts), len(pieces))
    slots, at, k = [{"dve": [], "bc": [], "decay": [], "add": []} for _ in range(SLOTS)], {}, 0
    for s, count in enumerate(counts):
        for piece in pieces[k:k + count]:
            slots[s]["dve"].append(piece)
            at[piece] = s
        k += count
    for n in range(NS):
        slots[at["poly", NPOLY - 4] if n < 2 else at["out", n - 2]]["bc"].append(n)
        slots[at["poly", NPOLY + 1] if n < 2 else at["run", n - 2]]["decay"].append(n)
        slots[at["out", n]]["add"].append(n)
    return slots


def spread_over(total, places):
    return [(k + 1) * total // places - k * total // places for k in range(places)]


PIECES = NPOLY + 2 + 3 * NS
IN_EVALS = [(0, 2, 1)[k] for f, k in EVAL]
IN_DOWN = 11
PLAN_FIRST = plan([0] * ATT + spread_over(PIECES, STEPS))
PLAN_NEXT = plan(IN_EVALS + spread_over(IN_DOWN, FT) + spread_over(PIECES - sum(IN_EVALS) - IN_DOWN, STEPS))


def projections(f):
    raw = f - 1 if 1 <= f <= MT + KV_HEADS else None
    back = f - 2 if 2 <= f <= MT + KV_HEADS + 1 else None
    return raw, back, f == MT + KV_HEADS + 2


def broadcasts(slots, s):
    return [("bc", 2 * n + c) for n in slots[s]["bc"] for c in range(2)]


def uses_of(first, last):
    names = []
    if not last:
        names += [("xin", j) for j in range(JT)]
    if first:
        names += [("dt", j) for j in range(JT)]
    else:
        names += [("xt2", k) for k in range(KT)] + [("mask", k) for k in range(4)] + [("lowg", 0), ("lowu", 0)]
        if not last:
            names += [("dt", j) for j in range(JT)]
            for e in range(EVALS):
                names += broadcasts(PLAN_NEXT, e)
    if not last:
        slots = PLAN_FIRST if first else PLAN_NEXT
        for f in range(FT):
            if f == 0:
                names += [("xt", k) for k in range(KT)]
            raw, back, _ = projections(f)
            names += [("raw", raw)] * (raw is not None) + [("back", back)] * (back is not None)
            if not first:
                names += broadcasts(slots, DOWN + f)
        for s in range(STEPS + 4):
            if s >= 4 and s % 2 == 0:
                names.append(("pv", (s - 4) // 2))
            if s < STEPS:
                names += broadcasts(slots, ATT + s)
        names += [("op", i) for i in range(NT)] + [("yt", i) for i in range(NT)]
    return {name: k for k, name in enumerate(names)}


USES_FIRST, USES_NEXT, USES_LAST = uses_of(True, False), uses_of(False, False), uses_of(False, True)
assert len(USES_FIRST) % 2 == 0 and len(USES_NEXT) % 2 == 0


def decoder_layer(nc, x, ctx_t, wq, wk, wv, wo, w_in, w_x, w_dt, w_lora, w_r, b_down, a_down, w_tiles, w_adapt, w_down,
                  vectors, constants, out):
    with ExitStack() as stack:
        def sb(name, shape, dt=F32):
            return stack.enter_context(nc.sbuf_tensor(name, shape, dt))

        def ps(name, shape):
            return stack.enter_context(nc.psum_tensor(name, shape, F32))

        def sem(name):
            return stack.enter_context(nc.semaphore(name))

        wq_sb = sb("wq_sb", [P, KT, HEADS * HD])
        wk_sb = sb("wk_sb", [P, KV_HEADS, KT, P])
        wv_sb = sb("wv_sb", [P, KT, KV_HEADS * HD])
        wo_sb = sb("wo_sb", [P, MT, D])
        win_sb = sb("win_sb", [P, CT, DI])
        wx_sb = sb("wx_sb", [P, JT, P])
        wdt_sb = sb("wdt_sb", [P, DI])
        lora_sb = sb("lora_sb", [P, 2, KT, P])
        wr_sb = sb("wr_sb", [P, KT, NE])
        bd_sb = sb("bd_sb", [P, D])
        ad_sb = sb("ad_sb", [P, FT, P])
        vec = sb("vec", [P, V_COLS])
        cst = sb("cst", [P, C_COLS])
        ident_b = sb("ident_b", [P, P], BF16)
        mask_b = sb("mask_b", [P, P], BF16)
        sel_b = sb("sel_b", [P, 2 * NS], BF16)
        decay_rate = sb("decay_rate", [P, JT, NS])
        conv_half = sb("conv_half", [P, 20])
        ident = cst[:, C_ID:C_ID + P]
        rot = cst[:, C_ROT:C_ROT + P]
        cos_t, sin_t = cst[:, C_COS:C_COS + L], cst[:, C_SIN:C_SIN + L]
        xa = sb("xa", [P, NT, D])
        xb = sb("xb", [P, NT, D])
        xt = sb("xt", [P, KT, L])
        r1 = sb("r1", [P, 12, L])
        probs, probs_t, xn, hb = r1[:, 0:4, :], r1[:, 4:8, :], r1[:, 8:12, :], r1[:, 0:FT, :]
        attn_t, down_low = xn, r1[:, FT, :]
        xn_att = sb("xn_att", [P, NT, D])
        hz, silu_z = r1[:, 0:4, :], r1[:, 4:8, :]
        r2 = sb("r2", [P, 15, L])
        keys, q_t, q_raw, rope_tmp = r2[:, 0:8, :], r2[:, 8:12, :], r2[:, 12:14, :], r2[:, 14, :]
        gate, hk, low, mask_t = r2[:, 0:2, :], r2[:, 2:6, :], r2[:, 6:10, :], r2[:, 10:14, :]
        expanded = r2[:, 2:6, :]
        v_sb = sb("v_sb", [P, NT, KV_HEADS * HD])
        w_sb = sb("w_sb", [P, 2, WBASE])
        wb_sb = sb("wb_sb", [P, 2, WADAPT])
        wd_sb = sb("wd_sb", [P, 2, D])
        ctx_sb = xn_att[:, 0:CT, :]
        dt_sb = sb("dt_sb", [P, JT, L])
        du_sb = sb("du_sb", [P, JT, L])
        y_sb = sb("y_sb", [P, JT, L])
        state = sb("state", [P, 2, JT, L])
        decay = sb("decay", [P, 2, JT, L])
        bc_sb = sb("bc_sb", [P, 2, 2, L])
        xdt_sb = sb("xdt_sb", [P, L])
        bc_stack = sb("bc_stack", [P, L], BF16)
        split_f = sb("split_f", [P, L])
        split_b = sb("split_b", [P, L], BF16)
        u_sb, exp_v, relu_v, conv_sb = state[:, 0, :, :], state[:, 1, :, :], decay[:, 0, :, :], decay[:, 1, :, :]
        scrap = sb("scrap", [1, 1])
        scrap_a = sb("scrap_a", [1, 1])
        stats = sb("stats", [P, NT, 6])
        mv = sb("mv", [P, NT, 2])
        var_eps = sb("var_eps", [P, NT])
        rstd = sb("rstd", [P, NT])
        neg_max = sb("neg_max", [P, 2, 2])
        bias_max = sb("bias_max", [P, 2, 2])
        row_sum = sb("row_sum", [P, 2, 2])
        row_inv = sb("row_inv", [P, 2, 2])
        rt = sb("rt", [P, 8, NT, NE])
        rs = sb("rs", [P, 8, NT])

        ps_a = ps("ps_a", [P, 4, L])
        ps_b = ps("ps_b", [P, 2, L])
        ps_w = ps("ps_w", [P, 2, L])

        loaded = {k: sem("loaded_" + k) for k in ("const", "att", "mamba", "ffn", "ctx", "x")}
        w_loaded = [sem(f"w_loaded{k}") for k in range(2)]
        wb_loaded = [sem(f"wb_loaded{k}") for k in range(2)]
        wd_loaded = [sem(f"wd_loaded{k}") for k in range(2)]
        stored = sem("stored")
        consts_ready = sem("consts_ready")
        work_full = [sem("work_full0"), sem("work_full1")]
        work_free = [sem("work_free0"), sem("work_free1")]
        norm_chain = {k: sem("norm_chain_" + k) for k in ("att", "z", "ffn")}
        rstd_ready = {k: sem("rstd_ready_" + k) for k in ("att", "z", "ffn")}
        xn_ready = {k: sem("xn_ready_" + k) for k in ("att", "z", "ffn")}
        xt_ready = {k: sem("xt_ready_" + k) for k in ("att", "ffn")}
        q_raw_ready = sem("q_raw_ready")
        rope_chain = sem("rope_chain")
        qk_ready = sem("qk_ready")
        keys_zero = sem("keys_zero")
        v_full = sem("v_full")
        v_ready = sem("v_ready")
        scores_ready = sem("scores_ready")
        max_chain = sem("max_chain")
        bias_ready = sem("bias_ready")
        exp_done = sem("exp_done")
        inv_chain = sem("inv_chain")
        probs_ready = sem("probs_ready")
        pt_full = sem("pt_full")
        pt_ready = sem("pt_ready")
        pv_done = sem("pv_done")
        attn_ready = sem("attn_ready")
        x1_ready = sem("x1_ready")
        tanh_z = sem("tanh_z")
        z_chain = sem("z_chain")
        gated_ready = sem("gated_ready")
        x2_ready = sem("x2_ready")
        tap_ready = sem("tap_ready")
        conv_chain = sem("conv_chain")
        conv_tanh = sem("conv_tanh")
        u_ready = sem("u_ready")
        xdbl_full = sem("xdbl_full")
        xdt_ready = sem("xdt_ready")
        split_chain = sem("split_chain")
        bc_stack_ready = sem("bc_stack_ready")
        softplus_chain = sem("softplus_chain")
        softplus_in = sem("softplus_in")
        y_init = sem("y_init")
        poly_chain = sem("poly_chain")
        dt_ready = sem("dt_ready")
        bc_ready = sem("bc_ready")
        decay_ready = sem("decay_ready")
        scan_chain = sem("scan_chain")
        y_added = sem("y_added")
        router_full = sem("router_full")
        router_chain = sem("router_chain")
        router_shift = sem("router_shift")
        router_exp = sem("router_exp")
        expanded_ready = sem("expanded_ready")
        mask_ready = sem("mask_ready")
        low_ready = sem("low_ready")
        gu_ready = sem("gu_ready")
        tanh_ready = sem("tanh_ready")
        gate_chain = sem("gate_chain")
        h_ready = sem("h_ready")
        d_done = sem("d_done")
        down_chain = sem("down_chain")
        down_ready = sem("down_ready")
        wd_used = sem("wd_used")
        out_full = sem("out_full")
        x3_ready = sem("x3_ready")

        class Count:

            def __init__(self, semaphore, per, b):
                self.semaphore, self.per, self.b, self.n = semaphore, per, b, 0

            def inc(self, instruction):
                instruction.then_inc(self.semaphore, 1)
                self.n += 1

            def link(self, eng, instruction):
                self.inc(instruction)
                eng.wait_ge(self.semaphore, self.b * self.per + self.n)

            def end(self):
                assert self.n == self.per, (self.semaphore, self.n, self.per)

        def use(name, b, ffn=False):
            if ffn and isinstance(b, int) and b == BATCH - 1:
                k, before = USES_LAST[name], len(USES_FIRST) + (BATCH - 1) * len(USES_NEXT)
            elif not ffn and isinstance(b, int) and b == 0:
                k, before = USES_FIRST[name], 0
            else:
                i = b if ffn else b - 1
                k, before = USES_NEXT[name], None
                return k % 2, i * (len(USES_NEXT) // 2) + (len(USES_FIRST) // 2 + k // 2)
            return k % 2, (before + k) // 2

        def fill(eng, name, b, ffn=False):
            bank, count = use(name, b, ffn)
            if not (isinstance(count, int) and count == 0):
                eng.wait_ge(work_free[bank], count)
            return bank

        def filled(eng, name, b, ffn=False):
            bank, count = use(name, b, ffn)
            eng.wait_ge(work_full[bank], count + 1)
            return bank

        def first_batch(b):
            return isinstance(b, int) and b == 0

        block = stack.enter_context(nc.Block())

        @block.sync
        def _(sp):
            def load_ctx(b):
                if not first_batch(b):
                    sp.wait_ge(qk_ready, b * (MT + KV_HEADS))
                sp.dma_start(ctx_sb[:], ctx_t[b].rearrange("(t p) l -> p t l", p=P)).then_inc(loaded["ctx"], 16)

            def load_x(b):
                if not first_batch(b):
                    sp.wait_ge(x2_ready, b)
                sp.dma_start(xa[:], x[b].rearrange("(i p) d -> p i d", p=P)).then_inc(loaded["x"], 16)

            def load_w(t, f):
                if f >= 2:
                    sp.wait_ge(gu_ready, t * EVALS + EVAL_AT[f - 2, 0] + 1)
                else:
                    sp.wait_ge(scores_ready, t * STEPS + 1)
                sp.dma_start(w_sb[:, f % 2, :], w_tiles[f]).then_inc(w_loaded[f % 2], 16)

            def load_wb(t, f):
                if f >= 2:
                    sp.wait_ge(gu_ready, t * EVALS + EVAL_AT[f - 2, 2] + 1)
                sp.dma_start(wb_sb[:, f % 2, :], w_adapt[f]).then_inc(wb_loaded[f % 2], 16)

            def load_wd(t, f):
                if f >= 2:
                    sp.wait_ge(wd_used, t * FT + f - 1)
                else:
                    sp.wait_ge(scores_ready, t * STEPS + 1)
                sp.dma_start(wd_sb[:, f % 2, :], w_down[f]).then_inc(wd_loaded[f % 2], 16)

            def ffn_loads(t):
                for f in range(2, FT):
                    load_w(t, f)
                    load_wb(t, f)
                for f in range(FT):
                    load_wd(t, f)
                for i in range(NT):
                    sp.wait_ge(x3_ready, t * NT + i + 1)
                    sp.dma_start(out[t].rearrange("(i p) d -> p i d", p=P)[:, i, :], xb[:, i, :]).then_inc(stored, 16)

            load_ctx(0)
            load_x(0)
            sp.dma_start(wk_sb[:], wk).then_inc(loaded["att"], 16)
            sp.dma_start(wv_sb[:], wv).then_inc(loaded["att"], 16)
            sp.dma_start(wo_sb[:], wo).then_inc(loaded["att"], 16)
            sp.dma_start(lora_sb[:], w_lora).then_inc(loaded["ffn"], 16)
            sp.dma_start(wr_sb[:], w_r).then_inc(loaded["ffn"], 16)
            sp.dma_start(bd_sb[:], b_down).then_inc(loaded["ffn"], 16)
            sp.dma_start(ad_sb[:], a_down).then_inc(loaded["ffn"], 16)
            with sp.Fori(0, BATCH - 1) as t:
                load_ctx(t + 1)
                for f in range(2):
                    load_w(t, f)
                    load_wb(t, f)
                load_x(t + 1)
                ffn_loads(t)
            for f in range(2):
                load_w(BATCH - 1, f)
                load_wb(BATCH - 1, f)
            ffn_loads(BATCH - 1)
            sp.wait_ge(stored, 16 * NT * BATCH)

        @block.gpsimd
        def _(pool):
            def inverse_deviation(kind, b):
                pool.wait_ge(norm_chain[kind], b * 9 + 9)
                nc.gpsimd.tensor_tensor(rstd[:], var_eps[:], cst[:, C_HALF:C_HALF + NT], ALU.pow).then_inc(rstd_ready[kind], 1)

            def add_states(b, slot):
                for n in slot["add"]:
                    pool.wait_ge(scan_chain, b * 3 * NS + 3 * n + 3)
                    if n == 0:
                        pool.wait_ge(y_init, b * JT + JT)
                    else:
                        pool.wait_ge(y_added, b * NS + n)
                    nc.gpsimd.tensor_tensor(y_sb[:], y_sb[:], state[:, n % 2, :, :], ALU.add).then_inc(y_added, 1)

            def clear_keys(b):
                pool.wait_ge(loaded["const"], 32)
                if not first_batch(b):
                    pool.wait_ge(down_ready, b)
                nc.gpsimd.memset(keys, 0.0).then_inc(keys_zero, 1)

            def attention(b, slots):
                for s in range(STEPS):
                    add_states(b, slots[ATT + s])
                inverse_deviation("z", b)

            pool.wait_ge(loaded["const"], 32)
            inverse_deviation("att", 0)
            clear_keys(0)
            attention(0, PLAN_FIRST)
            with pool.Fori(0, BATCH - 1) as t:
                inverse_deviation("ffn", t)
                for e in range(EVALS):
                    add_states(t + 1, PLAN_NEXT[e])
                    if e == NORM_SLOT:
                        inverse_deviation("att", t + 1)
                clear_keys(t + 1)
                for f in range(FT):
                    add_states(t + 1, PLAN_NEXT[DOWN + f])
                attention(t + 1, PLAN_NEXT)
            inverse_deviation("ffn", BATCH - 1)

        @block.scalar
        def _(act):
            def to_sbuf(dst, src, name, b, ffn=False):
                bank = use(name, b, ffn)[0]
                return nc.scalar.activation(dst, src, ACT.Copy).then_inc(work_free[bank], 1)

            def conv_tap(b):
                for j in range(JT):
                    bank = filled(act, ("xin", j), b)
                    nc.scalar.activation(conv_sb[:, j, :], ps_w[:, bank, :], ACT.Identity,
                                         bias=conv_half[:, 16 + j:17 + j],
                                         scale=conv_half[:, TAPS * j + 3:TAPS * j + 4]).then_inc(tap_ready, 1)

            def conv_gate(b):
                for j in range(JT):
                    act.wait_ge(conv_chain, b * 3 * JT + 3 * j + 3)
                    nc.scalar.activation(exp_v[:, j, :], conv_sb[:, j, :], ACT.Tanh).then_inc(conv_tanh, 1)

            def split_first(b):
                act.wait_ge(xdbl_full, b + 1)
                nc.scalar.activation(xdt_sb[:], ps_b[:, 1, :], ACT.Copy).then_inc(xdt_ready, 1)
                act.wait_ge(u_ready, b * JT + JT)
                for j in range(JT):
                    nc.scalar.activation(y_sb[:, j, :], u_sb[:, j, :], ACT.Identity,
                                         scale=vec[:, V_D + j:V_D + j + 1]).then_inc(y_init, 1)

            def softplus_parts(b):
                chain = Count(softplus_chain, 2 * JT, b)
                for j in range(JT):
                    bank = filled(act, ("dt", j), b)
                    bias = vec[:, V_DTB + j:V_DTB + j + 1]
                    chain.link(act, nc.scalar.activation(exp_v[:, j, :], ps_w[:, bank, :], ACT.Abs, bias=bias))
                    chain.inc(nc.scalar.activation(exp_v[:, j, :], exp_v[:, j, :], ACT.Exp, scale=-1.0))
                    nc.scalar.activation(relu_v[:, j, :], ps_w[:, bank, :], ACT.Relu, bias=bias)\
                        .then_inc(work_free[bank], 1)
                act.wait_ge(softplus_chain, (b + 1) * 2 * JT)
                nc.scalar.activation(scrap_a[:], vec[0:1, 0:1], ACT.Copy).then_inc(softplus_in, 1)
                chain.end()

            def scan_inputs(b, slot):
                for n in slot["bc"]:
                    for c in range(2):
                        if n >= 2:
                            act.wait_ge(scan_chain, b * 3 * NS + 3 * (n - 2) + (1 if c == 0 else 3))
                        elif not first_batch(b):
                            act.wait_ge(scan_chain, b * 3 * NS)
                        bank = filled(act, ("bc", 2 * n + c), b)
                        nc.scalar.activation(bc_sb[:, n % 2, c, :], ps_w[:, bank, :], ACT.Copy)\
                            .then_inc(work_free[bank], 1)
                for n in slot["decay"]:
                    if n == 0:
                        act.wait_ge(dt_ready, b + 1)
                    if n >= 2:
                        act.wait_ge(scan_chain, b * 3 * NS + 3 * (n - 2) + 2)
                    for j in range(JT):
                        nc.scalar.activation(decay[:, n % 2, j, 1:L], dt_sb[:, j, 1:L], ACT.Exp,
                                             scale=decay_rate[:, j, n:n + 1]).then_inc(decay_ready, 1)

            def transposed(kind, name, b, ffn):
                for k in range(KT):
                    bank = filled(act, (name, k), b, ffn)
                    nc.scalar.activation(xt[:, k, :], ps_w[:, bank, :], ACT.Copy).then_inc(work_free[bank], 1)

            def project(b, f):
                if f == 0:
                    transposed("att", "xt", b, False)
                n = projections(f)[0]
                if n is not None:
                    bank = filled(act, ("raw", n), b)
                    if n >= 2:
                        act.wait_ge(qk_ready, b * (MT + KV_HEADS) + n - 1)
                    elif not first_batch(b):
                        act.wait_ge(down_ready, b)
                    nc.scalar.activation(q_raw[:, n % 2, :], ps_w[:, bank, :], ACT.Identity,
                                         bias=vec[:, V_BQ + n:V_BQ + n + 1]).then_inc(work_free[bank], 1)

            def attention(b, slots):
                def exponents(s):
                    i = (s // 2) % NT
                    act.wait_ge(bias_ready, b * STEPS + s + 1)
                    for k in range(2):
                        if s >= 2:
                            act.wait_ge(pt_full, b * 2 * STEPS + 2 * (s - 2) + k + 1)
                        nc.scalar.activation(probs[:, (2 * s + k) % 4, 0:(i + 1) * P],
                                             ps_a[:, 2 * (s % 2) + k, 0:(i + 1) * P], ACT.Exp,
                                             bias=bias_max[:, s % 2, k:k + 1], scale=SCALE,
                                             accum_out=row_sum[:, s % 2, k:k + 1]).then_inc(exp_done, 1)

                def move_transposed(s):
                    i = (s // 2) % NT
                    for k in range(2):
                        act.wait_ge(pt_full, b * 2 * STEPS + 2 * s + k + 1)
                        if s >= 2:
                            act.wait_ge(pv_done, b * (STEPS // 2) + s // 2)
                        nc.scalar.activation(probs_t[:, (2 * s + k) % 4, 0:(i + 1) * P],
                                             ps_b[:, k, 0:(i + 1) * P], ACT.Copy).then_inc(pt_ready, 1)

                def move_output(g):
                    m, i = g // NT, g % NT
                    bank = filled(act, ("pv", g), b)
                    nc.scalar.activation(attn_t[:, m, i * P:(i + 1) * P], ps_w[:, bank, 0:P], ACT.Copy)\
                        .then_inc(work_free[bank], 1)

                for s in range(STEPS + 4):
                    if s < STEPS:
                        exponents(s)
                    if s >= 4 and s % 2 == 0:
                        move_output((s - 4) // 2)
                    if 2 <= s < STEPS + 2:
                        move_transposed(s - 2)
                    if s < STEPS:
                        scan_inputs(b, slots[ATT + s])
                for i in range(NT):
                    act.wait_ge(xn_ready["z"], b * NT + i + 1)
                    nc.scalar.activation(silu_z[:, i, :], hz[:, i, :], ACT.Tanh, scale=0.5).then_inc(tanh_z, 1)

            def ffn_head(t):
                transposed("ffn", "xt2", t, True)

            def ffn_masks(t):
                act.wait_ge(router_shift, t + 1)
                nc.scalar.activation(rt[:, 1, :, :], rt[:, 0, :, :], ACT.Exp).then_inc(router_exp, 1)
                for k in range(4):
                    bank = filled(act, ("mask", k), t, True)
                    nc.scalar.activation(mask_t[:, k, :], ps_w[:, bank, :], ACT.Copy).then_inc(work_free[bank], 1)

            def evaluate(t, e):
                f, k = EVAL[e]
                act.wait_ge(gu_ready, t * EVALS + e + 1)
                if e >= 2:
                    act.wait_ge(h_ready, t * EVALS + e - 1)
                nc.scalar.activation(gate[:, e % 2, :], ps_a[:, 2 * (f % 2), :], ACT.Tanh, scale=0.5)\
                    .then_inc(tanh_ready, 1)

            act.dma_start(vec[:], vectors).then_inc(loaded["const"], 16)
            act.dma_start(cst[:], constants).then_inc(loaded["const"], 16)
            act.dma_start(win_sb[:], w_in).then_inc(loaded["mamba"], 16)
            act.dma_start(wx_sb[:], w_x).then_inc(loaded["mamba"], 16)
            act.dma_start(wdt_sb[:], w_dt).then_inc(loaded["mamba"], 16)
            act.dma_start(wq_sb[:], wq).then_inc(loaded["att"], 16)
            act.wait_ge(loaded["const"], 32)
            nc.scalar.activation(ident_b[:], ident, ACT.Copy).then_inc(consts_ready, 1)
            nc.scalar.activation(mask_b[:], cst[:, C_MASK:C_MASK + P], ACT.Copy).then_inc(consts_ready, 1)
            nc.scalar.activation(sel_b[:], cst[:, C_SEL:C_SEL + 2 * NS], ACT.Copy).then_inc(consts_ready, 1)
            nc.scalar.activation(decay_rate[:], vec[:, V_AL:V_AL + JT * NS].rearrange("p (j n) -> p j n", n=NS),
                                 ACT.Exp).then_inc(consts_ready, 1)
            act.wait_ge(consts_ready, 7)

            conv_tap(0)
            conv_gate(0)
            split_first(0)
            softplus_parts(0)
            for f in range(FT):
                project(0, f)
            attention(0, PLAN_FIRST)
            with act.Fori(0, BATCH - 1) as t:
                conv_tap(t + 1)
                ffn_head(t)
                conv_gate(t + 1)
                ffn_masks(t)
                split_first(t + 1)
                softplus_parts(t + 1)
                for e in range(EVALS):
                    evaluate(t, e)
                    scan_inputs(t + 1, PLAN_NEXT[e])
                for f in range(FT):
                    project(t + 1, f)
                    scan_inputs(t + 1, PLAN_NEXT[DOWN + f])
                attention(t + 1, PLAN_NEXT)
            ffn_head(BATCH - 1)
            ffn_masks(BATCH - 1)
            for e in range(EVALS):
                evaluate(BATCH - 1, e)

        @block.tensor
        def _(pe):
            def project_in(b):
                pe.wait_ge(loaded["ctx"], 16 * b + 16)
                for j in range(JT):
                    bank = fill(pe, ("xin", j), b)
                    for k in range(CT):
                        mm = nc.tensor.matmul(ps_w[:, bank, :], win_sb[:, k, j * P:(j + 1) * P], ctx_sb[:, k, :],
                                              start=(k == 0), stop=(k == CT - 1))
                    mm.then_inc(work_full[bank], 1)

            def project_x(b):
                for j in range(JT):
                    pe.wait_ge(u_ready, b * JT + j + 1)
                    mm = nc.tensor.matmul(ps_b[:, 1, :], wx_sb[:, j, :], u_sb[:, j, :],
                                          start=(j == 0), stop=(j == JT - 1))
                mm.then_inc(xdbl_full, 1)

            def project_dt(b):
                pe.wait_ge(xdt_ready, b + 1)
                for j in range(JT):
                    bank = fill(pe, ("dt", j), b)
                    nc.tensor.matmul(ps_w[:, bank, :], wdt_sb[:, j * P:(j + 1) * P], xdt_sb[:],
                                     start=True, stop=True).then_inc(work_full[bank], 1)

            def broadcast_bc(b, slot):
                for n in slot["bc"]:
                    if n == 0:
                        pe.wait_ge(bc_stack_ready, b + 1)
                    for c in range(2):
                        bank = fill(pe, ("bc", 2 * n + c), b)
                        pick = sel_b[:, NS * c + n:NS * c + n + 1].to_broadcast([P, P])
                        nc.tensor.matmul(ps_w[:, bank, :], pick, bc_stack[:], start=True, stop=True)\
                            .then_inc(work_full[bank], 1)

            def transpose_normed(kind, name, b, ffn):
                src = xn if ffn else xn_att
                pe.wait_ge(xn_ready[kind], b * NT + NT)
                for k in range(KT):
                    bank = fill(pe, (name, k), b, ffn)
                    for i in range(NT):
                        mm = nc.tensor.transpose(ps_w[:, bank, i * P:(i + 1) * P], src[:, i, k * P:(k + 1) * P], ident)
                    mm.then_inc(work_full[bank], 1)

            def xt_moved(name, b, ffn):
                for k in (KT - 2, KT - 1):
                    bank, count = use((name, k), b, ffn)
                    pe.wait_ge(work_free[bank], count + 1)

            def project(b, f):
                if f == 0:
                    transpose_normed("att", "xt", b, False)
                raw, back, values = projections(f)
                if raw is not None:
                    if raw == 0:
                        xt_moved("xt", b, False)
                    bank = fill(pe, ("raw", raw), b)
                    for k in range(KT):
                        w = wq_sb[:, k, raw * P:(raw + 1) * P] if raw < MT else wk_sb[:, raw - MT, k, :]
                        mm = nc.tensor.matmul(ps_w[:, bank, :], w, xt[:, k, :], start=(k == 0), stop=(k == KT - 1))
                    mm.then_inc(work_full[bank], 1)
                if back is not None:
                    bank = fill(pe, ("back", back), b)
                    raw_bank, raw_count = use(("raw", back), b)
                    pe.wait_ge(work_free[raw_bank], raw_count + 1)
                    nc.tensor.matmul(ps_w[:, bank, :], rot, q_raw[:, back % 2, :], start=True, stop=True)\
                        .then_inc(work_full[bank], 1)
                if values:
                    if not first_batch(b):
                        pe.wait_ge(down_ready, b)
                    for i in range(NT):
                        for k in range(KT):
                            mm = nc.tensor.matmul(ps_b[:, 0, i * 64:(i + 1) * 64], xt[:, k, i * P:(i + 1) * P],
                                                  wv_sb[:, k, :], start=(k == 0), stop=(k == KT - 1))
                    mm.then_inc(v_full, 1)

            def attention(b, slots):
                pe.wait_ge(qk_ready, (b + 1) * (MT + KV_HEADS))
                pe.wait_ge(v_ready, b + 1)
                if not first_batch(b):
                    pe.wait_ge(x3_ready, b * NT)

                def scores(s):
                    m, i, pair = s // (2 * NT), (s // 2) % NT, s % 2
                    if s >= 2:
                        pe.wait_ge(exp_done, b * 2 * STEPS + 2 * (s - 2) + 2)
                    for k in range(2):
                        bank, head = 2 * (s % 2) + k, 2 * pair + k
                        nc.tensor.matmul(ps_a[:, bank, 0:(i + 1) * P], q_t[:, m, i * P:(i + 1) * P],
                                         keys[:, (m * KV_HEADS // MT) * HPT + head, 0:(i + 1) * P],
                                         start=True, stop=False)
                        mm = nc.tensor.matmul(ps_a[:, bank, i * P:(i + 1) * P], ident_b[:], mask_b[:],
                                              start=False, stop=True)
                    mm.then_inc(scores_ready, 1)

                def transpose_probs(s):
                    i = (s // 2) % NT
                    pe.wait_ge(probs_ready, b * STEPS + s + 1)
                    for k in range(2):
                        if s >= 1:
                            pe.wait_ge(pt_ready, b * 2 * STEPS + 2 * (s - 1) + k + 1)
                        for kt in range(i + 1):
                            mm = nc.tensor.transpose(ps_b[:, k, kt * P:(kt + 1) * P],
                                                     probs[:, (2 * s + k) % 4, kt * P:(kt + 1) * P], ident)
                        mm.then_inc(pt_full, 1)

                def weigh_values(g):
                    m, i = g // NT, g % NT
                    bank = fill(pe, ("pv", g), b)
                    pe.wait_ge(pt_ready, b * 2 * STEPS + 4 * g + 4)
                    kv = m * KV_HEADS // MT
                    for kt in range(i + 1):
                        for j in range(HPT):
                            mm = nc.tensor.matmul(ps_w[j * HD:(j + 1) * HD, bank, 0:P],
                                                  v_sb[:, kt, kv * HD:(kv + 1) * HD],
                                                  probs_t[:, j, kt * P:(kt + 1) * P],
                                                  start=(kt == 0), stop=(kt == i), tile_position=(0, j * HD))
                    mm.then_inc(work_full[bank], 1)
                    nc.tensor.nop().then_inc(pv_done, 1)

                for s in range(STEPS + 4):
                    if s < STEPS:
                        scores(s)
                    if s >= 4 and s % 2 == 0:
                        weigh_values((s - 4) // 2)
                    if 2 <= s < STEPS + 2:
                        transpose_probs(s - 2)
                    if s < STEPS:
                        broadcast_bc(b, slots[ATT + s])
                for g in (MT * NT - 2, MT * NT - 1):
                    bank, count = use(("pv", g), b)
                    pe.wait_ge(work_free[bank], count + 1)
                for i in range(NT):
                    bank = fill(pe, ("op", i), b)
                    for m in range(MT):
                        mm = nc.tensor.matmul(ps_w[:, bank, :], attn_t[:, m, i * P:(i + 1) * P], wo_sb[:, m, :],
                                              start=(m == 0), stop=(m == MT - 1))
                    mm.then_inc(work_full[bank], 1)
                pe.wait_ge(gated_ready, b * JT + JT)
                for i in range(NT):
                    bank = fill(pe, ("yt", i), b)
                    for j in range(JT):
                        mm = nc.tensor.transpose(ps_w[:, bank, j * P:(j + 1) * P], silu_z[:, j, i * P:(i + 1) * P], ident)
                    mm.then_inc(work_full[bank], 1)

            def base(t, f):
                slot = f % 2
                of_slot = (FT - slot + 1) // 2
                pe.wait_ge(w_loaded[slot], 16 * (t * of_slot + f // 2 + 1))
                if f >= 2:
                    pe.wait_ge(h_ready, t * EVALS + EVAL_AT[f - 2, 2] + 1)
                for half, at in ((0, WG), (1, WU)):
                    for k in range(KT):
                        mm = nc.tensor.matmul(ps_a[:, 2 * (f % 2) + half, :],
                                              w_sb[:, slot, at + k * P:at + (k + 1) * P], xt[:, k, :],
                                              start=(k == 0), stop=False, skip_group_check=True)
                mm.then_inc(gu_ready, 1)

            def add_slot(t, f, k):
                if k == 1:
                    of_slot = (FT - f % 2 + 1) // 2
                    pe.wait_ge(wb_loaded[f % 2], 16 * (t * of_slot + f // 2 + 1))
                pe.wait_ge(h_ready, t * EVALS + EVAL_AT[f, k - 1] + 1)
                for half, at in ((0, BG), (1, BU)):
                    mm = nc.tensor.matmul(ps_a[:, 2 * (f % 2) + half, :], wb_sb[:, f % 2, at:at + P],
                                          low[:, 2 * half + k - 1, :], start=False, stop=(k == 2),
                                          skip_group_check=True)
                mm.then_inc(gu_ready, 1)

            def down_adapters(t, f):
                pe.wait_ge(h_ready, t * EVALS + EVAL_AT[f, 2] + 1)
                for k in (1, 2):
                    mm = nc.tensor.matmul(ps_b[:, k - 1, :], ad_sb[:, f, :], hk[:, (2 * f + k - 1) % 4, :],
                                          start=(f == 0), stop=(f == FT - 1), skip_group_check=True)
                mm.then_inc(d_done, 1)

            def ffn_head(t):
                transpose_normed("ffn", "xt2", t, True)
                xt_moved("xt2", t, True)
                for i in range(NT):
                    for k in range(KT):
                        mm = nc.tensor.matmul(ps_b[:, 0, i * NE:(i + 1) * NE], xt[:, k, i * P:(i + 1) * P],
                                              wr_sb[:, k, :], start=(k == 0), stop=(k == KT - 1))
                mm.then_inc(router_full, 1)
                base(t, 0)

            def ffn_masks(t):
                pe.wait_ge(expanded_ready, 4 * t + 4)
                for k in range(4):
                    bank = fill(pe, ("mask", k), t, True)
                    for i in range(NT):
                        mm = nc.tensor.transpose(ps_w[:, bank, i * P:(i + 1) * P], expanded[:, k, i * P:(i + 1) * P],
                                                 ident)
                    mm.then_inc(work_full[bank], 1)
                for half, name in ((0, "lowg"), (1, "lowu")):
                    bank = fill(pe, (name, 0), t, True)
                    for k in range(KT):
                        mm = nc.tensor.matmul(ps_w[:, bank, :], lora_sb[:, half, k, :], xt[:, k, :],
                                              start=(k == 0), stop=(k == KT - 1))
                    mm.then_inc(work_full[bank], 1)

            def ffn_tiles(t, b, slots):
                pe.wait_ge(low_ready, 4 * t + 4)
                if b is not None:
                    pe.wait_ge(xdt_ready, b + 1)
                def beside(e):
                    if b is not None:
                        broadcast_bc(b, slots[e])

                beside(0)
                for f in range(FT):
                    add_slot(t, f, 1)
                    beside(EVAL_AT[f, 1])
                    if f + 1 < FT:
                        base(t, f + 1)
                        beside(EVAL_AT[f + 1, 0])
                    add_slot(t, f, 2)
                    beside(EVAL_AT[f, 2])
                    if f > 0:
                        down_adapters(t, f - 1)
                down_adapters(t, FT - 1)
                for f in range(FT):
                    of_slot = (FT - f % 2 + 1) // 2
                    pe.wait_ge(wd_loaded[f % 2], 16 * (t * of_slot + f // 2 + 1))
                    for i in range(NT):
                        mm = nc.tensor.matmul(ps_a[:, i, :], hb[:, f, i * P:(i + 1) * P], wd_sb[:, f % 2, :],
                                              start=(f == 0), stop=False, skip_group_check=True)
                    mm.then_inc(wd_used, 1)
                    if b is not None:
                        project(b, f)
                        broadcast_bc(b, slots[DOWN + f])
                pe.wait_ge(down_ready, t + 1)
                for i in range(NT):
                    nc.tensor.matmul(ps_a[:, i, :], down_low[:, i * P:(i + 1) * P], bd_sb[:],
                                     start=False, stop=True, skip_group_check=True).then_inc(out_full, 1)

            pe.wait_ge(consts_ready, 7)
            pe.wait_ge(loaded["mamba"], 48)
            project_in(0)
            project_x(0)
            project_dt(0)
            pe.wait_ge(loaded["att"], 64)
            for f in range(FT):
                project(0, f)
            attention(0, PLAN_FIRST)
            pe.wait_ge(loaded["ffn"], 64)
            with pe.Fori(0, BATCH - 1) as t:
                project_in(t + 1)
                ffn_head(t)
                project_x(t + 1)
                ffn_masks(t)
                project_dt(t + 1)
                ffn_tiles(t, t + 1, PLAN_NEXT)
                attention(t + 1, PLAN_NEXT)
            ffn_head(BATCH - 1)
            ffn_masks(BATCH - 1)
            ffn_tiles(BATCH - 1, None, None)

        @block.vector
        def _(dve):
            tt, ts, stt = nc.vector.tensor_tensor, nc.vector.tensor_scalar, nc.vector.scalar_tensor_tensor

            def normalize(kind, b, src, dst):
                chain = Count(norm_chain[kind], 9, b)
                for i in range(NT):
                    chain.inc(nc.vector.bn_stats(stats[:, i, :], src[:, i, :]))
                dve.wait_ge(norm_chain[kind], b * 9 + 4)
                nc.vector.tensor_copy(scrap[:], vec[0:1, 0:1])
                for i in range(NT):
                    chain.inc(nc.vector.bn_aggr(mv[:, i, :], stats[:, i, :]))
                dve.wait_ge(norm_chain[kind], b * 9 + 8)
                chain.inc(ts(var_eps[:], mv[:, :, 1], EPS, None, ALU.add))
                chain.end()
                dve.wait_ge(rstd_ready[kind], b + 1)
                for i in range(NT):
                    ts(dst[:, i, :], src[:, i, :], mv[:, i, 0:1], rstd[:, i:i + 1], ALU.subtract, ALU.mult)\
                        .then_inc(xn_ready[kind], 1)

            def convolve(b):
                chain = Count(conv_chain, 3 * JT, b)
                for j in range(JT):
                    bank = use(("xin", j), b)[0]
                    dve.wait_ge(tap_ready, b * JT + j + 1)
                    for back in range(1, TAPS):
                        tap = conv_half[:, TAPS * j + TAPS - 1 - back:TAPS * j + TAPS - back]
                        op = stt(conv_sb[:, j, back:L], ps_w[:, bank, 0:L - back], tap, conv_sb[:, j, back:L],
                                 ALU.mult, ALU.add)
                        chain.link(dve, op)
                    nc.vector.tensor_copy(scrap[:], ps_w[0:1, bank, 0:1]).then_inc(work_free[bank], 1)
                chain.end()
                for j in range(JT):
                    dve.wait_ge(conv_tanh, b * JT + j + 1)
                    stt(u_sb[:, j, :], exp_v[:, j, :], 1.0, conv_sb[:, j, :], ALU.add, ALU.mult).then_inc(u_ready, 1)

            def split_bc(b):
                chain = Count(split_chain, 3, b)
                dve.wait_ge(xdt_ready, b + 1)
                nc.vector.tensor_copy(bc_stack[32:64, :], xdt_sb[32:64, :])
                chain.link(dve, nc.vector.tensor_copy(split_b[64:128, :], xdt_sb[64:128, :]))
                chain.link(dve, tt(split_f[64:128, :], xdt_sb[64:128, :], split_b[64:128, :], ALU.subtract))
                nc.vector.tensor_copy(bc_stack[64:96, :], split_f[64:96, :])
                chain.link(dve, nc.vector.tensor_copy(split_b[96:128, :], split_f[96:128, :]))
                tt(bc_stack[96:128, :], split_f[96:128, :], split_b[96:128, :], ALU.subtract).then_inc(bc_stack_ready, 1)
                chain.end()

            def scan_piece(b, piece):
                kind, n = piece
                if kind == "poly":
                    if n == 0:
                        dve.wait_ge(softplus_in, b + 1)
                        ts(du_sb[:], exp_v, POLY[-1], None, ALU.mult).then_inc(poly_chain, 1)
                    elif n < NPOLY:
                        dve.wait_ge(poly_chain, b * (NPOLY + 2) + n)
                        stt(du_sb[:].rearrange("p j l -> p (j l)"), du_sb[:].rearrange("p j l -> p (j l)"),
                            POLY[NPOLY - 1 - n], exp_v.rearrange("p j l -> p (j l)"), ALU.add, ALU.mult)\
                            .then_inc(poly_chain, 1)
                    elif n == NPOLY:
                        dve.wait_ge(poly_chain, b * (NPOLY + 2) + n)
                        tt(dt_sb[:], du_sb[:], relu_v, ALU.add).then_inc(poly_chain, 1)
                    else:
                        dve.wait_ge(poly_chain, b * (NPOLY + 2) + n)
                        tt(du_sb[:], dt_sb[:], u_sb, ALU.mult).then_inc(poly_chain, 1)
                        nc.vector.memset(decay[:, :, :, 0:1], 0.0).then_inc(dt_ready, 1)
                    return
                base = b * 3 * NS + 3 * n
                flat = state[:, n % 2, :, :].rearrange("p j l -> p (j l)")
                if kind == "mul":
                    if n == 0:
                        dve.wait_ge(poly_chain, (b + 1) * (NPOLY + 2))
                        dve.wait_ge(y_init, b * JT + JT)
                    elif n >= 2:
                        dve.wait_ge(y_added, b * NS + n - 1)
                    bank, count = use(("bc", 2 * n), b)
                    dve.wait_ge(work_free[bank], count + 1)
                    row = bc_sb[:, n % 2, 0, :].unsqueeze(1).to_broadcast([P, JT, L])
                    tt(state[:, n % 2, :, :], du_sb[:], row, ALU.mult).then_inc(scan_chain, 1)
                elif kind == "run":
                    dve.wait_ge(decay_ready, b * JT * NS + JT * n + JT)
                    dve.wait_ge(dt_ready, b + 1)
                    dve.wait_ge(scan_chain, base + 1)
                    nc.vector.tensor_tensor_scan(flat, decay[:, n % 2, :, :].rearrange("p j l -> p (j l)"), flat, 0.0,
                                                 ALU.mult, ALU.add).then_inc(scan_chain, 1)
                else:
                    bank, count = use(("bc", 2 * n + 1), b)
                    dve.wait_ge(work_free[bank], count + 1)
                    dve.wait_ge(scan_chain, base + 2)
                    row = bc_sb[:, n % 2, 1, :].unsqueeze(1).to_broadcast([P, JT, L])
                    tt(state[:, n % 2, :, :], state[:, n % 2, :, :], row, ALU.mult).then_inc(scan_chain, 1)

            def rotate(b, f):
                total = MT + KV_HEADS
                _, n, values = projections(f)
                if n is not None:
                    raw_bank, raw_count = use(("raw", n), b)
                    dve.wait_ge(work_free[raw_bank], raw_count + 1)
                    tt(rope_tmp, q_raw[:, n % 2, :], cos_t, ALU.mult).then_inc(rope_chain, 1)
                    bank = filled(dve, ("back", n), b)
                    part = q_t[:, n, :] if n < MT else split_f[:]
                    tt(part, ps_w[:, bank, :], sin_t, ALU.mult).then_inc(work_free[bank], 1)
                    dve.wait_ge(rope_chain, b * total + n + 1)
                    bank, count = use(("back", n), b)
                    dve.wait_ge(work_free[bank], count + 1)
                    if n < MT:
                        tt(part, part, rope_tmp, ALU.add).then_inc(qk_ready, 1)
                    else:
                        if n == MT:
                            dve.wait_ge(keys_zero, b + 1)
                        for j in range(HPT):
                            rows = slice(j * HD, (j + 1) * HD)
                            op = tt(keys[rows, (n - MT) * HPT + j, :], split_f[rows, :], rope_tmp[rows, :], ALU.add)
                        op.then_inc(qk_ready, 1)
                    dve.wait_ge(qk_ready, b * total + n + 1)
                if values:
                    dve.wait_ge(v_full, b + 1)
                    tt(v_sb[:], ps_b[:, 0, 0:NT * 64].rearrange("p (i d) -> p i d", i=NT),
                       vec[:, V_BV:V_BV + 64].unsqueeze(1).to_broadcast([P, NT, 64]), ALU.add).then_inc(v_ready, 1)

            def attention(b, slots):
                def maxima(s):
                    i = (s // 2) % NT
                    dve.wait_ge(scores_ready, b * STEPS + s + 1)
                    nc.vector.tensor_reduce(neg_max[:, s % 2, :], ps_a[:, 2 * (s % 2):2 * (s % 2) + 2, 0:(i + 1) * P],
                                            AX.X, ALU.max).then_inc(max_chain, 1)
                    dve.wait_ge(max_chain, b * STEPS + s + 1)
                    ts(bias_max[:, s % 2, :], neg_max[:, s % 2, :], -SCALE, None, ALU.mult).then_inc(bias_ready, 1)

                def divide(s):
                    i = (s // 2) % NT
                    dve.wait_ge(exp_done, b * 2 * STEPS + 2 * s + 2)
                    nc.vector.reciprocal(row_inv[:, s % 2, :], row_sum[:, s % 2, :]).then_inc(inv_chain, 1)
                    dve.wait_ge(inv_chain, b * STEPS + s + 1)
                    for k in range(2):
                        place = probs[:, (2 * s + k) % 4, 0:(i + 1) * P]
                        op = ts(place, place, row_inv[:, s % 2, k:k + 1], None, ALU.mult)
                    op.then_inc(probs_ready, 1)

                for s in range(STEPS + 1):
                    if s < STEPS:
                        maxima(s)
                    if s >= 1:
                        divide(s - 1)
                    if s < STEPS:
                        for piece in slots[ATT + s]["dve"]:
                            scan_piece(b, piece)
                for i in range(NT):
                    bank = filled(dve, ("op", i), b)
                    tt(xa[:, i, :], ps_w[:, bank, :], xa[:, i, :], ALU.add).then_inc(work_free[bank], 1)
                for k in (NT - 2, NT - 1):
                    bank, count = use(("op", k), b)
                    dve.wait_ge(work_free[bank], count + 1)
                normalize("z", b, xa, hz)
                chain = Count(z_chain, NT, b)
                for i in range(NT):
                    dve.wait_ge(tanh_z, b * NT + i + 1)
                    chain.inc(stt(silu_z[:, i, :], silu_z[:, i, :], 1.0, hz[:, i, :], ALU.add, ALU.mult))
                chain.end()
                dve.wait_ge(y_added, b * NS + NS)
                dve.wait_ge(z_chain, b * NT + NT)
                for i in range(NT):
                    stt(silu_z[:, i, :], y_sb[:, i, :], 0.5, silu_z[:, i, :], ALU.mult, ALU.mult)\
                        .then_inc(gated_ready, 1)
                if not first_batch(b):
                    dve.wait_ge(stored, b * 16 * NT)
                for i in range(NT):
                    bank = filled(dve, ("yt", i), b)
                    tt(xb[:, i, :], ps_w[:, bank, :], xa[:, i, :], ALU.add).then_inc(work_free[bank], 1)
                for k in (NT - 2, NT - 1):
                    bank, count = use(("yt", k), b)
                    dve.wait_ge(work_free[bank], count + 1)
                nc.vector.tensor_copy(scrap[:], vec[0:1, 0:1]).then_inc(x2_ready, 1)

            def route(t):
                logits, prob, onehot, second = rt[:, 0], rt[:, 1], rt[:, 2], rt[:, 3]
                rank, tmp = rt[:, 4], rt[:, 5]
                cand = cst[:, C_CAND:C_CAND + NE].unsqueeze(1).to_broadcast([P, NT, NE])

                def spread(v):
                    return v.unsqueeze(2).to_broadcast([P, NT, NE])

                chain = Count(router_chain, 18, t)

                def then(op):
                    chain.link(dve, op)

                raw = ps_b[:, 0, 0:NT * NE].rearrange("p (i e) -> p i e", i=NT)
                dve.wait_ge(router_full, t + 1)
                then(nc.vector.tensor_reduce(rs[:, 0, :], raw, AX.X, ALU.max))
                tt(logits, raw, spread(rs[:, 0, :]), ALU.subtract).then_inc(router_shift, 1)
                dve.wait_ge(router_exp, t + 1)
                then(nc.vector.tensor_reduce(rs[:, 1, :], prob, AX.X, ALU.add))
                then(nc.vector.reciprocal(rs[:, 2, :], rs[:, 1, :]))
                then(tt(prob, prob, spread(rs[:, 2, :]), ALU.mult))

                def pick(source, weight, winner):
                    then(nc.vector.tensor_reduce(weight, source, AX.X, ALU.max))
                    then(tt(rank, source, spread(weight), ALU.is_equal))
                    then(tt(rank, rank, cand, ALU.mult))
                    then(nc.vector.tensor_reduce(rs[:, 5, :], rank, AX.X, ALU.max))
                    then(tt(winner, rank, spread(rs[:, 5, :]), ALU.is_equal))

                pick(prob, rs[:, 3, :], onehot)
                then(stt(tmp, onehot, -2.0, prob, ALU.mult, ALU.add))
                pick(tmp, rs[:, 4, :], second)

                then(tt(rt[:, 6], second, onehot, ALU.subtract))
                then(tt(rt[:, 7], onehot, spread(rs[:, 3, :]), ALU.mult))
                then(tt(rt[:, 5], second, spread(rs[:, 4, :]), ALU.mult))
                for k, table in enumerate((onehot, rt[:, 6], rt[:, 7], rt[:, 5])):
                    wide = expanded[:, k, :].rearrange("p (ie r) -> p ie r", r=LR)
                    narrow = table.rearrange("p i e -> p (i e)").unsqueeze(2).to_broadcast([P, NT * NE, LR])
                    ts(wide, narrow, 2.0, None, ALU.mult).then_inc(expanded_ready, 1)
                chain.end()

            def mask_low(t):
                for k in (2, 3):
                    bank, count = use(("mask", k), t, True)
                    dve.wait_ge(work_free[bank], count + 1)
                for half, name in ((0, "lowg"), (1, "lowu")):
                    bank = filled(dve, (name, 0), t, True)
                    tt(low[:, 2 * half, :], ps_w[:, bank, :], mask_t[:, 0, :], ALU.mult).then_inc(low_ready, 1)
                    tt(low[:, 2 * half + 1, :], ps_w[:, bank, :], mask_t[:, 1, :], ALU.mult).then_inc(low_ready, 1)
                    dve.wait_ge(low_ready, 4 * t + 2 * half + 2)
                    nc.vector.tensor_copy(scrap[:], ps_w[0:1, bank, 0:1]).then_inc(work_free[bank], 1)

            def evaluate(t, e):
                f, k = EVAL[e]
                bank = 2 * (f % 2)
                dve.wait_ge(tanh_ready, t * EVALS + e + 1)
                stt(gate[:, e % 2, :], gate[:, e % 2, :], 1.0, ps_a[:, bank, :], ALU.add, ALU.mult)\
                    .then_inc(gate_chain, 1)
                if k > 0 and f >= 2:
                    dve.wait_ge(d_done, t * FT + f - 1)
                dst = hb[:, f, :] if k == 0 else hk[:, (2 * f + k - 1) % 4, :]
                dve.wait_ge(gate_chain, t * EVALS + e + 1)
                tt(dst, gate[:, e % 2, :], ps_a[:, bank + 1, :], ALU.mult).then_inc(h_ready, 1)

            def weigh_down(t):
                dve.wait_ge(d_done, t * FT + FT)
                chain = Count(down_chain, 2, t)
                chain.inc(tt(mask_t[:, 2, :], ps_b[:, 0, :], mask_t[:, 2, :], ALU.mult))
                chain.link(dve, tt(mask_t[:, 3, :], ps_b[:, 1, :], mask_t[:, 3, :], ALU.mult))
                tt(down_low, mask_t[:, 2, :], mask_t[:, 3, :], ALU.add).then_inc(down_ready, 1)
                chain.end()

            def finish(t):
                for i in range(NT):
                    dve.wait_ge(out_full, t * NT + i + 1)
                    stt(xb[:, i, :], ps_a[:, i, :], 0.5, xb[:, i, :], ALU.mult, ALU.add).then_inc(x3_ready, 1)

            dve.wait_ge(consts_ready, 4)
            ts(decay_rate[:], decay_rate[:], -1.0, None, ALU.mult).then_inc(consts_ready, 1)
            ts(conv_half[:], vec[:, V_CW:V_CW + 20], 0.5, None, ALU.mult).then_inc(consts_ready, 1)
            nc.vector.memset(bc_stack[0:32, :], 0.0).then_inc(consts_ready, 1)
            dve.wait_ge(consts_ready, 7)
            dve.wait_ge(loaded["x"], 16)
            convolve(0)
            normalize("att", 0, xa, xn_att)
            split_bc(0)
            for f in range(FT):
                rotate(0, f)
            attention(0, PLAN_FIRST)
            with dve.Fori(0, BATCH - 1) as t:
                dve.wait_ge(x2_ready, t + 1)
                normalize("ffn", t, xb, xn)
                convolve(t + 1)
                route(t)
                split_bc(t + 1)
                mask_low(t)
                for e in range(EVALS):
                    evaluate(t, e)
                    for piece in PLAN_NEXT[e]["dve"]:
                        scan_piece(t + 1, piece)
                    if e == NORM_SLOT:
                        dve.wait_ge(loaded["x"], 16 * t + 32)
                        normalize("att", t + 1, xa, xn_att)
                weigh_down(t)
                for f in range(FT):
                    rotate(t + 1, f)
                    for piece in PLAN_NEXT[DOWN + f]["dve"]:
                        scan_piece(t + 1, piece)
                finish(t)
                attention(t + 1, PLAN_NEXT)
            dve.wait_ge(x2_ready, BATCH)
            normalize("ffn", BATCH - 1, xb, xn)
            route(BATCH - 1)
            mask_low(BATCH - 1)
            for e in range(EVALS):
                evaluate(BATCH - 1, e)
            weigh_down(BATCH - 1)
            finish(BATCH - 1)


def constant_table():
    import numpy as np
    c = np.zeros((P, C_COLS), np.float32)
    p = np.arange(P)
    c[:, C_ID:C_ID + P] = np.eye(P)
    half = HD // 2
    for m in range(P):
        if m % HD < half:
            c[m + half, C_ROT + m] = -1.0
        else:
            c[m - half, C_ROT + m] = 1.0
    c[:, C_MASK:C_MASK + P] = np.where(p[None, :] <= p[:, None], 0.0, NEG)
    for k in range(32, P):
        c[k, C_SEL + k % 32] = 1.0
    inv = (np.float32(10000.0) ** (-np.arange(half, dtype=np.float32) / np.float32(half))).astype(np.float32)
    ang = (np.arange(L, dtype=np.float32)[None, :] * inv[p % half][:, None]).astype(np.float32)
    c[:, C_COS:C_COS + L] = np.cos(ang)
    c[:, C_SIN:C_SIN + L] = np.sin(ang)
    c[:, C_CAND:C_CAND + NE] = np.arange(NE, 0, -1)
    c[:, C_HALF:C_HALF + NT] = -0.5
    return c


def kernel(**inputs):
    import numpy as np
    import concourse.bacc as bacc
    from concourse.bass_utils import run_bass_kernel_spmd

    a = {k: np.asarray(v) for k, v in inputs.items()}

    def rows(w):
        return w.reshape(-1, P, w.shape[1]).transpose(1, 0, 2)

    def column(v):
        return v.reshape(-1, P).T

    wk4 = [rows(np.tile(a["L0_attn_wk"][g * HD:(g + 1) * HD].T, (1, HPT))) for g in range(KV_HEADS)]
    xw = a["L0_xattn_x_proj_w"].T
    bc = xw[:, RANK:]
    w_x = rows(np.concatenate([xw[:, :RANK], np.zeros((DI, 16), np.float32), bc, bc, bc], axis=1))
    w_dt = np.zeros((P, DI), np.float32)
    w_dt[:RANK] = a["L0_xattn_dt_proj_w"].T

    def adapters(w):
        return rows(w.reshape(NE * LR, D).T)

    wg, wu = rows(a["L0_ffn_Wg"].T), rows(a["L0_ffn_Wu"].T)
    bg = a["L0_ffn_Bg"].transpose(0, 2, 1).reshape(NE * LR, DFF)
    bu = a["L0_ffn_Bu"].transpose(0, 2, 1).reshape(NE * LR, DFF)
    ad = a["L0_ffn_Ad"].reshape(NE * LR, DFF).T
    tiles, tile_adapters = [], []
    for f in range(FT):
        cols = slice(f * P, (f + 1) * P)
        tiles.append(np.concatenate([wg[:, :, cols].reshape(P, -1), wu[:, :, cols].reshape(P, -1)], axis=1))
        tile_adapters.append(np.concatenate([bg[:, cols], bu[:, cols]], axis=1))
    vectors = np.concatenate([
        a["L0_xattn_conv_w"].reshape(JT, P, TAPS).transpose(1, 0, 2).reshape(P, -1),
        column(a["L0_xattn_conv_b"]), column(a["L0_xattn_dt_proj_b"]),
        a["L0_xattn_A_log"].reshape(JT, P, NS).transpose(1, 0, 2).reshape(P, -1),
        column(a["L0_xattn_D"]), column(a["L0_attn_bq"]),
        np.stack([np.tile(a["L0_attn_bk"][g * HD:(g + 1) * HD], HPT) for g in range(KV_HEADS)], axis=1),
        np.tile(a["L0_attn_bv"][None, :], (P, 1)),
    ], axis=1)
    arrays = {
        "x": a["x"],
        "ctx_t": a["ctx_1024"].transpose(0, 2, 1),
        "wq": rows(a["L0_attn_wq"].T),
        "wk": np.stack(wk4, axis=1),
        "wv": rows(a["L0_attn_wv"].T),
        "wo": rows(a["L0_attn_wo"].T),
        "w_in": rows(a["L0_xattn_in_proj_w"].T),
        "w_x": w_x,
        "w_dt": w_dt,
        "w_lora": np.stack([adapters(a["L0_ffn_Ag"]), adapters(a["L0_ffn_Au"])], axis=1),
        "w_r": rows(a["L0_ffn_Wr"].T),
        "b_down": a["L0_ffn_Bd"].transpose(0, 2, 1).reshape(NE * LR, D),
        "a_down": rows(ad),
        "w_tiles": np.stack(tiles),
        "w_adapt": np.stack(tile_adapters),
        "w_down": a["L0_ffn_Wd"].T.reshape(FT, P, D),
        "vectors": vectors,
        "constants": constant_table(),
    }
    arrays = {k: np.ascontiguousarray(v) for k, v in arrays.items()}
    nc = bacc.Bacc("TRN2", target_bir_lowering=False, num_devices=1, dynamic_dma_scratch_size=1024)
    args = [nc.dram_tensor("in_" + k, v.shape, mybir.dt.from_np(v.dtype), kind="ExternalInput").ap()
            for k, v in arrays.items()]
    args.append(nc.dram_tensor("out_x", (BATCH, L, D), F32, kind="ExternalOutput").ap())
    decoder_layer(nc, *args)
    r = run_bass_kernel_spmd(nc, [{"in_" + k: v for k, v in arrays.items()}], core_ids=[0])
    return r.results[0]["out_x"]
```

```python
from contextlib import ExitStack

import concourse.bass as bass
from concourse import mybir

F32 = mybir.dt.float32
BF16 = mybir.dt.bfloat16
ALU = mybir.AluOpType
ACT = mybir.ActivationFunctionType
AX = mybir.AxisListType

P = 128
BATCH, L, D = 4, 512, 512
HEADS, KV_HEADS, HD = 16, 2, 32
NT = L // P
KT = D // P
MT = HEADS * HD // P
HPT = P // HD
CTX = 256
CT = CTX // P
DI = 512
JT = DI // P
NS = 16
RANK = 16
TAPS = 4
DFF = 1408
FT = DFF // P
NE, LR = 8, 16
EPS = 1e-5
SCALE = HD ** -0.5
NEG = -1e30

WG, WU, WBASE = 0, KT * P, 2 * KT * P
BG, BU, WADAPT = 0, P, 2 * P
C_ID, C_ROT, C_MASK, C_SEL, C_COS, C_SIN = 0, 128, 256, 384, 416, 928
C_CAND, C_HALF = 1440, 1448
C_COLS = 1452
V_CW, V_CB, V_DTB, V_AL, V_D, V_BQ, V_BK, V_BV = 0, 16, 20, 24, 88, 92, 96, 98
V_COLS = V_BV + 1
VD = KV_HEADS * HD

def log1p_coefficients(degree):
    import numpy as np
    nodes = 0.5 + 0.5 * np.cos(np.pi * (np.arange(64) + 0.5) / 64)
    fit = np.polynomial.Chebyshev.fit(nodes, np.log1p(nodes) / nodes, degree, domain=[0, 1])
    return [float(c) for c in fit.convert(kind=np.polynomial.Polynomial).coef]


POLY = log1p_coefficients(9)
NPOLY = len(POLY)


EVAL = [(0, 0)]
for _f in range(FT):
    EVAL += [(_f, 1)] + [(_f + 1, 0)] * (_f + 1 < FT) + [(_f, 2)]
EVAL_AT = {fk: e for e, fk in enumerate(EVAL)}
EVALS = len(EVAL)
STEPS = MT * NT * 2
DOWN = EVALS
ATT = DOWN + FT
SLOTS = ATT + STEPS
NORM_SLOTS = [EVAL_AT[FT - 2 - NT + i, 2] for i in range(NT)]
DT_SLOTS = (2, 3)
POLY_AT = 4
PV_AT = 5
OUT_AT = (STEPS - 1, STEPS + 1, STEPS + 2, STEPS + 3)
XIN_EARLY = JT - 1


def between(free, used):
    for s in range(free + 1, used):
        if s >= EVALS or EVAL[s][1] == 1:
            return s
    assert used > free
    return min(free + 1, used)


def plan(counts):
    pieces = [("poly", k) for k in range(NPOLY + 2)]
    for n in range(NS):
        pieces += [("mul", n), ("run", n), ("out", n)]
    assert sum(counts) == len(pieces), (sum(counts), len(pieces))
    slots, at, k = [{"dve": [], "bc": [], "decay": [], "add": []} for _ in range(SLOTS)], {}, 0
    for s, count in enumerate(counts):
        for piece in pieces[k:k + count]:
            slots[s]["dve"].append(piece)
            at[piece] = s
        k += count
    for n in range(NS):
        slots[between(at["poly", NPOLY - 4] if n < 2 else at["out", n - 2], at["mul", n])]["bc"].append(n)
        slots[between(at["poly", NPOLY + 1] if n < 2 else at["run", n - 2], at["run", n])]["decay"].append(n)
        slots[at["out", n]]["add"].append(n)
    return slots


def spread_over(total, places):
    return [(k + 1) * total // places - k * total // places for k in range(places)]


PIECES = NPOLY + 2 + 3 * NS
IN_EVALS = [(0, 2, 1)[k] if e >= POLY_AT else 0 for e, (f, k) in enumerate(EVAL)]
IN_DOWN = 22
FREE_DOWN = 1
LAST_STEPS = 1
EARLY_FIRST = [5, 5]
IN_DOWN_FIRST = 13
PLAN_FIRST = plan([0] * DOWN + EARLY_FIRST + spread_over(IN_DOWN_FIRST - sum(EARLY_FIRST), FT - 2) +
                  spread_over(PIECES - IN_DOWN_FIRST, STEPS - LAST_STEPS) + [0] * LAST_STEPS)
PLAN_NEXT = plan(IN_EVALS + spread_over(IN_DOWN, FT - FREE_DOWN) + [0] * FREE_DOWN +
                 spread_over(PIECES - sum(IN_EVALS) - IN_DOWN, STEPS - LAST_STEPS) + [0] * LAST_STEPS)


def projections(f):
    raw = f - 1 if 1 <= f <= MT + KV_HEADS else None
    back = f - 2 if 2 <= f <= MT + KV_HEADS + 1 else None
    return raw, back, {MT + KV_HEADS + 2: 0, MT + KV_HEADS + 3: 1}.get(f)


def broadcasts(slots, s):
    return [("bc", 2 * n + c) for n in slots[s]["bc"] for c in range(2)]


def dt_uses(e):
    return [("dt", j) for j in range(JT) if DT_SLOTS[j * len(DT_SLOTS) // JT] == e]


def out_tiles(s):
    return [OUT_AT.index(s)] if s in OUT_AT else []


def value_groups(s):
    if s == PV_AT + STEPS - 3:
        return [STEPS // 2 - 1]
    return [(s - PV_AT) // 2] if PV_AT <= s < PV_AT + STEPS - 3 and (s - PV_AT) % 2 == 0 else []


def uses_of(first, last):
    names = []
    if first:
        names += [("xin", j) for j in range(JT)] + [("dt", j) for j in range(JT)]
    else:
        if not last:
            names += [("xin", j) for j in range(XIN_EARLY)]
        names += [("yt", i) for i in range(NT)]
        if not last:
            names += [("xin", j) for j in range(XIN_EARLY, JT)]
        names += [("xt2", i) for i in range(NT)] + [("mask", k) for k in range(4)] + [("lowg", 0), ("lowu", 0)]
        if not last:
            for e in range(EVALS):
                names += broadcasts(PLAN_NEXT, e) + dt_uses(e)
            names += [("xt", i) for i in range(NT)]
    if not last:
        slots = PLAN_FIRST if first else PLAN_NEXT
        for f in range(FT):
            if f == 0 and first:
                names += [("xt", i) for i in range(NT)]
            raw, back, _ = projections(f)
            names += broadcasts(slots, DOWN + f)
            names += [("raw", raw)] * (raw is not None) + [("back", back)] * (back is not None)
        for s in range(STEPS + 4):
            if s < STEPS:
                names += broadcasts(slots, ATT + s)
            names += [("pv", g) for g in value_groups(s)]
            names += [("op", i) for i in out_tiles(s)]
    return {name: k for k, name in enumerate(names)}


USES_FIRST, USES_NEXT, USES_LAST = uses_of(True, False), uses_of(False, False), uses_of(False, True)
assert len(USES_FIRST) % 2 == 0 and len(USES_NEXT) % 2 == 0


def decoder_layer(nc, x, ctx_t, wq, wk, wv, wo, w_in, w_x, w_dt, w_lora, w_r, b_down, a_down, w_tiles, w_adapt, w_down,
                  vectors, constants, out):
    with ExitStack() as stack:
        def sb(name, shape, dt=F32):
            return stack.enter_context(nc.sbuf_tensor(name, shape, dt))

        def ps(name, shape):
            return stack.enter_context(nc.psum_tensor(name, shape, F32))

        def sem(name):
            return stack.enter_context(nc.semaphore(name))

        wq_sb = sb("wq_sb", [P, KT, HEADS * HD])
        wk_sb = sb("wk_sb", [P, KV_HEADS, KT, P])
        wv_sb = sb("wv_sb", [P, KT, P])
        wo_sb = sb("wo_sb", [P, MT, D])
        win_sb = sb("win_sb", [P, CT, DI])
        wx_sb = sb("wx_sb", [P, JT, P])
        wdt_sb = sb("wdt_sb", [P, DI])
        lora_sb = sb("lora_sb", [P, 2, KT, P])
        wr_sb = sb("wr_sb", [P, KT, NE])
        bd_sb = sb("bd_sb", [P, D])
        ad_sb = sb("ad_sb", [P, FT, P])
        vec = sb("vec", [P, V_COLS])
        cst = sb("cst", [P, C_COLS])
        ident_b = sb("ident_b", [P, P], BF16)
        mask_b = sb("mask_b", [P, P], BF16)
        sel_b = sb("sel_b", [P, 2 * NS], BF16)
        decay_rate = sb("decay_rate", [P, JT, NS])
        conv_half = sb("conv_half", [P, 20])
        ident = cst[:, C_ID:C_ID + P]
        rot = cst[:, C_ROT:C_ROT + P]
        cos_t, sin_t = cst[:, C_COS:C_COS + L], cst[:, C_SIN:C_SIN + L]
        xa = sb("xa", [P, NT, D])
        xb = sb("xb", [P, NT, D])
        xt = sb("xt", [P, KT, L])
        r1 = sb("r1", [P, 12, L])
        probs, xn, hb = r1[:, 0:4, :], r1[:, 8:12, :], r1[:, 0:FT, :]
        probs_t = [r1[:, 4 + k, :] for k in range(4)] + [xt[:, k, :] for k in range(4)]
        attn_t, down_low = xn, r1[:, FT, :]
        xn_att = sb("xn_att", [P, NT, D])
        r2 = sb("r2", [P, 15, L])
        keys, q_t, q_raw, rope_tmp = r2[:, 0:8, :], r2[:, 8:12, :], r2[:, 12:14, :], r2[:, 14, :]
        gate, hk, low, mask_t = r2[:, 0:2, :], r2[:, 2:6, :], r2[:, 6:10, :], r2[:, 10:14, :]
        expanded = r2[:, 2:6, :]
        hz = r2[:, 0:4, :]
        silu_z = [r2[:, k, :] for k in (8, 9, 10, 12)]
        v_sb = sb("v_sb", [P, NT, KV_HEADS * HD])
        w_sb = sb("w_sb", [P, 2, WBASE])
        wb_sb = sb("wb_sb", [P, 2, WADAPT])
        wd_sb = sb("wd_sb", [P, 2, D])
        ctx_sb = xn_att[:, 0:CT, :]
        dt_sb = sb("dt_sb", [P, JT, L])
        du_sb = sb("du_sb", [P, JT, L])
        y_sb = sb("y_sb", [P, JT, L])
        state = sb("state", [P, 2, JT, L])
        decay = sb("decay", [P, 2, JT, L])
        bc_sb = sb("bc_sb", [P, 2, 2, L])
        xdt_sb = sb("xdt_sb", [P, L])
        bc_stack = sb("bc_stack", [P, L], BF16)
        split_f = sb("split_f", [P, L])
        split_b = sb("split_b", [P, L], BF16)
        u_sb, exp_v, relu_v, conv_sb = state[:, 0, :, :], state[:, 1, :, :], decay[:, 0, :, :], decay[:, 1, :, :]
        xin_sb = relu_v
        keys_flat = [split_f[:], xdt_sb[:]]
        scrap = sb("scrap", [1, 1])
        scrap_a = sb("scrap_a", [1, 1])
        stats = sb("stats", [P, NT, 6])
        mv = sb("mv", [P, NT, 2])
        var_eps = sb("var_eps", [P, NT])
        rstd = sb("rstd", [P, NT])
        neg_max = sb("neg_max", [P, 2, 2])
        q_bias = sb("q_bias", [P, MT])
        row_sum = sb("row_sum", [P, 2, 2])
        row_inv = sb("row_inv", [P, 4, HPT])
        rt = sb("rt", [P, 8, NT, NE])
        rs = sb("rs", [P, 8, NT])

        ps_a = ps("ps_a", [P, 4, L])
        def score_place(s, k):
            width = (s // 2 % NT + 1) * P
            if 2 * width <= L:
                return ps_a[:, 2 * (s % 2), k * width:(k + 1) * width]
            return ps_a[:, 2 * (s % 2) + k, 0:width]

        ps_b = ps("ps_b", [P, 2, L])
        ps_w = ps("ps_w", [P, 2, L])

        loaded = {k: sem("loaded_" + k) for k in ("vec", "const", "in", "att", "mamba", "ffn", "ctx", "x")}
        w_loaded = [sem(f"w_loaded{k}") for k in range(2)]
        wb_loaded = [sem(f"wb_loaded{k}") for k in range(2)]
        wd_loaded = [sem(f"wd_loaded{k}") for k in range(2)]
        stored = sem("stored")
        consts_ready = sem("consts_ready")
        conv_halved = sem("conv_halved")
        work_full = [sem("work_full0"), sem("work_full1")]
        work_free = [sem("work_free0"), sem("work_free1")]
        norm_chain = {k: sem("norm_chain_" + k) for k in ("att", "z", "ffn")}
        rstd_ready = {k: sem("rstd_ready_" + k) for k in ("att", "z", "ffn")}
        xn_ready = {k: sem("xn_ready_" + k) for k in ("att", "z", "ffn")}
        xt_ready = {k: sem("xt_ready_" + k) for k in ("att", "ffn")}
        rope_chain = sem("rope_chain")
        qk_ready = sem("qk_ready")
        keys_zero = sem("keys_zero")
        keys_ready = sem("keys_ready")
        v_full = sem("v_full")
        v_moved = sem("v_moved")
        v_turned = sem("v_turned")
        v_ready = sem("v_ready")
        scores_ready = sem("scores_ready")
        neg_max_ready = sem("neg_max_ready")
        exp_done = sem("exp_done")
        inv_chain = sem("inv_chain")
        pt_full = sem("pt_full")
        pt_ready = sem("pt_ready")
        pv_done = sem("pv_done")
        inv_moved = sem("inv_moved")
        tanh_z = sem("tanh_z")
        z_chain = sem("z_chain")
        gated_ready = sem("gated_ready")
        x2_ready = sem("x2_ready")
        tap_ready = sem("tap_ready")
        conv_chain = sem("conv_chain")
        conv_tanh = sem("conv_tanh")
        u_ready = sem("u_ready")
        xdbl_full = sem("xdbl_full")
        xdt_ready = sem("xdt_ready")
        split_chain = sem("split_chain")
        bc_stack_ready = sem("bc_stack_ready")
        softplus_chain = sem("softplus_chain")
        softplus_in = sem("softplus_in")
        y_init = sem("y_init")
        poly_chain = sem("poly_chain")
        dt_ready = sem("dt_ready")
        decay_ready = sem("decay_ready")
        scan_chain = sem("scan_chain")
        y_added = sem("y_added")
        router_full = sem("router_full")
        router_chain = sem("router_chain")
        router_shift = sem("router_shift")
        router_exp = sem("router_exp")
        expanded_ready = sem("expanded_ready")
        low_ready = sem("low_ready")
        gu_ready = sem("gu_ready")
        tanh_ready = sem("tanh_ready")
        gate_chain = sem("gate_chain")
        h_ready = sem("h_ready")
        d_done = sem("d_done")
        down_chain = sem("down_chain")
        down_ready = sem("down_ready")
        wd_used = sem("wd_used")
        out_full = sem("out_full")
        x3_ready = sem("x3_ready")

        class Count:

            def __init__(self, semaphore, per, b):
                self.semaphore, self.per, self.b, self.n = semaphore, per, b, 0

            def inc(self, instruction):
                instruction.then_inc(self.semaphore, 1)
                self.n += 1

            def link(self, eng, instruction):
                self.inc(instruction)
                eng.wait_ge(self.semaphore, self.b * self.per + self.n)

            def end(self):
                assert self.n == self.per, (self.semaphore, self.n, self.per)

        def use(name, b, ffn=False):
            if ffn and isinstance(b, int) and b == BATCH - 1:
                k, before = USES_LAST[name], len(USES_FIRST) + (BATCH - 1) * len(USES_NEXT)
            elif not ffn and isinstance(b, int) and b == 0:
                k, before = USES_FIRST[name], 0
            else:
                i = b if ffn else b - 1
                k, before = USES_NEXT[name], None
                return k % 2, i * (len(USES_NEXT) // 2) + (len(USES_FIRST) // 2 + k // 2)
            return k % 2, (before + k) // 2

        def fill(eng, name, b, ffn=False):
            bank, count = use(name, b, ffn)
            if not (isinstance(count, int) and count == 0):
                eng.wait_ge(work_free[bank], count)
            return bank

        def filled(eng, name, b, ffn=False):
            bank, count = use(name, b, ffn)
            eng.wait_ge(work_full[bank], count + 1)
            return bank

        def first_batch(b):
            return isinstance(b, int) and b == 0

        block = stack.enter_context(nc.Block())

        @block.sync
        def _(sp):
            def load_ctx(b):
                if not first_batch(b):
                    sp.wait_ge(qk_ready, b * (MT + KV_HEADS))
                sp.dma_start(ctx_sb[:], ctx_t[b].rearrange("(t p) l -> p t l", p=P)).then_inc(loaded["ctx"], 16)

            def load_x(b):
                if not first_batch(b):
                    sp.wait_ge(x2_ready, b)
                sp.dma_start(xa[:], x[b].rearrange("(i p) d -> p i d", p=P)).then_inc(loaded["x"], 16)

            def load_w(t, f):
                if f >= 2:
                    sp.wait_ge(gu_ready, t * EVALS + EVAL_AT[f - 2, 0] + 1)
                else:
                    sp.wait_ge(scores_ready, t * STEPS + 1)
                sp.dma_start(w_sb[:, f % 2, :], w_tiles[f]).then_inc(w_loaded[f % 2], 16)

            def load_wb(t, f):
                if f >= 2:
                    sp.wait_ge(gu_ready, t * EVALS + EVAL_AT[f - 2, 2] + 1)
                sp.dma_start(wb_sb[:, f % 2, :], w_adapt[f]).then_inc(wb_loaded[f % 2], 16)

            def load_wd(t, f):
                if f >= 2:
                    sp.wait_ge(wd_used, t * FT + f - 1)
                else:
                    sp.wait_ge(scores_ready, t * STEPS + 1)
                sp.dma_start(wd_sb[:, f % 2, :], w_down[f]).then_inc(wd_loaded[f % 2], 16)

            def ffn_loads(t):
                for f in range(2, FT):
                    load_w(t, f)
                    load_wb(t, f)
                for f in range(FT):
                    load_wd(t, f)
                for i in range(NT):
                    sp.wait_ge(x3_ready, t * NT + i + 1)
                    sp.dma_start(out[t].rearrange("(i p) d -> p i d", p=P)[:, i, :], xb[:, i, :]).then_inc(stored, 16)

            load_ctx(0)
            sp.dma_start(wx_sb[:], w_x).then_inc(loaded["mamba"], 16)
            load_x(0)
            sp.dma_start(wk_sb[:], wk).then_inc(loaded["att"], 16)
            sp.dma_start(wv_sb[:], wv).then_inc(loaded["att"], 16)
            sp.dma_start(wo_sb[:], wo).then_inc(loaded["att"], 16)
            sp.dma_start(lora_sb[:], w_lora).then_inc(loaded["ffn"], 16)
            sp.dma_start(wr_sb[:], w_r).then_inc(loaded["ffn"], 16)
            sp.dma_start(bd_sb[:], b_down).then_inc(loaded["ffn"], 16)
            sp.dma_start(ad_sb[:], a_down).then_inc(loaded["ffn"], 16)
            with sp.Fori(0, BATCH - 1) as t:
                load_ctx(t + 1)
                for f in range(2):
                    load_w(t, f)
                    load_wb(t, f)
                load_x(t + 1)
                ffn_loads(t)
            for f in range(2):
                load_w(BATCH - 1, f)
                load_wb(BATCH - 1, f)
            ffn_loads(BATCH - 1)
            sp.wait_ge(stored, 16 * NT * BATCH)

        @block.gpsimd
        def _(pool):
            def inverse_deviation(kind, b, tiles=range(NT)):
                for i in tiles:
                    pool.wait_ge(norm_chain[kind], (b * NT + i) * 3 + 3)
                    nc.gpsimd.tensor_tensor(rstd[:, i:i + 1], var_eps[:, i:i + 1], cst[:, C_HALF:C_HALF + 1], ALU.pow)\
                        .then_inc(rstd_ready[kind], 1)

            def add_states(b, slot):
                for n in slot["add"]:
                    pool.wait_ge(scan_chain, b * 3 * NS + 3 * n + 3)
                    if n == 0:
                        pool.wait_ge(y_init, b * JT + JT)
                    else:
                        pool.wait_ge(y_added, b * NS + n)
                    nc.gpsimd.tensor_tensor(y_sb[:], y_sb[:], state[:, n % 2, :, :], ALU.add).then_inc(y_added, 1)

            def clear_keys(b):
                pool.wait_ge(loaded["const"], 16)
                if not first_batch(b):
                    pool.wait_ge(down_ready, b)
                nc.gpsimd.memset(keys, 0.0).then_inc(keys_zero, 1)

            def attention(b, slots):
                for s in range(STEPS):
                    add_states(b, slots[ATT + s])
                inverse_deviation("z", b)

            pool.wait_ge(loaded["const"], 16)
            inverse_deviation("att", 0)
            clear_keys(0)
            for f in range(FT):
                add_states(0, PLAN_FIRST[DOWN + f])
            attention(0, PLAN_FIRST)
            with pool.Fori(0, BATCH - 1) as t:
                inverse_deviation("ffn", t)
                for e in range(EVALS):
                    inverse_deviation("att", t + 1, [i for i in range(NT) if NORM_SLOTS[i] == e])
                    add_states(t + 1, PLAN_NEXT[e])
                clear_keys(t + 1)
                for f in range(FT):
                    add_states(t + 1, PLAN_NEXT[DOWN + f])
                attention(t + 1, PLAN_NEXT)
            inverse_deviation("ffn", BATCH - 1)

        @block.scalar
        def _(act):
            def to_sbuf(dst, src, name, b, ffn=False):
                bank = use(name, b, ffn)[0]
                return nc.scalar.activation(dst, src, ACT.Copy).then_inc(work_free[bank], 1)

            def conv_tap(b, tiles):
                for j in tiles:
                    bank = filled(act, ("xin", j), b)
                    nc.scalar.activation(xin_sb[:, j, :], ps_w[:, bank, :], ACT.Copy).then_inc(tap_ready, 1)
                    nc.scalar.activation(conv_sb[:, j, :], ps_w[:, bank, :], ACT.Identity,
                                         bias=conv_half[:, 16 + j:17 + j],
                                         scale=conv_half[:, TAPS * j + 3:TAPS * j + 4]).then_inc(work_free[bank], 1)

            def conv_gate(b):
                for j in range(JT):
                    act.wait_ge(conv_chain, b * 3 * JT + 3 * j + 3)
                    nc.scalar.activation(exp_v[:, j, :], conv_sb[:, j, :], ACT.Tanh).then_inc(conv_tanh, 1)

            def split_first(b):
                act.wait_ge(xdbl_full, b + 1)
                nc.scalar.activation(xdt_sb[:], ps_b[:, 1, :], ACT.Copy).then_inc(xdt_ready, 1)
                act.wait_ge(u_ready, b * JT + JT)
                for j in range(JT):
                    nc.scalar.activation(y_sb[:, j, :], u_sb[:, j, :], ACT.Identity,
                                         scale=vec[:, V_D + j:V_D + j + 1]).then_inc(y_init, 1)

            def softplus_parts(b, tiles):
                for j in tiles:
                    bank = filled(act, ("dt", j), b)
                    bias = vec[:, V_DTB + j:V_DTB + j + 1]
                    nc.scalar.activation(exp_v[:, j, :], ps_w[:, bank, :], ACT.Abs, bias=bias)\
                        .then_inc(softplus_chain, 1)
                    act.wait_ge(softplus_chain, (b * JT + j) * 2 + 1)
                    nc.scalar.activation(exp_v[:, j, :], exp_v[:, j, :], ACT.Exp, scale=-1.0)\
                        .then_inc(softplus_chain, 1)
                    nc.scalar.activation(relu_v[:, j, :], ps_w[:, bank, :], ACT.Relu, bias=bias)\
                        .then_inc(work_free[bank], 1)
                if JT - 1 in tiles:
                    act.wait_ge(softplus_chain, (b + 1) * 2 * JT)
                    nc.scalar.activation(scrap_a[:], vec[0:1, 0:1], ACT.Copy).then_inc(softplus_in, 1)

            def scan_inputs(b, slot):
                move_bc(b, slot)
                make_decay(b, slot)

            def move_bc(b, slot):
                for n in slot["bc"]:
                    for c in range(2):
                        if n >= 2:
                            act.wait_ge(scan_chain, b * 3 * NS + 3 * (n - 2) + (1 if c == 0 else 3))
                        elif not first_batch(b):
                            act.wait_ge(scan_chain, b * 3 * NS)
                        bank = filled(act, ("bc", 2 * n + c), b)
                        nc.scalar.activation(bc_sb[:, n % 2, c, :], ps_w[:, bank, :], ACT.Copy)\
                            .then_inc(work_free[bank], 1)

            def make_decay(b, slot):
                for n in slot["decay"]:
                    if n == 0:
                        act.wait_ge(dt_ready, b + 1)
                    if n >= 2:
                        act.wait_ge(scan_chain, b * 3 * NS + 3 * (n - 2) + 2)
                    for j in range(JT):
                        nc.scalar.activation(decay[:, n % 2, j, 1:L], dt_sb[:, j, 1:L], ACT.Exp,
                                             scale=decay_rate[:, j, n:n + 1]).then_inc(decay_ready, 1)

            def transposed(kind, name, b, ffn):
                for i in range(NT):
                    bank = filled(act, (name, i), b, ffn)
                    nc.scalar.activation(xt[:, :, i * P:(i + 1) * P],
                                         ps_w[:, bank, :].rearrange("p (k l) -> p k l", k=KT), ACT.Copy)\
                        .then_inc(work_free[bank], 1)

            def project(b, f):
                n = projections(f)[0]
                if n is not None:
                    bank = filled(act, ("raw", n), b)
                    if n >= 2:
                        act.wait_ge(qk_ready, b * (MT + KV_HEADS) + n - 1)
                    elif not first_batch(b):
                        act.wait_ge(down_ready, b)
                    bias = q_bias[:, n:n + 1] if n < MT else vec[:, V_BQ + n:V_BQ + n + 1]
                    nc.scalar.activation(q_raw[:, n % 2, :], ps_w[:, bank, :], ACT.Identity, bias=bias,
                                         scale=SCALE if n < MT else 1.0).then_inc(work_free[bank], 1)
                n = projections(f - 1)[1]
                if n is not None and n >= MT:
                    act.wait_ge(qk_ready, b * (MT + KV_HEADS) + n + 1)
                    if n == MT:
                        act.wait_ge(keys_zero, b + 1)
                    for j in range(HPT):
                        rows = slice(j * HD, (j + 1) * HD)
                        op = nc.scalar.activation(keys[rows, (n - MT) * HPT + j, :], keys_flat[n - MT][rows, :], ACT.Copy)
                    op.then_inc(keys_ready, 1)
                if projections(f)[2] == 0:
                    act.wait_ge(v_full, b + 1)
                    act.wait_ge(qk_ready, b * (MT + KV_HEADS) + MT + KV_HEADS - 1)
                    nc.scalar.activation(q_raw[:, 0, :], ps_b[:, 0, :], ACT.Identity,
                                         bias=vec[:, V_BV:V_BV + 1]).then_inc(v_moved, 1)

            def attention(b, slots):
                def exponents(s):
                    i = (s // 2) % NT
                    act.wait_ge(neg_max_ready, b * STEPS + s + 1)
                    if s >= 2:
                        act.wait_ge(inv_chain, b * STEPS + s - 1)
                    for k in range(2):
                        if s >= 2:
                            act.wait_ge(pt_full, b * 2 * STEPS + 2 * (s - 2) + k + 1)
                        nc.scalar.activation(probs[:, (2 * s + k) % 4, 0:(i + 1) * P],
                                             score_place(s, k), ACT.Exp,
                                             bias=neg_max[:, s % 2, k:k + 1],
                                             accum_out=row_sum[:, s % 2, k:k + 1]).then_inc(exp_done, 1)

                def move_transposed(s):
                    i = (s // 2) % NT
                    for k in range(2):
                        act.wait_ge(pt_full, b * 2 * STEPS + 2 * s + k + 1)
                        if s >= 4:
                            act.wait_ge(pv_done, b * (STEPS // 2) + s // 2 - 1)
                        nc.scalar.activation(probs_t[(2 * s + k) % 8][:, 0:(i + 1) * P],
                                             ps_b[:, k, 0:(i + 1) * P], ACT.Copy).then_inc(pt_ready, 1)

                def move_output(g):
                    m, i = g // NT, g % NT
                    bank = filled(act, ("pv", g), b)
                    nc.scalar.activation(attn_t[:, m, i * P:(i + 1) * P], ps_w[:, bank, P:2 * P], ACT.Copy)\
                        .then_inc(inv_moved, 1)

                for s in range(STEPS + 4):
                    if 2 <= s < STEPS + 2:
                        move_transposed(s - 2)
                    if s < STEPS:
                        move_bc(b, slots[ATT + s])
                        exponents(s)
                    for g in value_groups(s):
                        move_output(g)
                    if s < STEPS:
                        make_decay(b, slots[ATT + s])
                for i in range(NT - 1):
                    gate_z(b, i)

            def gate_z(b, i):
                act.wait_ge(xn_ready["z"], b * NT + i + 1)
                nc.scalar.activation(silu_z[i], hz[:, i, :], ACT.Tanh, scale=0.5).then_inc(tanh_z, 1)

            def ffn_masks(t):
                act.wait_ge(router_shift, t + 1)
                nc.scalar.activation(rt[:, 1, :, :], rt[:, 0, :, :], ACT.Exp).then_inc(router_exp, 1)
                for k in range(4):
                    bank = filled(act, ("mask", k), t, True)
                    nc.scalar.activation(mask_t[:, k, :], ps_w[:, bank, :], ACT.Copy).then_inc(work_free[bank], 1)

            def evaluate(t, e):
                f, k = EVAL[e]
                act.wait_ge(gu_ready, t * EVALS + e + 1)
                if e >= 2:
                    act.wait_ge(h_ready, t * EVALS + e - 1)
                nc.scalar.activation(gate[:, e % 2, :], ps_a[:, 2 * (f % 2), :], ACT.Tanh, scale=0.5)\
                    .then_inc(tanh_ready, 1)

            act.dma_start(win_sb[:], w_in).then_inc(loaded["in"], 16)
            act.dma_start(vec[:], vectors).then_inc(loaded["vec"], 16)
            act.dma_start(wdt_sb[:], w_dt).then_inc(loaded["mamba"], 16)
            act.dma_start(cst[:], constants).then_inc(loaded["const"], 16)
            act.dma_start(wq_sb[:], wq).then_inc(loaded["att"], 16)
            act.wait_ge(loaded["vec"], 16)
            nc.scalar.activation(decay_rate[:], vec[:, V_AL:V_AL + JT * NS].rearrange("p (j n) -> p j n", n=NS),
                                 ACT.Exp).then_inc(consts_ready, 1)
            act.wait_ge(conv_halved, 1)
            conv_tap(0, range(JT))
            act.wait_ge(loaded["const"], 16)
            nc.scalar.activation(ident_b[:], ident, ACT.Copy).then_inc(consts_ready, 1)
            nc.scalar.activation(mask_b[:], cst[:, C_MASK:C_MASK + P], ACT.Copy).then_inc(consts_ready, 1)
            nc.scalar.activation(sel_b[:], cst[:, C_SEL:C_SEL + 2 * NS], ACT.Copy).then_inc(consts_ready, 1)
            conv_gate(0)
            split_first(0)
            softplus_parts(0, range(JT))
            for f in range(FT):
                if f == 0:
                    transposed("att", "xt", 0, False)
                move_bc(0, PLAN_FIRST[DOWN + f])
                project(0, f)
                make_decay(0, PLAN_FIRST[DOWN + f])
            attention(0, PLAN_FIRST)
            with act.Fori(0, BATCH - 1) as t:
                conv_tap(t + 1, [0])
                gate_z(t, NT - 1)
                conv_tap(t + 1, range(1, JT))
                transposed("ffn", "xt2", t, True)
                ffn_masks(t)
                evaluate(t, 0)
                conv_gate(t + 1)
                split_first(t + 1)
                for e in range(EVALS):
                    if e > 0:
                        evaluate(t, e)
                    scan_inputs(t + 1, PLAN_NEXT[e])
                    softplus_parts(t + 1, [j for _, j in dt_uses(e)])
                for f in range(FT):
                    if f == 0:
                        transposed("att", "xt", t + 1, False)
                    move_bc(t + 1, PLAN_NEXT[DOWN + f])
                    project(t + 1, f)
                    make_decay(t + 1, PLAN_NEXT[DOWN + f])
                attention(t + 1, PLAN_NEXT)
            gate_z(BATCH - 1, NT - 1)
            transposed("ffn", "xt2", BATCH - 1, True)
            ffn_masks(BATCH - 1)
            for e in range(EVALS):
                evaluate(BATCH - 1, e)

        @block.tensor
        def _(pe):
            def project_in(b, tiles):
                pe.wait_ge(loaded["ctx"], 16 * b + 16)
                for j in tiles:
                    bank = fill(pe, ("xin", j), b)
                    for k in range(CT):
                        mm = nc.tensor.matmul(ps_w[:, bank, :], win_sb[:, k, j * P:(j + 1) * P], ctx_sb[:, k, :],
                                              start=(k == 0), stop=(k == CT - 1))
                    mm.then_inc(work_full[bank], 1)

            def project_x(b):
                for j in range(JT):
                    pe.wait_ge(u_ready, b * JT + j + 1)
                    mm = nc.tensor.matmul(ps_b[:, 1, :], wx_sb[:, j, :], u_sb[:, j, :],
                                          start=(j == 0), stop=(j == JT - 1))
                mm.then_inc(xdbl_full, 1)

            def project_dt(b, tiles):
                if 0 in tiles:
                    pe.wait_ge(xdt_ready, b + 1)
                for j in tiles:
                    bank = fill(pe, ("dt", j), b)
                    nc.tensor.matmul(ps_w[:, bank, :], wdt_sb[:, j * P:(j + 1) * P], xdt_sb[:],
                                     start=True, stop=True).then_inc(work_full[bank], 1)

            def broadcast_bc(b, slot):
                for n in slot["bc"]:
                    if n == 0:
                        pe.wait_ge(bc_stack_ready, b + 1)
                    for c in range(2):
                        bank = fill(pe, ("bc", 2 * n + c), b)
                        pick = sel_b[:, NS * c + n:NS * c + n + 1].to_broadcast([P, P])
                        nc.tensor.matmul(ps_w[:, bank, :], pick, bc_stack[:], start=True, stop=True)\
                            .then_inc(work_full[bank], 1)

            def transpose_normed(kind, name, b, ffn):
                src = xn if ffn else xn_att
                for i in range(NT):
                    pe.wait_ge(xn_ready[kind], b * NT + i + 1)
                    bank = fill(pe, (name, i), b, ffn)
                    for k in range(KT):
                        mm = nc.tensor.transpose(ps_w[:, bank, k * P:(k + 1) * P], src[:, i, k * P:(k + 1) * P], ident)
                    mm.then_inc(work_full[bank], 1)

            def xt_moved(name, b, ffn):
                for i in (NT - 2, NT - 1):
                    bank, count = use((name, i), b, ffn)
                    pe.wait_ge(work_free[bank], count + 1)

            def project(b, f):
                raw, back, values = projections(f)
                if raw is not None:
                    if raw == 0:
                        xt_moved("xt", b, False)
                    bank = fill(pe, ("raw", raw), b)
                    for k in range(KT):
                        w = wq_sb[:, k, raw * P:(raw + 1) * P] if raw < MT else wk_sb[:, raw - MT, k, :]
                        mm = nc.tensor.matmul(ps_w[:, bank, :], w, xt[:, k, :], start=(k == 0), stop=(k == KT - 1))
                    mm.then_inc(work_full[bank], 1)
                if back is not None:
                    bank = fill(pe, ("back", back), b)
                    raw_bank, raw_count = use(("raw", back), b)
                    pe.wait_ge(work_free[raw_bank], raw_count + 1)
                    nc.tensor.matmul(ps_w[:, bank, :], rot, q_raw[:, back % 2, :], start=True, stop=True)\
                        .then_inc(work_full[bank], 1)
                if values == 0:
                    if not first_batch(b):
                        pe.wait_ge(down_ready, b)
                    for k in range(KT):
                        mm = nc.tensor.matmul(ps_b[:, 0, :], wv_sb[:, k, :], xt[:, k, :],
                                              start=(k == 0), stop=(k == KT - 1))
                    mm.then_inc(v_full, 1)
                if values == 1:
                    pe.wait_ge(v_moved, b + 1)
                    for i in range(NT):
                        mm = nc.tensor.transpose(ps_b[:, 0, i * P:(i + 1) * P], q_raw[:, 0, i * P:(i + 1) * P], ident)
                    mm.then_inc(v_turned, 1)

            def attention(b, slots):
                pe.wait_ge(qk_ready, (b + 1) * (MT + KV_HEADS))
                pe.wait_ge(keys_ready, (b + 1) * KV_HEADS)
                pe.wait_ge(v_ready, b + 1)

                def scores(s):
                    m, i, pair = s // (2 * NT), (s // 2) % NT, s % 2
                    if s >= 2:
                        pe.wait_ge(exp_done, b * 2 * STEPS + 2 * (s - 2) + 2)
                    elif not first_batch(b):
                        pe.wait_ge(x3_ready, b * NT - 2 + 2 * s)
                    width = (i + 1) * P
                    first_key = (m * KV_HEADS // MT) * HPT + 2 * pair
                    if 2 * width <= L:
                        both = ps_a[:, 2 * (s % 2), 0:2 * width].rearrange("p (k l) -> p k l", k=2)
                        nc.tensor.matmul(both, q_t[:, m, i * P:(i + 1) * P], keys[:, first_key:first_key + 2, 0:width],
                                         start=True, stop=False)
                        mm = nc.tensor.matmul(both[:, :, i * P:width], ident_b[:],
                                              mask_b[:].unsqueeze(1).to_broadcast([P, 2, P]), start=False, stop=True)
                    else:
                        for k in range(2):
                            nc.tensor.matmul(score_place(s, k), q_t[:, m, i * P:(i + 1) * P],
                                             keys[:, first_key + k, 0:width], start=True, stop=False)
                            mm = nc.tensor.matmul(score_place(s, k)[:, i * P:width], ident_b[:], mask_b[:],
                                                  start=False, stop=True)
                    mm.then_inc(scores_ready, 1)

                def transpose_probs(s):
                    i = (s // 2) % NT
                    for k in range(2):
                        pe.wait_ge(exp_done, b * 2 * STEPS + 2 * s + k + 1)
                        if s >= 1:
                            pe.wait_ge(pt_ready, b * 2 * STEPS + 2 * (s - 1) + k + 1)
                        for kt in range(i + 1):
                            mm = nc.tensor.transpose(ps_b[:, k, kt * P:(kt + 1) * P],
                                                     probs[:, (2 * s + k) % 4, kt * P:(kt + 1) * P], ident)
                        mm.then_inc(pt_full, 1)

                def weigh_values(g):
                    m, i = g // NT, g % NT
                    bank = fill(pe, ("pv", g), b)
                    pe.wait_ge(pt_ready, b * 2 * STEPS + 4 * g + 4)
                    kv = m * KV_HEADS // MT
                    pe.wait_ge(inv_chain, b * STEPS + 2 * g + 2)
                    for j in range(HPT):
                        nc.tensor.matmul(ps_w[j * HD:(j + 1) * HD, bank, P:2 * P],
                                         row_inv[:, g % 4, j:j + 1].to_broadcast([P, HD]), ident,
                                         start=True, stop=True, tile_position=(0, j * HD))
                    for kt in range(i + 1):
                        for j in range(HPT):
                            mm = nc.tensor.matmul(ps_w[j * HD:(j + 1) * HD, bank, 0:P],
                                                  v_sb[:, kt, kv * HD:(kv + 1) * HD],
                                                  probs_t[4 * (g % 2) + j][:, kt * P:(kt + 1) * P],
                                                  start=(kt == 0), stop=(kt == i), tile_position=(0, j * HD))
                    mm.then_inc(work_full[bank], 1)
                    nc.tensor.nop().then_inc(pv_done, 1)

                for s in range(STEPS + 4):
                    if s < STEPS:
                        scores(s)
                    if 2 <= s < STEPS + 2:
                        transpose_probs(s - 2)
                    if s < STEPS:
                        broadcast_bc(b, slots[ATT + s])
                    for g in value_groups(s):
                        weigh_values(g)
                    for i in out_tiles(s):
                        project_out(b, i)

            def project_out(b, i):
                bank = fill(pe, ("op", i), b)
                pv_bank, pv_count = use(("pv", (MT - 1) * NT + i), b)
                pe.wait_ge(work_free[pv_bank], pv_count + 1)
                for m in range(MT):
                    mm = nc.tensor.matmul(ps_w[:, bank, :], attn_t[:, m, i * P:(i + 1) * P], wo_sb[:, m, :],
                                          start=(m == 0), stop=(m == MT - 1))
                mm.then_inc(work_full[bank], 1)

            def transpose_gated(t):
                pe.wait_ge(gated_ready, t * JT + JT)
                for i in range(NT):
                    bank = fill(pe, ("yt", i), t, True)
                    for j in range(JT):
                        mm = nc.tensor.transpose(ps_w[:, bank, j * P:(j + 1) * P], silu_z[j][:, i * P:(i + 1) * P], ident)
                    mm.then_inc(work_full[bank], 1)

            def base(t, f):
                slot = f % 2
                of_slot = (FT - slot + 1) // 2
                pe.wait_ge(w_loaded[slot], 16 * (t * of_slot + f // 2 + 1))
                if f >= 2:
                    pe.wait_ge(h_ready, t * EVALS + EVAL_AT[f - 2, 2] + 1)
                for half, at in ((0, WG), (1, WU)):
                    for k in range(KT):
                        mm = nc.tensor.matmul(ps_a[:, 2 * (f % 2) + half, :],
                                              w_sb[:, slot, at + k * P:at + (k + 1) * P], xt[:, k, :],
                                              start=(k == 0), stop=False, skip_group_check=True)
                mm.then_inc(gu_ready, 1)

            def add_slot(t, f, k):
                if k == 1:
                    of_slot = (FT - f % 2 + 1) // 2
                    pe.wait_ge(wb_loaded[f % 2], 16 * (t * of_slot + f // 2 + 1))
                pe.wait_ge(h_ready, t * EVALS + EVAL_AT[f, k - 1] + 1)
                for half, at in ((0, BG), (1, BU)):
                    mm = nc.tensor.matmul(ps_a[:, 2 * (f % 2) + half, :], wb_sb[:, f % 2, at:at + P],
                                          low[:, 2 * half + k - 1, :], start=False, stop=(k == 2),
                                          skip_group_check=True)
                mm.then_inc(gu_ready, 1)

            def down_adapters(t, f):
                pe.wait_ge(h_ready, t * EVALS + EVAL_AT[f, 2] + 1)
                for k in (1, 2):
                    mm = nc.tensor.matmul(ps_b[:, k - 1, :], ad_sb[:, f, :], hk[:, (2 * f + k - 1) % 4, :],
                                          start=(f == 0), stop=(f == FT - 1), skip_group_check=True)
                mm.then_inc(d_done, 1)

            def ffn_head(t):
                transpose_normed("ffn", "xt2", t, True)
                for i in range(NT):
                    bank, count = use(("xt2", i), t, True)
                    pe.wait_ge(work_free[bank], count + 1)
                    for k in range(KT):
                        mm = nc.tensor.matmul(ps_b[:, 0, i * NE:(i + 1) * NE], xt[:, k, i * P:(i + 1) * P],
                                              wr_sb[:, k, :], start=(k == 0), stop=(k == KT - 1))
                mm.then_inc(router_full, 1)
                base(t, 0)

            def ffn_masks(t):
                pe.wait_ge(expanded_ready, 4 * t + 4)
                for k in range(4):
                    bank = fill(pe, ("mask", k), t, True)
                    for i in range(NT):
                        mm = nc.tensor.transpose(ps_w[:, bank, i * P:(i + 1) * P], expanded[:, k, i * P:(i + 1) * P],
                                                 ident)
                    mm.then_inc(work_full[bank], 1)
                for half, name in ((0, "lowg"), (1, "lowu")):
                    bank = fill(pe, (name, 0), t, True)
                    for k in range(KT):
                        mm = nc.tensor.matmul(ps_w[:, bank, :], lora_sb[:, half, k, :], xt[:, k, :],
                                              start=(k == 0), stop=(k == KT - 1))
                    mm.then_inc(work_full[bank], 1)

            def ffn_tiles(t, b, slots):
                pe.wait_ge(low_ready, 4 * t + 4)
                if b is not None:
                    pe.wait_ge(xdt_ready, b + 1)

                def beside(e):
                    if b is not None:
                        broadcast_bc(b, slots[e])
                        project_dt(b, [j for _, j in dt_uses(e)])

                beside(0)
                for f in range(FT):
                    add_slot(t, f, 1)
                    beside(EVAL_AT[f, 1])
                    if f + 1 < FT:
                        base(t, f + 1)
                        beside(EVAL_AT[f + 1, 0])
                    if f == FT - 1:
                        down_adapters(t, f - 1)
                    add_slot(t, f, 2)
                    beside(EVAL_AT[f, 2])
                    if 0 < f < FT - 1:
                        down_adapters(t, f - 1)
                if b is not None:
                    transpose_normed("att", "xt", b, False)
                down_adapters(t, FT - 1)
                for f in range(FT):
                    if b is not None:
                        broadcast_bc(b, slots[DOWN + f])
                    of_slot = (FT - f % 2 + 1) // 2
                    pe.wait_ge(wd_loaded[f % 2], 16 * (t * of_slot + f // 2 + 1))
                    for i in range(NT):
                        mm = nc.tensor.matmul(ps_a[:, i, :], hb[:, f, i * P:(i + 1) * P], wd_sb[:, f % 2, :],
                                              start=(f == 0), stop=False, skip_group_check=True)
                    mm.then_inc(wd_used, 1)
                    if b is not None:
                        project(b, f)
                pe.wait_ge(down_ready, t + 1)
                for i in range(NT):
                    nc.tensor.matmul(ps_a[:, i, :], down_low[:, i * P:(i + 1) * P], bd_sb[:],
                                     start=False, stop=True, skip_group_check=True).then_inc(out_full, 1)

            pe.wait_ge(loaded["in"], 16)
            project_in(0, range(JT))
            pe.wait_ge(loaded["mamba"], 32)
            project_x(0)
            project_dt(0, range(JT))
            pe.wait_ge(consts_ready, 6)
            pe.wait_ge(loaded["att"], 64)
            transpose_normed("att", "xt", 0, False)
            for f in range(FT):
                broadcast_bc(0, PLAN_FIRST[DOWN + f])
                project(0, f)
            attention(0, PLAN_FIRST)
            pe.wait_ge(loaded["ffn"], 64)
            with pe.Fori(0, BATCH - 1) as t:
                project_in(t + 1, range(XIN_EARLY))
                transpose_gated(t)
                project_in(t + 1, range(XIN_EARLY, JT))
                ffn_head(t)
                ffn_masks(t)
                project_x(t + 1)
                ffn_tiles(t, t + 1, PLAN_NEXT)
                attention(t + 1, PLAN_NEXT)
            transpose_gated(BATCH - 1)
            ffn_head(BATCH - 1)
            ffn_masks(BATCH - 1)
            ffn_tiles(BATCH - 1, None, None)

        @block.vector
        def _(dve):
            tt, ts, stt = nc.vector.tensor_tensor, nc.vector.tensor_scalar, nc.vector.scalar_tensor_tensor

            def deviation(kind, b, src, i):
                at = (b * NT + i) * 3
                nc.vector.bn_stats(stats[:, i, :], src[:, i, :]).then_inc(norm_chain[kind], 1)
                dve.wait_ge(norm_chain[kind], at + 1)
                nc.vector.tensor_copy(scrap[:], vec[0:1, 0:1])
                nc.vector.bn_aggr(mv[:, i, :], stats[:, i, :]).then_inc(norm_chain[kind], 1)
                dve.wait_ge(norm_chain[kind], at + 2)
                ts(var_eps[:, i:i + 1], mv[:, i, 1:2], EPS, None, ALU.add).then_inc(norm_chain[kind], 1)

            def scaled(kind, b, src, dst, i):
                dve.wait_ge(rstd_ready[kind], b * NT + i + 1)
                ts(dst[:, i, :], src[:, i, :], mv[:, i, 0:1], rstd[:, i:i + 1], ALU.subtract, ALU.mult)\
                    .then_inc(xn_ready[kind], 1)

            def normalize(kind, b, src, dst):
                for i in range(NT):
                    deviation(kind, b, src, i)
                for i in range(NT):
                    scaled(kind, b, src, dst, i)

            def convolve(b, tiles):
                for j in tiles:
                    bank, count = use(("xin", j), b)
                    dve.wait_ge(tap_ready, b * JT + j + 1)
                    dve.wait_ge(work_free[bank], count + 1)
                    for back in range(1, TAPS):
                        tap = conv_half[:, TAPS * j + TAPS - 1 - back:TAPS * j + TAPS - back]
                        stt(conv_sb[:, j, back:L], xin_sb[:, j, 0:L - back], tap, conv_sb[:, j, back:L],
                            ALU.mult, ALU.add).then_inc(conv_chain, 1)
                        dve.wait_ge(conv_chain, (b * JT + j) * 3 + back)

            def activate(b):
                for j in range(JT):
                    dve.wait_ge(conv_tanh, b * JT + j + 1)
                    stt(u_sb[:, j, :], exp_v[:, j, :], 1.0, conv_sb[:, j, :], ALU.add, ALU.mult).then_inc(u_ready, 1)

            def split_bc(b):
                chain = Count(split_chain, 3, b)
                dve.wait_ge(xdt_ready, b + 1)
                nc.vector.tensor_copy(bc_stack[32:64, :], xdt_sb[32:64, :])
                chain.link(dve, nc.vector.tensor_copy(split_b[64:128, :], xdt_sb[64:128, :]))
                chain.link(dve, tt(split_f[64:128, :], xdt_sb[64:128, :], split_b[64:128, :], ALU.subtract))
                nc.vector.tensor_copy(bc_stack[64:96, :], split_f[64:96, :])
                chain.link(dve, nc.vector.tensor_copy(split_b[96:128, :], split_f[96:128, :]))
                tt(bc_stack[96:128, :], split_f[96:128, :], split_b[96:128, :], ALU.subtract).then_inc(bc_stack_ready, 1)
                chain.end()

            def scan_piece(b, piece):
                kind, n = piece
                if kind == "poly":
                    if n == 0:
                        dve.wait_ge(softplus_in, b + 1)
                        ts(du_sb[:], exp_v, POLY[-1], None, ALU.mult).then_inc(poly_chain, 1)
                    elif n < NPOLY:
                        dve.wait_ge(poly_chain, b * (NPOLY + 2) + n)
                        stt(du_sb[:].rearrange("p j l -> p (j l)"), du_sb[:].rearrange("p j l -> p (j l)"),
                            POLY[NPOLY - 1 - n], exp_v.rearrange("p j l -> p (j l)"), ALU.add, ALU.mult)\
                            .then_inc(poly_chain, 1)
                    elif n == NPOLY:
                        dve.wait_ge(poly_chain, b * (NPOLY + 2) + n)
                        tt(dt_sb[:], du_sb[:], relu_v, ALU.add).then_inc(poly_chain, 1)
                    else:
                        dve.wait_ge(poly_chain, b * (NPOLY + 2) + n)
                        tt(du_sb[:], dt_sb[:], u_sb, ALU.mult).then_inc(poly_chain, 1)
                        nc.vector.memset(decay[:, :, :, 0:1], 0.0).then_inc(dt_ready, 1)
                    return
                base = b * 3 * NS + 3 * n
                flat = state[:, n % 2, :, :].rearrange("p j l -> p (j l)")
                if kind == "mul":
                    if n == 0:
                        dve.wait_ge(poly_chain, (b + 1) * (NPOLY + 2))
                        dve.wait_ge(y_init, b * JT + JT)
                    elif n >= 2:
                        dve.wait_ge(y_added, b * NS + n - 1)
                    bank, count = use(("bc", 2 * n), b)
                    dve.wait_ge(work_free[bank], count + 1)
                    row = bc_sb[:, n % 2, 0, :].unsqueeze(1).to_broadcast([P, JT, L])
                    tt(state[:, n % 2, :, :], du_sb[:], row, ALU.mult).then_inc(scan_chain, 1)
                elif kind == "run":
                    dve.wait_ge(decay_ready, b * JT * NS + JT * n + JT)
                    dve.wait_ge(dt_ready, b + 1)
                    dve.wait_ge(scan_chain, base + 1)
                    nc.vector.tensor_tensor_scan(flat, decay[:, n % 2, :, :].rearrange("p j l -> p (j l)"), flat, 0.0,
                                                 ALU.mult, ALU.add).then_inc(scan_chain, 1)
                else:
                    bank, count = use(("bc", 2 * n + 1), b)
                    dve.wait_ge(work_free[bank], count + 1)
                    dve.wait_ge(scan_chain, base + 2)
                    row = bc_sb[:, n % 2, 1, :].unsqueeze(1).to_broadcast([P, JT, L])
                    tt(state[:, n % 2, :, :], state[:, n % 2, :, :], row, ALU.mult).then_inc(scan_chain, 1)

            def rotate(b, f):
                total = MT + KV_HEADS
                _, n, values = projections(f)
                if n is not None:
                    raw_bank, raw_count = use(("raw", n), b)
                    dve.wait_ge(work_free[raw_bank], raw_count + 1)
                    tt(rope_tmp, q_raw[:, n % 2, :], cos_t, ALU.mult).then_inc(rope_chain, 1)
                    bank = filled(dve, ("back", n), b)
                    part = q_t[:, n, :] if n < MT else keys_flat[n - MT]
                    tt(part, ps_w[:, bank, :], sin_t, ALU.mult).then_inc(work_free[bank], 1)
                    dve.wait_ge(rope_chain, b * total + n + 1)
                    bank, count = use(("back", n), b)
                    dve.wait_ge(work_free[bank], count + 1)
                    tt(part, part, rope_tmp, ALU.add).then_inc(qk_ready, 1)
                    dve.wait_ge(qk_ready, b * total + n + 1)
                if values == 1:
                    dve.wait_ge(v_turned, b + 1)
                    nc.vector.tensor_copy(v_sb[:], ps_b[:, 0, :].rearrange("p (i d) -> p i d", i=NT)[:, :, 0:VD])\
                        .then_inc(v_ready, 1)

            def attention(b, slots):
                def maxima(s):
                    i = (s // 2) % NT
                    dve.wait_ge(scores_ready, b * STEPS + s + 1)
                    width = (i + 1) * P
                    both = (ps_a[:, 2 * (s % 2), 0:2 * width].rearrange("p (k l) -> p k l", k=2) if 2 * width <= L
                            else ps_a[:, 2 * (s % 2):2 * (s % 2) + 2, 0:width])
                    nc.vector.tensor_reduce(neg_max[:, s % 2, :], both, AX.X, ALU.max, negate=True)\
                        .then_inc(neg_max_ready, 1)

                def invert_sums(s):
                    dve.wait_ge(exp_done, b * 2 * STEPS + 2 * s + 2)
                    nc.vector.reciprocal(row_inv[:, (s // 2) % 4, 2 * (s % 2):2 * (s % 2) + 2], row_sum[:, s % 2, :])\
                        .then_inc(inv_chain, 1)

                def divide(g):
                    m, i = g // NT, g % NT
                    bank = use(("pv", g), b)[0]
                    dve.wait_ge(inv_moved, b * MT * NT + g + 1)
                    place = attn_t[:, m, i * P:(i + 1) * P]
                    tt(place, ps_w[:, bank, 0:P], place, ALU.mult).then_inc(work_free[bank], 1)

                def gate_stages(i):
                    if i < NT:
                        first_sum(b, i)
                        deviation("z", b, xa, i)
                    if 1 <= i < NT + 1:
                        scaled("z", b, xa, hz, i - 1)
                    if i >= 2:
                        gate_y(b, i - 2)

                for s in range(STEPS + 4):
                    if s < STEPS:
                        maxima(s)
                    if 1 <= s <= STEPS:
                        invert_sums(s - 1)
                    if s < STEPS:
                        for piece in slots[ATT + s]["dve"]:
                            scan_piece(b, piece)
                    for g in value_groups(s):
                        divide(g)
                    for i in out_tiles(s):
                        gate_stages(i)
                gate_stages(NT)
                gate_stages(NT + 1)
                if not first_batch(b):
                    dve.wait_ge(stored, b * 16 * NT)

            def first_sum(b, i):
                bank = filled(dve, ("op", i), b)
                tt(xa[:, i, :], ps_w[:, bank, :], xa[:, i, :], ALU.add).then_inc(work_free[bank], 1)
                bank, count = use(("op", i), b)
                dve.wait_ge(work_free[bank], count + 1)

            def gate_y(b, j):
                dve.wait_ge(tanh_z, b * NT + j + 1)
                stt(silu_z[j], silu_z[j], 1.0, hz[:, j, :], ALU.add, ALU.mult).then_inc(z_chain, 1)
                if j == 0:
                    dve.wait_ge(y_added, b * NS + NS)
                dve.wait_ge(z_chain, b * NT + j + 1)
                stt(silu_z[j], y_sb[:, j, :], 0.5, silu_z[j], ALU.mult, ALU.mult).then_inc(gated_ready, 1)

            def second_sum(t):
                for i in range(NT + 1):
                    if i < NT:
                        bank, count = use(("yt", i), t, True)
                        dve.wait_ge(work_full[bank], count + 1)
                        tt(xb[:, i, :], ps_w[:, bank, :], xa[:, i, :], ALU.add).then_inc(work_free[bank], 1)
                        dve.wait_ge(work_free[bank], count + 1)
                        deviation("ffn", t, xb, i)
                    if i >= 1:
                        scaled("ffn", t, xb, xn, i - 1)
                nc.vector.tensor_copy(scrap[:], vec[0:1, 0:1]).then_inc(x2_ready, 1)

            def route(t):
                logits, prob, onehot, second = rt[:, 0], rt[:, 1], rt[:, 2], rt[:, 3]
                rank, tmp = rt[:, 4], rt[:, 5]
                cand = cst[:, C_CAND:C_CAND + NE].unsqueeze(1).to_broadcast([P, NT, NE])

                def spread(v):
                    return v.unsqueeze(2).to_broadcast([P, NT, NE])

                chain = Count(router_chain, 18, t)

                def then(op):
                    chain.link(dve, op)

                raw = ps_b[:, 0, 0:NT * NE].rearrange("p (i e) -> p i e", i=NT)
                dve.wait_ge(router_full, t + 1)
                then(nc.vector.tensor_reduce(rs[:, 0, :], raw, AX.X, ALU.max))
                tt(logits, raw, spread(rs[:, 0, :]), ALU.subtract).then_inc(router_shift, 1)
                dve.wait_ge(router_exp, t + 1)
                then(nc.vector.tensor_reduce(rs[:, 1, :], prob, AX.X, ALU.add))
                then(nc.vector.reciprocal(rs[:, 2, :], rs[:, 1, :]))
                then(tt(prob, prob, spread(rs[:, 2, :]), ALU.mult))

                def pick(source, weight, winner):
                    then(nc.vector.tensor_reduce(weight, source, AX.X, ALU.max))
                    then(tt(rank, source, spread(weight), ALU.is_equal))
                    then(tt(rank, rank, cand, ALU.mult))
                    then(nc.vector.tensor_reduce(rs[:, 5, :], rank, AX.X, ALU.max))
                    then(tt(winner, rank, spread(rs[:, 5, :]), ALU.is_equal))

                pick(prob, rs[:, 3, :], onehot)
                then(stt(tmp, onehot, -2.0, prob, ALU.mult, ALU.add))
                pick(tmp, rs[:, 4, :], second)

                then(tt(rt[:, 6], second, onehot, ALU.subtract))
                then(tt(rt[:, 7], onehot, spread(rs[:, 3, :]), ALU.mult))
                then(tt(rt[:, 5], second, spread(rs[:, 4, :]), ALU.mult))
                for k, table in enumerate((onehot, rt[:, 6], rt[:, 7], rt[:, 5])):
                    wide = expanded[:, k, :].rearrange("p (ie r) -> p ie r", r=LR)
                    narrow = table.rearrange("p i e -> p (i e)").unsqueeze(2).to_broadcast([P, NT * NE, LR])
                    ts(wide, narrow, 2.0, None, ALU.mult).then_inc(expanded_ready, 1)
                chain.end()

            def mask_low(t):
                for k in (2, 3):
                    bank, count = use(("mask", k), t, True)
                    dve.wait_ge(work_free[bank], count + 1)
                for half, name in ((0, "lowg"), (1, "lowu")):
                    bank = filled(dve, (name, 0), t, True)
                    tt(low[:, 2 * half, :], ps_w[:, bank, :], mask_t[:, 0, :], ALU.mult).then_inc(low_ready, 1)
                    tt(low[:, 2 * half + 1, :], ps_w[:, bank, :], mask_t[:, 1, :], ALU.mult).then_inc(low_ready, 1)
                    dve.wait_ge(low_ready, 4 * t + 2 * half + 2)
                    nc.vector.tensor_copy(scrap[:], ps_w[0:1, bank, 0:1]).then_inc(work_free[bank], 1)

            def evaluate(t, e):
                f, k = EVAL[e]
                bank = 2 * (f % 2)
                dve.wait_ge(tanh_ready, t * EVALS + e + 1)
                stt(gate[:, e % 2, :], gate[:, e % 2, :], 1.0, ps_a[:, bank, :], ALU.add, ALU.mult)\
                    .then_inc(gate_chain, 1)
                if k > 0 and f >= 2:
                    dve.wait_ge(d_done, t * FT + f - 1)
                dst = hb[:, f, :] if k == 0 else hk[:, (2 * f + k - 1) % 4, :]
                dve.wait_ge(gate_chain, t * EVALS + e + 1)
                tt(dst, gate[:, e % 2, :], ps_a[:, bank + 1, :], ALU.mult).then_inc(h_ready, 1)

            def weigh_down(t):
                dve.wait_ge(d_done, t * FT + FT)
                chain = Count(down_chain, 2, t)
                chain.inc(tt(mask_t[:, 2, :], ps_b[:, 0, :], mask_t[:, 2, :], ALU.mult))
                chain.link(dve, tt(mask_t[:, 3, :], ps_b[:, 1, :], mask_t[:, 3, :], ALU.mult))
                tt(down_low, mask_t[:, 2, :], mask_t[:, 3, :], ALU.add).then_inc(down_ready, 1)
                chain.end()

            def finish(t):
                for i in range(NT):
                    dve.wait_ge(out_full, t * NT + i + 1)
                    stt(xb[:, i, :], ps_a[:, i, :], 0.5, xb[:, i, :], ALU.mult, ALU.add).then_inc(x3_ready, 1)

            dve.wait_ge(loaded["vec"], 16)
            ts(q_bias[:], vec[:, V_BQ:V_BQ + MT], SCALE, None, ALU.mult)
            ts(conv_half[:], vec[:, V_CW:V_CW + 20], 0.5, None, ALU.mult).then_inc(conv_halved, 1)
            dve.wait_ge(consts_ready, 1)
            ts(decay_rate[:], decay_rate[:], -1.0, None, ALU.mult).then_inc(consts_ready, 1)
            nc.vector.memset(bc_stack[0:32, :], 0.0).then_inc(consts_ready, 1)
            dve.wait_ge(conv_halved, 1)
            convolve(0, range(JT))
            activate(0)
            dve.wait_ge(consts_ready, 6)
            dve.wait_ge(loaded["x"], 16)
            normalize("att", 0, xa, xn_att)
            split_bc(0)
            for f in range(FT):
                rotate(0, f)
                for piece in PLAN_FIRST[DOWN + f]["dve"]:
                    scan_piece(0, piece)
            attention(0, PLAN_FIRST)
            with dve.Fori(0, BATCH - 1) as t:
                second_sum(t)
                convolve(t + 1, [0])
                route(t)
                convolve(t + 1, range(1, JT))
                evaluate(t, 0)
                activate(t + 1)
                mask_low(t)
                for e in range(1, EVALS):
                    evaluate(t, e)
                    if e == 1:
                        split_bc(t + 1)
                    if e in NORM_SLOTS:
                        dve.wait_ge(loaded["x"], 16 * t + 32)
                        deviation("att", t + 1, xa, NORM_SLOTS.index(e))
                    for piece in PLAN_NEXT[e]["dve"]:
                        scan_piece(t + 1, piece)
                    if e in NORM_SLOTS:
                        scaled("att", t + 1, xa, xn_att, NORM_SLOTS.index(e))
                weigh_down(t)
                for f in range(FT):
                    rotate(t + 1, f)
                    for piece in PLAN_NEXT[DOWN + f]["dve"]:
                        scan_piece(t + 1, piece)
                finish(t)
                attention(t + 1, PLAN_NEXT)
            second_sum(BATCH - 1)
            route(BATCH - 1)
            mask_low(BATCH - 1)
            for e in range(EVALS):
                evaluate(BATCH - 1, e)
            weigh_down(BATCH - 1)
            finish(BATCH - 1)


def constant_table():
    import numpy as np
    c = np.zeros((P, C_COLS), np.float32)
    p = np.arange(P)
    c[:, C_ID:C_ID + P] = np.eye(P)
    half = HD // 2
    for m in range(P):
        if m % HD < half:
            c[m + half, C_ROT + m] = -1.0
        else:
            c[m - half, C_ROT + m] = 1.0
    c[:, C_MASK:C_MASK + P] = np.where(p[None, :] <= p[:, None], 0.0, NEG)
    for k in range(32, P):
        c[k, C_SEL + k % 32] = 1.0
    inv = (np.float32(10000.0) ** (-np.arange(half, dtype=np.float32) / np.float32(half))).astype(np.float32)
    ang = (np.arange(L, dtype=np.float32)[None, :] * inv[p % half][:, None]).astype(np.float32)
    c[:, C_COS:C_COS + L] = np.cos(ang)
    c[:, C_SIN:C_SIN + L] = np.sin(ang)
    c[:, C_CAND:C_CAND + NE] = np.arange(NE, 0, -1)
    c[:, C_HALF:C_HALF + NT] = -0.5
    return c


def kernel(**inputs):
    import numpy as np
    import concourse.bacc as bacc
    from concourse.bass_utils import run_bass_kernel_spmd

    a = {k: np.asarray(v) for k, v in inputs.items()}

    def rows(w):
        return w.reshape(-1, P, w.shape[1]).transpose(1, 0, 2)

    def column(v):
        return v.reshape(-1, P).T

    wk4 = [rows(np.tile(a["L0_attn_wk"][g * HD:(g + 1) * HD].T, (1, HPT))) for g in range(KV_HEADS)]
    xw = a["L0_xattn_x_proj_w"].T
    bc = xw[:, RANK:]
    w_x = rows(np.concatenate([xw[:, :RANK], np.zeros((DI, 16), np.float32), bc, bc, bc], axis=1))
    w_dt = np.zeros((P, DI), np.float32)
    w_dt[:RANK] = a["L0_xattn_dt_proj_w"].T

    def adapters(w):
        return rows(w.reshape(NE * LR, D).T)

    wg, wu = rows(a["L0_ffn_Wg"].T), rows(a["L0_ffn_Wu"].T)
    bg = a["L0_ffn_Bg"].transpose(0, 2, 1).reshape(NE * LR, DFF)
    bu = a["L0_ffn_Bu"].transpose(0, 2, 1).reshape(NE * LR, DFF)
    ad = a["L0_ffn_Ad"].reshape(NE * LR, DFF).T
    tiles, tile_adapters = [], []
    for f in range(FT):
        cols = slice(f * P, (f + 1) * P)
        tiles.append(np.concatenate([wg[:, :, cols].reshape(P, -1), wu[:, :, cols].reshape(P, -1)], axis=1))
        tile_adapters.append(np.concatenate([bg[:, cols], bu[:, cols]], axis=1))
    vectors = np.concatenate([
        a["L0_xattn_conv_w"].reshape(JT, P, TAPS).transpose(1, 0, 2).reshape(P, -1),
        column(a["L0_xattn_conv_b"]), column(a["L0_xattn_dt_proj_b"]),
        a["L0_xattn_A_log"].reshape(JT, P, NS).transpose(1, 0, 2).reshape(P, -1),
        column(a["L0_xattn_D"]), column(a["L0_attn_bq"]),
        np.stack([np.tile(a["L0_attn_bk"][g * HD:(g + 1) * HD], HPT) for g in range(KV_HEADS)], axis=1),
        np.tile(a["L0_attn_bv"], P // VD)[:, None],
    ], axis=1)
    arrays = {
        "x": a["x"],
        "ctx_t": a["ctx_1024"].transpose(0, 2, 1),
        "wq": rows(a["L0_attn_wq"].T),
        "wk": np.stack(wk4, axis=1),
        "wv": rows(np.tile(a["L0_attn_wv"].T, (1, P // VD))),
        "wo": rows(a["L0_attn_wo"].T),
        "w_in": rows(a["L0_xattn_in_proj_w"].T),
        "w_x": w_x,
        "w_dt": w_dt,
        "w_lora": np.stack([adapters(a["L0_ffn_Ag"]), adapters(a["L0_ffn_Au"])], axis=1),
        "w_r": rows(a["L0_ffn_Wr"].T),
        "b_down": a["L0_ffn_Bd"].transpose(0, 2, 1).reshape(NE * LR, D),
        "a_down": rows(ad),
        "w_tiles": np.stack(tiles),
        "w_adapt": np.stack(tile_adapters),
        "w_down": a["L0_ffn_Wd"].T.reshape(FT, P, D),
        "vectors": vectors,
        "constants": constant_table(),
    }
    arrays = {k: np.ascontiguousarray(v) for k, v in arrays.items()}
    nc = bacc.Bacc("TRN2", target_bir_lowering=False, num_devices=1, dynamic_dma_scratch_size=1024)
    args = [nc.dram_tensor("in_" + k, v.shape, mybir.dt.from_np(v.dtype), kind="ExternalInput").ap()
            for k, v in arrays.items()]
    args.append(nc.dram_tensor("out_x", (BATCH, L, D), F32, kind="ExternalOutput").ap())
    decoder_layer(nc, *args)
    r = run_bass_kernel_spmd(nc, [{"in_" + k: v for k, v in arrays.items()}], core_ids=[0])
    return r.results[0]["out_x"]
```
